# Optimizing a Trainium2 kernel written in Bass

```python
import numpy as np
import jax
import jax.numpy as jnp

def _softmax(x, axis=-1):
    return jax.nn.softmax(x, axis=axis)

def _gelu(x):
    return jax.nn.gelu(x, approximate=True)

def _silu(x):
    return jax.nn.silu(x)

def _sigmoid(x):
    return jax.nn.sigmoid(x)

def _layernorm(x, axis=-1, eps=1e-05):
    m = jnp.mean(x, axis=axis, keepdims=True)
    v = jnp.var(x, axis=axis, keepdims=True)
    return (x - m) / jnp.sqrt(v + eps)

def _scatter_add(tgt, idx, src, axis=0):
    return tgt.at[idx].add(src)

def _segment_sum(src, seg, n):
    return jax.ops.segment_sum(src, seg, n)
kernel_name = 'mk_xattn_ffn_d4_seqx_r4_5e1ba7'

def setup_inputs(seed: int=0):
    np.random.seed(seed)
    _w = jnp.asarray

    def _rec_inputs():
        import jax
        import jax.numpy as jnp
        _rk = jax.random.key(seed)
        x = -0.0003929 + 0.9999 * jax.random.normal(jax.random.fold_in(_rk, 1), (4, 1024, 256), jnp.float32)
        _lenS = 1024 - jax.random.randint(jax.random.fold_in(_rk, 7), (4,), 0, max(1, 1024 // 4) + 1, jnp.int32)
        _lenS2 = 64 - jax.random.randint(jax.random.fold_in(_rk, 8), (4,), 0, max(1, 64 // 4) + 1, jnp.int32)
        _ctx_1024P = jax.random.normal(jax.random.fold_in(_rk, 11), (4, 16, 256), jnp.float32)
        _ctx_1024c = jax.random.dirichlet(jax.random.fold_in(_rk, 511), 0.3 * jnp.ones((16,), jnp.float32), (4, 64))
        _ctx_1024t = jnp.einsum('bsk,bkd->bsd', _ctx_1024c, _ctx_1024P)
        _ctx_1024t = _ctx_1024t * jax.lax.rsqrt(jnp.mean(jnp.square(_ctx_1024t)) + 1e-12) * 0.953939
        ctx_1024 = 2.81802e-05 + 1.00001 * (_ctx_1024t + 0.3 * jax.random.normal(jax.random.fold_in(_rk, 611), (4, 64, 256), jnp.float32))
        _validS = jnp.arange(1024)[None, :] < _lenS[:, None]
        _validS2 = jnp.arange(64)[None, :] < _lenS2[:, None]
        _causal = jnp.tril(jnp.ones((1024, 1024), dtype=bool))
        mask_BxSxS2_fk0 = jnp.where(jnp.broadcast_to(_validS2[:, None, :], (4, 1024, 64)), -1000000000.0, 0.0).astype(jnp.float32)
        return (x, ctx_1024, mask_BxSxS2_fk0)
    x, ctx_1024, mask_BxSxS2_fk0 = _rec_inputs()

    def _L0_xattn_setup():
        import jax, jax.numpy as jnp
        import numpy as np
        B, NQ, NK, DQ, DV = (8, 512, 512, 256, 256)
        NEG = -1000000000.0
        key = jax.random.key(seed)
        kq, kk, kv = jax.random.split(key, 3)
        queries = jax.random.normal(kq, (B, NQ, DQ), dtype=jnp.float32)
        keys = jax.random.normal(kk, (B, NK, DQ), dtype=jnp.float32)
        values = jax.random.normal(kv, (B, NK, DV), dtype=jnp.float32)
        i = jnp.arange(NQ)[:, None]
        j = jnp.arange(NK)[None, :]
        attention_mask = jnp.where(j > i, jnp.float32(NEG), jnp.float32(0.0))
        attention_mask = jnp.broadcast_to(attention_mask, (B, NQ, NK)).copy()
        return {'queries': queries, 'keys': keys, 'values': values, 'attention_mask': attention_mask}
    _L0_xattn_all = _L0_xattn_setup()
    _L0_xattn_in = {k: v for k, v in _L0_xattn_all.items() if k in ()}
    del _L0_xattn_all

    def _L0_ffn_setup():
        import jax, jax.numpy as jnp
        import numpy as np
        LN_EPS = 1e-05

        def layer_norm(x, g, b):
            mu = jnp.mean(x, axis=-1, keepdims=True)
            var = jnp.var(x, axis=-1, keepdims=True)
            return (x - mu) / jnp.sqrt(var + LN_EPS) * g + b

        def balanced_assignment(scores):
            T, E = scores.shape
            C = T // E
            taken = jnp.zeros((T,), dtype=bool)
            parts = []
            for e in range(E):
                s = jnp.where(taken, -jnp.inf, scores[:, e])
                _, idx = jax.lax.top_k(s, C)
                parts.append(idx)
                taken = taken.at[idx].set(True)
            return jnp.concatenate(parts)
        key = jax.random.key(seed)
        ks = jax.random.split(key, 4)
        B, S, D, F, E = (4, 512, 256, 1024, 8)
        return {'x': jax.random.normal(ks[0], (B, S, D), dtype=jnp.float32), 'centroids': jax.random.normal(ks[1], (E, D), dtype=jnp.float32) * 0.1, 'ln_g': jnp.ones((D,), dtype=jnp.float32), 'ln_b': jnp.zeros((D,), dtype=jnp.float32), 'w1': jax.random.normal(ks[2], (E, D, F), dtype=jnp.float32) * 0.02, 'b1': jnp.zeros((E, F), dtype=jnp.float32), 'w2': jax.random.normal(ks[3], (E, F, D), dtype=jnp.float32) * 0.02, 'b2': jnp.zeros((E, D), dtype=jnp.float32)}
    _L0_ffn_all = _L0_ffn_setup()
    _L0_ffn_in = {k: v for k, v in _L0_ffn_all.items() if k in ('centroids', 'ln_g', 'ln_b', 'w1', 'b1', 'w2', 'b2')}
    del _L0_ffn_all

    def _L1_xattn_setup():
        import jax, jax.numpy as jnp
        import numpy as np
        EMBED_DIM = 256
        NUM_HEADS = 16
        HEAD_DIM = EMBED_DIM // NUM_HEADS
        B, L = (4, 512)
        NEG_INF = jnp.float32(-1e+30)

        def _split_heads(x):
            b, l, _ = x.shape
            return x.reshape(b, l, NUM_HEADS, HEAD_DIM).transpose(0, 2, 1, 3)
        key = jax.random.key(seed)
        ks = jax.random.split(key, 11)
        s = 1.0 / np.sqrt(EMBED_DIM)
        d = {'query': jax.random.normal(ks[0], (B, L, EMBED_DIM), jnp.float32), 'key': jax.random.normal(ks[1], (B, L, EMBED_DIM), jnp.float32), 'value': jax.random.normal(ks[2], (B, L, EMBED_DIM), jnp.float32), 'Wq': jax.random.uniform(ks[3], (EMBED_DIM, EMBED_DIM), jnp.float32, -s, s), 'bq': jax.random.uniform(ks[4], (EMBED_DIM,), jnp.float32, -s, s), 'Wk': jax.random.uniform(ks[5], (EMBED_DIM, EMBED_DIM), jnp.float32, -s, s), 'bk': jax.random.uniform(ks[6], (EMBED_DIM,), jnp.float32, -s, s), 'Wv': jax.random.uniform(ks[7], (EMBED_DIM, EMBED_DIM), jnp.float32, -s, s), 'bv': jax.random.uniform(ks[8], (EMBED_DIM,), jnp.float32, -s, s), 'Wo': jax.random.uniform(ks[9], (EMBED_DIM, EMBED_DIM), jnp.float32, -s, s), 'bo': jax.random.uniform(ks[10], (EMBED_DIM,), jnp.float32, -s, s)}
        return d
    _L1_xattn_all = _L1_xattn_setup()
    _L1_xattn_in = {k: v for k, v in _L1_xattn_all.items() if k in ('Wq', 'bq', 'Wk', 'bk', 'Wv', 'bv', 'Wo', 'bo')}
    del _L1_xattn_all

    def _L1_ffn_setup():
        import jax, jax.numpy as jnp
        import numpy as np
        D_MODEL = 256
        HIDDEN = 1024
        N_EXPERTS = 8
        TOP_K = 2
        key = jax.random.key(seed)
        k_x, k_r, k_w1, k_w2 = jax.random.split(key, 4)
        x = jax.random.normal(k_x, (2, 256, D_MODEL), dtype=jnp.float32)
        Wr = jax.random.normal(k_r, (D_MODEL, N_EXPERTS), dtype=jnp.float32) * 0.02
        W1 = jax.random.normal(k_w1, (N_EXPERTS, D_MODEL, HIDDEN), dtype=jnp.float32) * 0.02
        W2 = jax.random.normal(k_w2, (N_EXPERTS, HIDDEN, D_MODEL), dtype=jnp.float32) * 0.02
        return {'x': x, 'Wr': Wr, 'W1': W1, 'W2': W2}
    _L1_ffn_all = _L1_ffn_setup()
    _L1_ffn_in = {k: v for k, v in _L1_ffn_all.items() if k in ('Wr', 'W1', 'W2')}
    del _L1_ffn_all

    def _L2_xattn_setup():
        import jax, jax.numpy as jnp
        import numpy as np
        B, NT, NM, C, H, FF = (8, 256, 512, 256, 8, 1024)

        def _ln(x, g, b):
            m = x.mean(-1, keepdims=True)
            v = jnp.mean((x - m) ** 2, axis=-1, keepdims=True)
            return (x - m) / jnp.sqrt(v + 1e-05) * g + b
        key = jax.random.key(seed)
        ks = jax.random.split(key, 8)
        w = lambda k, shape, s=0.02: jax.random.normal(k, shape, dtype=jnp.float32) * s
        return {'tgt': jax.random.normal(ks[0], (B, NT, C), dtype=jnp.float32), 'memory': jax.random.normal(ks[1], (B, NM, C), dtype=jnp.float32), 'qkv_w': w(ks[2], (3 * C, C)), 'qkv_b': jnp.zeros((3 * C,), jnp.float32), 'sa_out_w': w(ks[3], (C, C)), 'sa_out_b': jnp.zeros((C,), jnp.float32), 'in_proj_w': w(ks[4], (3 * C, C)), 'in_proj_b': jnp.zeros((3 * C,), jnp.float32), 'mha_out_w': w(ks[5], (C, C)), 'mha_out_b': jnp.zeros((C,), jnp.float32), 'lin1_w': w(ks[6], (FF, C)), 'lin1_b': jnp.zeros((FF,), jnp.float32), 'lin2_w': w(ks[7], (C, FF)), 'lin2_b': jnp.zeros((C,), jnp.float32), 'ln1_g': jnp.ones((C,), jnp.float32), 'ln1_b': jnp.zeros((C,), jnp.float32), 'ln2_g': jnp.ones((C,), jnp.float32), 'ln2_b': jnp.zeros((C,), jnp.float32), 'ln3_g': jnp.ones((C,), jnp.float32), 'ln3_b': jnp.zeros((C,), jnp.float32)}
    _L2_xattn_all = _L2_xattn_setup()
    _L2_xattn_in = {k: v for k, v in _L2_xattn_all.items() if k in ('qkv_w', 'qkv_b', 'sa_out_w', 'sa_out_b', 'in_proj_w', 'in_proj_b', 'mha_out_w', 'mha_out_b', 'lin1_w', 'lin1_b', 'lin2_w', 'lin2_b', 'ln1_g', 'ln1_b', 'ln2_g', 'ln2_b', 'ln3_g', 'ln3_b')}
    del _L2_xattn_all

    def _L2_ffn_setup():
        import jax, jax.numpy as jnp
        import numpy as np
        EPS = 1e-05
        THRESHOLD = 0.7
        QMAX = 127.0

        def _fake_quant_act(x):
            scale = jnp.maximum(jnp.max(jnp.abs(x)), 1e-08) / QMAX
            q = jnp.round(jnp.clip(x / scale, -QMAX, QMAX)) * scale
            return x + jax.lax.stop_gradient(q - x)

        def _ternary_quant_weight(w):
            absw = jnp.abs(w)
            delta = THRESHOLD * jnp.mean(absw)
            mask = (absw > delta).astype(w.dtype)
            alpha = jnp.sum(absw * mask) / jnp.maximum(jnp.sum(mask), 1.0)
            wq = alpha * jnp.sign(w) * mask
            return w + jax.lax.stop_gradient(wq - w)
        key = jax.random.key(seed)
        k1, k2 = jax.random.split(key)
        B, S, D_IN, D_OUT = (4, 2048, 256, 256)
        x = jax.random.normal(k1, (B, S, D_IN), dtype=jnp.float32)
        weight = jax.random.normal(k2, (D_OUT, D_IN), dtype=jnp.float32) * np.sqrt(2.0 / D_IN)
        gamma = jnp.ones((D_IN,), dtype=jnp.float32)
        beta = jnp.zeros((D_IN,), dtype=jnp.float32)
        return {'x': x, 'weight': weight, 'gamma': gamma, 'beta': beta}
    _L2_ffn_all = _L2_ffn_setup()
    _L2_ffn_in = {k: v for k, v in _L2_ffn_all.items() if k in ('weight', 'gamma', 'beta')}
    del _L2_ffn_all

    def _L3_xattn_setup():
        import jax, jax.numpy as jnp
        import numpy as np
        B, S, D, H = (2, 512, 256, 16)
        HD = D // H

        def _split_heads(x):
            b, s, d = x.shape
            return x.reshape(b, s, H, d // H).transpose(0, 2, 1, 3)
        key = jax.random.key(seed)
        ks = jax.random.split(key, 11)
        sc = 1.0 / np.sqrt(D)
        return {'q': jax.random.normal(ks[0], (B, S, D), jnp.float32), 'k': jax.random.normal(ks[1], (B, S, D), jnp.float32), 'v': jax.random.normal(ks[2], (B, S, D), jnp.float32), 'Wq': jax.random.normal(ks[3], (D, D), jnp.float32) * sc, 'bq': jnp.zeros((D,), jnp.float32), 'Wk': jax.random.normal(ks[4], (D, D), jnp.float32) * sc, 'bk': jnp.zeros((D,), jnp.float32), 'Wv': jax.random.normal(ks[5], (D, D), jnp.float32) * sc, 'bv': jnp.zeros((D,), jnp.float32), 'Wo': jax.random.normal(ks[6], (D, D), jnp.float32) * sc, 'bo': jnp.zeros((D,), jnp.float32)}
    _L3_xattn_all = _L3_xattn_setup()
    _L3_xattn_in = {k: v for k, v in _L3_xattn_all.items() if k in ('Wq', 'bq', 'Wk', 'bk', 'Wv', 'bv', 'Wo', 'bo')}
    del _L3_xattn_all

    def _L3_ffn_setup():
        import jax, jax.numpy as jnp
        import numpy as np
        B, S, D, H, M, E, K = (4, 512, 256, 512, 64, 8, 2)

        def _layernorm(x, g, b, eps=1e-05):
            mu = x.mean(-1, keepdims=True)
            var = ((x - mu) ** 2).mean(-1, keepdims=True)
            return (x - mu) * jax.lax.rsqrt(var + eps) * g + b

        def _forward(inputs_embeds, enc_W, enc_b, s2c_W, s2c_b, rW1, rb1, rW2, rb2, We1, be1, We2, be2, c2s_W, c2s_b, dec_W, dec_b, ln_g, ln_b):
            b, s, _ = inputs_embeds.shape
            spikes_enc = jax.nn.sigmoid(inputs_embeds @ enc_W + enc_b)
            flat = spikes_enc.reshape(b * s, H)
            cont = flat @ s2c_W + s2c_b
            logits = jnp.tanh(cont @ rW1 + rb1) @ rW2 + rb2
            probs = jax.nn.softmax(logits, axis=-1)
            topw, topi = jax.lax.top_k(probs, K)
            w = topw / topw.sum(-1, keepdims=True)
            gates = (jax.nn.one_hot(topi, E, dtype=cont.dtype) * w[..., None]).sum(1)
            h = jax.nn.relu(jnp.einsum('nm,emh->enh', cont, We1) + be1[:, None, :])
            expert_out = jnp.einsum('enh,ehm->enm', h, We2) + be2[:, None, :]
            output_flat = jnp.einsum('enm,ne->nm', expert_out, gates)
            spikes_moe = jax.nn.sigmoid(output_flat @ c2s_W + c2s_b).reshape(b, s, H)
            decoded = jax.nn.sigmoid(spikes_moe @ dec_W + dec_b)
            return _layernorm(decoded, ln_g, ln_b)
        key = jax.random.key(seed)
        ks = jax.random.split(key, 10)
        r = lambda k, shape: jax.random.normal(k, shape, dtype=jnp.float32) * 0.02
        return {'inputs_embeds': jax.random.normal(ks[0], (B, S, D), dtype=jnp.float32), 'enc_W': r(ks[1], (D, H)), 'enc_b': jnp.zeros((H,), jnp.float32), 's2c_W': r(ks[2], (H, M)), 's2c_b': jnp.zeros((M,), jnp.float32), 'rW1': r(ks[3], (M, 64)), 'rb1': jnp.zeros((64,), jnp.float32), 'rW2': r(ks[4], (64, E)), 'rb2': jnp.zeros((E,), jnp.float32), 'We1': r(ks[5], (E, M, H // 2)), 'be1': jnp.zeros((E, H // 2), jnp.float32), 'We2': r(ks[6], (E, H // 2, M)), 'be2': jnp.zeros((E, M), jnp.float32), 'c2s_W': r(ks[7], (M, H)), 'c2s_b': jnp.zeros((H,), jnp.float32), 'dec_W': r(ks[8], (H, D)), 'dec_b': jnp.zeros((D,), jnp.float32), 'ln_g': jnp.ones((D,), jnp.float32), 'ln_b': jnp.zeros((D,), jnp.float32)}
    _L3_ffn_all = _L3_ffn_setup()
    _L3_ffn_in = {k: v for k, v in _L3_ffn_all.items() if k in ('enc_W', 'enc_b', 's2c_W', 's2c_b', 'rW1', 'rb1', 'rW2', 'rb2', 'We1', 'be1', 'We2', 'be2', 'c2s_W', 'c2s_b', 'dec_W', 'dec_b', 'ln_g', 'ln_b')}
    del _L3_ffn_all
    return {'x': x, 'ctx_1024': ctx_1024, 'mask_BxSxS2_fk0': mask_BxSxS2_fk0, 'L0_ffn_centroids': _L0_ffn_in['centroids'], 'L0_ffn_ln_g': _L0_ffn_in['ln_g'], 'L0_ffn_ln_b': _L0_ffn_in['ln_b'], 'L0_ffn_w1': _L0_ffn_in['w1'], 'L0_ffn_b1': _L0_ffn_in['b1'], 'L0_ffn_w2': _L0_ffn_in['w2'], 'L0_ffn_b2': _L0_ffn_in['b2'], 'L1_xattn_Wq': _L1_xattn_in['Wq'], 'L1_xattn_bq': _L1_xattn_in['bq'], 'L1_xattn_Wk': _L1_xattn_in['Wk'], 'L1_xattn_bk': _L1_xattn_in['bk'], 'L1_xattn_Wv': _L1_xattn_in['Wv'], 'L1_xattn_bv': _L1_xattn_in['bv'], 'L1_xattn_Wo': _L1_xattn_in['Wo'], 'L1_xattn_bo': _L1_xattn_in['bo'], 'L1_ffn_Wr': _L1_ffn_in['Wr'], 'L1_ffn_W1': _L1_ffn_in['W1'], 'L1_ffn_W2': _L1_ffn_in['W2'], 'L2_xattn_qkv_w': _L2_xattn_in['qkv_w'], 'L2_xattn_qkv_b': _L2_xattn_in['qkv_b'], 'L2_xattn_sa_out_w': _L2_xattn_in['sa_out_w'], 'L2_xattn_sa_out_b': _L2_xattn_in['sa_out_b'], 'L2_xattn_in_proj_w': _L2_xattn_in['in_proj_w'], 'L2_xattn_in_proj_b': _L2_xattn_in['in_proj_b'], 'L2_xattn_mha_out_w': _L2_xattn_in['mha_out_w'], 'L2_xattn_mha_out_b': _L2_xattn_in['mha_out_b'], 'L2_xattn_lin1_w': _L2_xattn_in['lin1_w'], 'L2_xattn_lin1_b': _L2_xattn_in['lin1_b'], 'L2_xattn_lin2_w': _L2_xattn_in['lin2_w'], 'L2_xattn_lin2_b': _L2_xattn_in['lin2_b'], 'L2_xattn_ln1_g': _L2_xattn_in['ln1_g'], 'L2_xattn_ln1_b': _L2_xattn_in['ln1_b'], 'L2_xattn_ln2_g': _L2_xattn_in['ln2_g'], 'L2_xattn_ln2_b': _L2_xattn_in['ln2_b'], 'L2_xattn_ln3_g': _L2_xattn_in['ln3_g'], 'L2_xattn_ln3_b': _L2_xattn_in['ln3_b'], 'L2_ffn_weight': _L2_ffn_in['weight'], 'L2_ffn_gamma': _L2_ffn_in['gamma'], 'L2_ffn_beta': _L2_ffn_in['beta'], 'L3_xattn_Wq': _L3_xattn_in['Wq'], 'L3_xattn_bq': _L3_xattn_in['bq'], 'L3_xattn_Wk': _L3_xattn_in['Wk'], 'L3_xattn_bk': _L3_xattn_in['bk'], 'L3_xattn_Wv': _L3_xattn_in['Wv'], 'L3_xattn_bv': _L3_xattn_in['bv'], 'L3_xattn_Wo': _L3_xattn_in['Wo'], 'L3_xattn_bo': _L3_xattn_in['bo'], 'L3_ffn_enc_W': _L3_ffn_in['enc_W'], 'L3_ffn_enc_b': _L3_ffn_in['enc_b'], 'L3_ffn_s2c_W': _L3_ffn_in['s2c_W'], 'L3_ffn_s2c_b': _L3_ffn_in['s2c_b'], 'L3_ffn_rW1': _L3_ffn_in['rW1'], 'L3_ffn_rb1': _L3_ffn_in['rb1'], 'L3_ffn_rW2': _L3_ffn_in['rW2'], 'L3_ffn_rb2': _L3_ffn_in['rb2'], 'L3_ffn_We1': _L3_ffn_in['We1'], 'L3_ffn_be1': _L3_ffn_in['be1'], 'L3_ffn_We2': _L3_ffn_in['We2'], 'L3_ffn_be2': _L3_ffn_in['be2'], 'L3_ffn_c2s_W': _L3_ffn_in['c2s_W'], 'L3_ffn_c2s_b': _L3_ffn_in['c2s_b'], 'L3_ffn_dec_W': _L3_ffn_in['dec_W'], 'L3_ffn_dec_b': _L3_ffn_in['dec_b'], 'L3_ffn_ln_g': _L3_ffn_in['ln_g'], 'L3_ffn_ln_b': _L3_ffn_in['ln_b']}

def reference(x, ctx_1024, mask_BxSxS2_fk0, L0_ffn_centroids, L0_ffn_ln_g, L0_ffn_ln_b, L0_ffn_w1, L0_ffn_b1, L0_ffn_w2, L0_ffn_b2, L1_xattn_Wq, L1_xattn_bq, L1_xattn_Wk, L1_xattn_bk, L1_xattn_Wv, L1_xattn_bv, L1_xattn_Wo, L1_xattn_bo, L1_ffn_Wr, L1_ffn_W1, L1_ffn_W2, L2_xattn_qkv_w, L2_xattn_qkv_b, L2_xattn_sa_out_w, L2_xattn_sa_out_b, L2_xattn_in_proj_w, L2_xattn_in_proj_b, L2_xattn_mha_out_w, L2_xattn_mha_out_b, L2_xattn_lin1_w, L2_xattn_lin1_b, L2_xattn_lin2_w, L2_xattn_lin2_b, L2_xattn_ln1_g, L2_xattn_ln1_b, L2_xattn_ln2_g, L2_xattn_ln2_b, L2_xattn_ln3_g, L2_xattn_ln3_b, L2_ffn_weight, L2_ffn_gamma, L2_ffn_beta, L3_xattn_Wq, L3_xattn_bq, L3_xattn_Wk, L3_xattn_bk, L3_xattn_Wv, L3_xattn_bv, L3_xattn_Wo, L3_xattn_bo, L3_ffn_enc_W, L3_ffn_enc_b, L3_ffn_s2c_W, L3_ffn_s2c_b, L3_ffn_rW1, L3_ffn_rb1, L3_ffn_rW2, L3_ffn_rb2, L3_ffn_We1, L3_ffn_be1, L3_ffn_We2, L3_ffn_be2, L3_ffn_c2s_W, L3_ffn_c2s_b, L3_ffn_dec_W, L3_ffn_dec_b, L3_ffn_ln_g, L3_ffn_ln_b):
    import jax
    import jax.numpy as jnp

    def _L0_xattn_ref(queries, keys, values, attention_mask):
        import jax, jax.numpy as jnp
        import numpy as np
        B, NQ, NK, DQ, DV = (8, 512, 512, 256, 256)
        NEG = -1000000000.0
        d_keys = jnp.sqrt(jnp.float32(keys.shape[-1]))
        logits = jnp.einsum('bqd,bkd->bqk', queries, keys) / d_keys
        logits = jnp.where(attention_mask < -1.0, attention_mask, logits)
        attn = jax.nn.softmax(logits, axis=-1)
        attn = jnp.where(jnp.isnan(attn), jnp.float32(0.0), attn)
        return jnp.einsum('bqk,bkv->bqv', attn, values)

    def _L0_ffn_ref(x, centroids, ln_g, ln_b, w1, b1, w2, b2):
        import jax, jax.numpy as jnp
        import numpy as np
        LN_EPS = 1e-05

        def layer_norm(x, g, b):
            mu = jnp.mean(x, axis=-1, keepdims=True)
            var = jnp.var(x, axis=-1, keepdims=True)
            return (x - mu) / jnp.sqrt(var + LN_EPS) * g + b

        def balanced_assignment(scores):
            T, E = scores.shape
            C = T // E
            taken = jnp.zeros((T,), dtype=bool)
            parts = []
            for e in range(E):
                s = jnp.where(taken, -jnp.inf, scores[:, e])
                _, idx = jax.lax.top_k(s, C)
                parts.append(idx)
                taken = taken.at[idx].set(True)
            return jnp.concatenate(parts)
        D = x.shape[-1]
        feat = x.reshape(-1, D)
        T = feat.shape[0]
        E = centroids.shape[0]
        C = T // E
        norm = layer_norm(feat, ln_g, ln_b)
        scores = jax.lax.stop_gradient(norm @ centroids.T)
        sort_by_expert = balanced_assignment(scores)
        routed = feat[sort_by_expert].reshape(E, C, D)
        h = layer_norm(routed, ln_g, ln_b)
        h = jax.nn.gelu(jnp.einsum('ecd,edf->ecf', h, w1) + b1[:, None, :])
        h = jnp.einsum('ecf,efd->ecd', h, w2) + b2[:, None, :]
        out = routed + h
        inv = jnp.zeros((T,), dtype=jnp.int32).at[sort_by_expert].set(jnp.arange(T, dtype=jnp.int32))
        return out.reshape(T, D)[inv].reshape(x.shape)

    def _L1_xattn_ref(query, key, value, Wq, bq, Wk, bk, Wv, bv, Wo, bo):
        import jax, jax.numpy as jnp
        import numpy as np
        EMBED_DIM = 256
        NUM_HEADS = 16
        HEAD_DIM = EMBED_DIM // NUM_HEADS
        B, L = (4, 512)
        NEG_INF = jnp.float32(-1e+30)

        def _split_heads(x):
            b, l, _ = x.shape
            return x.reshape(b, l, NUM_HEADS, HEAD_DIM).transpose(0, 2, 1, 3)
        q = _split_heads(query @ Wq.T + bq)
        k = _split_heads(key @ Wk.T + bk)
        v = _split_heads(value @ Wv.T + bv)
        scores = jnp.einsum('bhqd,bhkd->bhqk', q, k) / np.sqrt(HEAD_DIM)
        q_len, k_len = (query.shape[1], key.shape[1])
        causal = jnp.triu(jnp.ones((q_len, k_len), jnp.bool_), k=1)
        scores = jnp.where(causal[None, None], NEG_INF, scores)
        attn = jax.nn.softmax(scores, axis=-1)
        out = jnp.einsum('bhqk,bhkd->bhqd', attn, v)
        out = out.transpose(0, 2, 1, 3).reshape(query.shape[0], q_len, EMBED_DIM)
        return out @ Wo.T + bo

    def _L1_ffn_ref(x, Wr, W1, W2):
        import jax, jax.numpy as jnp
        import numpy as np
        D_MODEL = 256
        HIDDEN = 1024
        N_EXPERTS = 8
        TOP_K = 2
        B, S, D = x.shape
        flat = x.reshape(-1, D)
        logits = flat @ Wr
        top_vals, top_idx = jax.lax.top_k(logits, TOP_K)
        weights = jax.nn.softmax(top_vals, axis=-1)
        top1 = top_idx[:, 0]
        w_top1 = weights[:, 0]
        h = jax.nn.gelu(jnp.einsum('td,edh->teh', flat, W1), approximate=False)
        y = jnp.einsum('teh,ehd->ted', h, W2)
        y_sel = jnp.take_along_axis(y, top1[:, None, None], axis=1)[:, 0, :]
        out = (w_top1[:, None] * y_sel).reshape(B, S, D)
        return out

    def _L2_xattn_ref(tgt, memory, qkv_w, qkv_b, sa_out_w, sa_out_b, in_proj_w, in_proj_b, mha_out_w, mha_out_b, lin1_w, lin1_b, lin2_w, lin2_b, ln1_g, ln1_b, ln2_g, ln2_b, ln3_g, ln3_b):
        import jax, jax.numpy as jnp
        import numpy as np
        B, NT, NM, C, H, FF = (8, 256, 512, 256, 8, 1024)

        def _ln(x, g, b):
            m = x.mean(-1, keepdims=True)
            v = jnp.mean((x - m) ** 2, axis=-1, keepdims=True)
            return (x - m) / jnp.sqrt(v + 1e-05) * g + b
        Bx, N, Cx = tgt.shape
        qkv = tgt @ qkv_w.T + qkv_b
        q, k, v = jnp.split(qkv, 3, axis=-1)
        scores = jnp.einsum('bnc,bmc->bnm', q, k) * jnp.sqrt(jnp.float32(Cx))
        diag = jnp.eye(N, dtype=bool)
        scores = jnp.where(diag[None, :, :], scores, -jnp.inf)
        attn = jax.nn.softmax(scores, axis=-1)
        sa = jnp.einsum('bnm,bmc->bnc', attn, v) @ sa_out_w.T + sa_out_b
        x = _ln(tgt + sa, ln1_g, ln1_b)
        d = Cx // H
        wq, wk, wv = jnp.split(in_proj_w, 3, axis=0)
        bq, bk, bv = jnp.split(in_proj_b, 3, axis=0)
        qh = (x @ wq.T + bq).reshape(Bx, N, H, d).transpose(0, 2, 1, 3)
        kh = (memory @ wk.T + bk).reshape(Bx, -1, H, d).transpose(0, 2, 1, 3)
        vh = (memory @ wv.T + bv).reshape(Bx, -1, H, d).transpose(0, 2, 1, 3)
        a = jax.nn.softmax(jnp.einsum('bhnd,bhmd->bhnm', qh, kh) / jnp.sqrt(jnp.float32(d)), axis=-1)
        ca = jnp.einsum('bhnm,bhmd->bhnd', a, vh).transpose(0, 2, 1, 3).reshape(Bx, N, Cx)
        ca = ca @ mha_out_w.T + mha_out_b
        x = _ln(x + ca, ln2_g, ln2_b)
        ff = jax.nn.relu(x @ lin1_w.T + lin1_b) @ lin2_w.T + lin2_b
        return _ln(x + ff, ln3_g, ln3_b)

    def _L2_ffn_ref(x, weight, gamma, beta):
        import jax, jax.numpy as jnp
        import numpy as np
        EPS = 1e-05
        THRESHOLD = 0.7
        QMAX = 127.0

        def _fake_quant_act(x):
            scale = jnp.maximum(jnp.max(jnp.abs(x)), 1e-08) / QMAX
            q = jnp.round(jnp.clip(x / scale, -QMAX, QMAX)) * scale
            return x + jax.lax.stop_gradient(q - x)

        def _ternary_quant_weight(w):
            absw = jnp.abs(w)
            delta = THRESHOLD * jnp.mean(absw)
            mask = (absw > delta).astype(w.dtype)
            alpha = jnp.sum(absw * mask) / jnp.maximum(jnp.sum(mask), 1.0)
            wq = alpha * jnp.sign(w) * mask
            return w + jax.lax.stop_gradient(wq - w)
        mu = jnp.mean(x, axis=-1, keepdims=True)
        var = jnp.mean(jnp.square(x - mu), axis=-1, keepdims=True)
        xn = (x - mu) * jax.lax.rsqrt(var + EPS) * gamma + beta
        xq = _fake_quant_act(xn)
        wq = _ternary_quant_weight(weight)
        return jnp.einsum('bsi,oi->bso', xq, wq)

    def _L3_xattn_ref(q, k, v, Wq, bq, Wk, bk, Wv, bv, Wo, bo):
        import jax, jax.numpy as jnp
        import numpy as np
        B, S, D, H = (2, 512, 256, 16)
        HD = D // H

        def _split_heads(x):
            b, s, d = x.shape
            return x.reshape(b, s, H, d // H).transpose(0, 2, 1, 3)
        qh = _split_heads(q @ Wq + bq)
        kh = _split_heads(k @ Wk + bk)
        vh = _split_heads(v @ Wv + bv)
        scores = jnp.einsum('bhqd,bhkd->bhqk', qh, kh) / np.sqrt(HD)
        attn = jax.nn.softmax(scores, axis=-1)
        out = jnp.einsum('bhqk,bhkd->bhqd', attn, vh)
        out = out.transpose(0, 2, 1, 3).reshape(q.shape[0], q.shape[1], -1)
        return out @ Wo + bo

    def _L3_ffn_ref(inputs_embeds, enc_W, enc_b, s2c_W, s2c_b, rW1, rb1, rW2, rb2, We1, be1, We2, be2, c2s_W, c2s_b, dec_W, dec_b, ln_g, ln_b):
        import jax, jax.numpy as jnp
        import numpy as np
        B, S, D, H, M, E, K = (4, 512, 256, 512, 64, 8, 2)

        def _layernorm(x, g, b, eps=1e-05):
            mu = x.mean(-1, keepdims=True)
            var = ((x - mu) ** 2).mean(-1, keepdims=True)
            return (x - mu) * jax.lax.rsqrt(var + eps) * g + b

        def _forward(inputs_embeds, enc_W, enc_b, s2c_W, s2c_b, rW1, rb1, rW2, rb2, We1, be1, We2, be2, c2s_W, c2s_b, dec_W, dec_b, ln_g, ln_b):
            b, s, _ = inputs_embeds.shape
            spikes_enc = jax.nn.sigmoid(inputs_embeds @ enc_W + enc_b)
            flat = spikes_enc.reshape(b * s, H)
            cont = flat @ s2c_W + s2c_b
            logits = jnp.tanh(cont @ rW1 + rb1) @ rW2 + rb2
            probs = jax.nn.softmax(logits, axis=-1)
            topw, topi = jax.lax.top_k(probs, K)
            w = topw / topw.sum(-1, keepdims=True)
            gates = (jax.nn.one_hot(topi, E, dtype=cont.dtype) * w[..., None]).sum(1)
            h = jax.nn.relu(jnp.einsum('nm,emh->enh', cont, We1) + be1[:, None, :])
            expert_out = jnp.einsum('enh,ehm->enm', h, We2) + be2[:, None, :]
            output_flat = jnp.einsum('enm,ne->nm', expert_out, gates)
            spikes_moe = jax.nn.sigmoid(output_flat @ c2s_W + c2s_b).reshape(b, s, H)
            decoded = jax.nn.sigmoid(spikes_moe @ dec_W + dec_b)
            return _layernorm(decoded, ln_g, ln_b)
        return _forward(inputs_embeds, enc_W, enc_b, s2c_W, s2c_b, rW1, rb1, rW2, rb2, We1, be1, We2, be2, c2s_W, c2s_b, dec_W, dec_b, ln_g, ln_b)
    x = x + _L0_xattn_ref(_layernorm(x, axis=-1), ctx_1024, ctx_1024, mask_BxSxS2_fk0)
    x = x + _L0_ffn_ref(_layernorm(x, axis=-1), L0_ffn_centroids, L0_ffn_ln_g, L0_ffn_ln_b, L0_ffn_w1, L0_ffn_b1, L0_ffn_w2, L0_ffn_b2)
    x = x + _L1_xattn_ref(_layernorm(x, axis=-1), ctx_1024, ctx_1024, L1_xattn_Wq, L1_xattn_bq, L1_xattn_Wk, L1_xattn_bk, L1_xattn_Wv, L1_xattn_bv, L1_xattn_Wo, L1_xattn_bo)
    x = x + _L1_ffn_ref(_layernorm(x, axis=-1), L1_ffn_Wr, L1_ffn_W1, L1_ffn_W2)
    x = x + _L2_xattn_ref(_layernorm(x, axis=-1), ctx_1024, L2_xattn_qkv_w, L2_xattn_qkv_b, L2_xattn_sa_out_w, L2_xattn_sa_out_b, L2_xattn_in_proj_w, L2_xattn_in_proj_b, L2_xattn_mha_out_w, L2_xattn_mha_out_b, L2_xattn_lin1_w, L2_xattn_lin1_b, L2_xattn_lin2_w, L2_xattn_lin2_b, L2_xattn_ln1_g, L2_xattn_ln1_b, L2_xattn_ln2_g, L2_xattn_ln2_b, L2_xattn_ln3_g, L2_xattn_ln3_b)
    x = x + _L2_ffn_ref(_layernorm(x, axis=-1), L2_ffn_weight, L2_ffn_gamma, L2_ffn_beta)
    x = x + _L3_xattn_ref(_layernorm(x, axis=-1), ctx_1024, ctx_1024, L3_xattn_Wq, L3_xattn_bq, L3_xattn_Wk, L3_xattn_bk, L3_xattn_Wv, L3_xattn_bv, L3_xattn_Wo, L3_xattn_bo)
    x = x + _L3_ffn_ref(_layernorm(x, axis=-1), L3_ffn_enc_W, L3_ffn_enc_b, L3_ffn_s2c_W, L3_ffn_s2c_b, L3_ffn_rW1, L3_ffn_rb1, L3_ffn_rW2, L3_ffn_rb2, L3_ffn_We1, L3_ffn_be1, L3_ffn_We2, L3_ffn_be2, L3_ffn_c2s_W, L3_ffn_c2s_b, L3_ffn_dec_W, L3_ffn_dec_b, L3_ffn_ln_g, L3_ffn_ln_b)
    return x

_drawn_inputs = setup_inputs


def setup_inputs(seed=0):
    import zlib

    import numpy as np

    out = dict(_drawn_inputs(seed))
    spreads = {'L0_ffn_ln_g': (1.0, 0.2),
     'L0_ffn_ln_b': (0.0, 0.8),
     'L0_ffn_b1': (0.0, 0.449),
     'L0_ffn_b2': (0.0, 0.1),
     'L2_xattn_qkv_b': (0.0, 0.656),
     'L2_xattn_sa_out_b': (0.0, 0.1),
     'L2_xattn_in_proj_b': (0.0, 0.736),
     'L2_xattn_mha_out_b': (0.0, 0.267),
     'L2_xattn_lin1_b': (0.0, 0.534),
     'L2_xattn_lin2_b': (0.0, 0.275),
     'L2_xattn_ln1_g': (1.0, 0.2),
     'L2_xattn_ln1_b': (0.0, 0.1),
     'L2_xattn_ln2_g': (1.0, 0.2),
     'L2_xattn_ln2_b': (0.0, 0.274),
     'L2_xattn_ln3_g': (1.0, 0.2),
     'L2_xattn_ln3_b': (0.0, 0.1),
     'L2_ffn_gamma': (1.0, 0.2),
     'L2_ffn_beta': (0.0, 0.1),
     'L3_xattn_bq': (0.0, 0.8),
     'L3_xattn_bk': (0.0, 0.8),
     'L3_xattn_bv': (0.0, 0.315),
     'L3_xattn_bo': (0.0, 0.299),
     'L3_ffn_enc_b': (0.0, 0.8),
     'L3_ffn_s2c_b': (0.0, 0.8),
     'L3_ffn_rb1': (0.0, 0.8),
     'L3_ffn_rb2': (0.0, 0.8),
     'L3_ffn_be1': (0.0, 0.8),
     'L3_ffn_be2': (0.0, 0.8),
     'L3_ffn_c2s_b': (0.0, 0.673),
     'L3_ffn_dec_b': (0.0, 0.1),
     'L3_ffn_ln_g': (1.0, 0.2),
     'L3_ffn_ln_b': (0.0, 0.285)}
    factors = {'L1_xattn_Wq': 4.857,
     'L1_xattn_bq': 8.0,
     'L1_xattn_Wk': 4.896,
     'L1_xattn_bk': 8.0,
     'L1_xattn_bv': 5.518,
     'L1_xattn_bo': 3.285,
     'L2_xattn_in_proj_w': 3.484,
     'L2_xattn_mha_out_w': 3.018,
     'L3_ffn_enc_W': 8.0,
     'L3_ffn_s2c_W': 8.0,
     'L3_ffn_rW1': 8.0,
     'L3_ffn_rW2': 8.0,
     'L3_ffn_We1': 8.0,
     'L3_ffn_We2': 8.0,
     'L3_ffn_c2s_W': 8.0}
    for name, (base, spread) in spreads.items():
        noise = np.random.default_rng([zlib.crc32(name.encode()), seed]).standard_normal(out[name].shape)
        drawn = base * np.exp(spread * noise) if base else spread * noise
        out[name] = jnp.asarray(drawn.astype(out[name].dtype))
    for name, factor in factors.items():
        out[name] = (out[name] * factor).astype(out[name].dtype)
    return out
```

```python
import numpy as np
import concourse.bass as bass
from concourse import mybir
from contextlib import ExitStack

FP32 = mybir.dt.float32
BF16 = mybir.dt.bfloat16
I32 = mybir.dt.int32
U32 = mybir.dt.uint32
ALU = mybir.AluOpType
ACT = mybir.ActivationFunctionType
AX = mybir.AxisListType.X

P = 128
B, S, D, KEYS = 4, 1024, 256, 64
T = B * S
TILES = T // P
TPB = S // P
DC = D // P
EXPERTS, F = 8, 1024
FC = F // P
LN_EPS = 1e-5



def lagged(u, par, lag, tiles=TILES):
    t = u * 2 + (par - lag)
    q = (par - lag) % 2
    if isinstance(t, int) and not 0 <= t < tiles:
        return None
    return t, q, u + (par - lag - q) // 2


def over_tiles(eng, body, lag, tiles=TILES):
    head = (lag + 4) // 2
    for u in range(head):
        body(u)
    with eng.Fori(head, tiles // 2) as u:
        body(u)
    for u in range(tiles // 2, (tiles + lag + 1) // 2):
        body(u)


def wait_apart(nc, dve, sem, value, spare):
    at_least(dve, sem, value)
    if not isinstance(value, int):
        nc.vector.memset(spare, 0.0)


def at_least(eng, sem, value):
    if not (isinstance(value, int) and value <= 0):
        eng.wait_ge(sem, value)


def cols(t, w=D):
    return bass.ds(t * w, w)


def offsets(table):
    at, out = 0, {}
    for name, width in table:
        out[name] = (at, width)
        at += width
    return out, at


SEC0 = [("ident", P), ("tri", P), ("hmask16", 8), ("hmask8", 4), ("vmask", 2), ("ctxT", DC * B * P),
        ("ctx", B * D), ("centroids", DC * EXPERTS), ("wr", DC * EXPERTS),
        ("bq1", DC), ("bk1", DC), ("bvs2", DC), ("bq2", DC), ("bk2", DC), ("lin1_b", FC), ("bq3", DC), ("bk3", DC),
        ("enc_b", 4), ("s2c_b", 1), ("eb1", EXPERTS * FC), ("base0", EXPERTS), ("tstart", 24), ("nibble", 15), ("lower", 64),
        ("causal", 2 * KEYS)]
PROJ = [("wq", DC * D), ("wk", DC * D), ("wv", DC * D), ("wo", DC * D)]
SEC1 = PROJ
SEC2 = [("vs", DC * D), ("os", DC * D)] + PROJ + [("lin1", DC * F), ("lin2", FC * D), ("tern", DC * D)]
SEC3 = PROJ + [("enc", DC * 512), ("s2c", 4 * 64), ("we2", 16 * 64), ("dec", 4 * D)]
SEC65 = [("rw1", 64), ("rw2", EXPERTS), ("we1", EXPERTS * 256), ("c2s", 512)]
ROWS = [(n, D) for n in ("ln_g0", "ln_b0", "bv1", "bo1", "bos2", "g1", "b1", "bv2", "bo2", "g2", "b2", "lin2_b",
                         "g3", "b3", "gamma", "beta", "bv3", "bo3", "dec_b", "ln_g3", "ln_b3")] \
    + [("be2", EXPERTS * 64)]


class Kit:

    def part(self, name):
        for table, buf in self.packs:
            at, _ = offsets(table)
            if name in at:
                return buf[:, at[name][0]:at[name][0] + at[name][1]]
        raise KeyError(name)


class Norm:

    def __init__(self, k, sb, sem, name):
        self.nc, self.neghalf, self.eps, self.spare = k.nc, k.neghalf, k.eps, k.spare
        self.st, self.mv, self.rstd = sb(name + "_st", [P, 12]), sb(name + "_mv", [P, 4]), sb(name + "_rstd", [P, 2])
        self.stats_done = sem(name + "_stats_done")
        self.rstd_done = sem(name + "_rstd_done")
        self.done = sem(name + "_done")

    def stats(self, dve, src, t, q):
        self.nc.vector.bn_stats(self.st[:, 6 * q:6 * q + 6], src).then_inc(self.stats_done, 1)
        wait_apart(self.nc, dve, self.stats_done, t * 2 + 1, self.spare)
        self.nc.vector.bn_aggr(self.mv[:, 2 * q:2 * q + 2], self.st[:, 6 * q:6 * q + 6]).then_inc(self.stats_done, 1)

    def power(self, pool, t, q):
        pool.wait_ge(self.stats_done, t * 2 + 2)
        at_least(pool, self.done, t - 1)
        self.nc.gpsimd.tensor_tensor(self.rstd[:, q:q + 1], self.mv[:, 2 * q + 1:2 * q + 2], self.eps,
                                     ALU.add).then_inc(self.rstd_done, 1)
        pool.wait_ge(self.rstd_done, t * 2 + 1)
        self.nc.gpsimd.tensor_tensor(self.rstd[:, q:q + 1], self.rstd[:, q:q + 1], self.neghalf,
                                     ALU.pow).then_inc(self.rstd_done, 1)

    def apply(self, dve, out, src, t, q):
        dve.wait_ge(self.rstd_done, t * 2 + 2)
        self.nc.vector.tensor_scalar(out, src, self.mv[:, 2 * q:2 * q + 1], self.rstd[:, q:q + 1],
                                     ALU.subtract, ALU.mult).then_inc(self.done, 1)


class Flip:

    def __init__(self, k, sem, name, bank):
        self.nc, self.ident, self.bank = k.nc, k.ident, bank
        self.turned, self.copied = sem(name + "_turned"), sem(name + "_copied")

    def turn(self, pe, src, t, pieces=DC):
        at_least(pe, self.copied, t)
        for c in range(pieces):
            last = self.nc.tensor.transpose(self.bank[:, c * P:(c + 1) * P], src(c), self.ident)
        last.then_inc(self.turned, 1)

    def copy(self, act, dst, t, pieces=DC):
        act.wait_ge(self.turned, t + 1)
        self.nc.scalar.activation(dst, self.bank[:, 0:pieces * P], ACT.Copy).then_inc(self.copied, 1)


def stage_tools(ctx, k, name):
    used = []

    def sb(n, shape, dtype=FP32):
        return ctx.enter_context(k.nc.sbuf_tensor(f"{name}_{n}", shape, dtype))

    def sem(n):
        used.append(k.nc.alloc_semaphore(f"{name}_{n}"))
        return used[-1]

    def clear():
        k.nc.clear_and_free_semaphores(used)
        k.nc.all_engine_barrier(sem_only=True)
    ctx.callback(clear)
    return sb, sem


def part_of(table, buf, name):
    at, _ = offsets(table)
    return buf[:, at[name][0]:at[name][0] + at[name][1]]


def run_lagged(u, steps, tiles=TILES):
    for par in range(2):
        for lag, step in steps:
            if (at := lagged(u, par, lag, tiles)) is not None:
                step(*at)

GROUP = 256
SORTED = T + (EXPERTS - 1) * GROUP



def context_attention(k):
    nc, x, ps = k.nc, k.x, k.ps
    with ExitStack() as ctx:
        sb, sem = stage_tools(ctx, k, "ca")
        ln = Norm(k, sb, sem, "ln")
        h, hT = sb("h", [P, 2 * D]), sb("hT", [P, 2 * D])
        mask, use_mask = sb("mask", [P, TILES * KEYS]), sb("use_mask", [P, KEYS], I32)
        logit, prob, attn = sb("logit", [P, 2 * KEYS]), sb("prob", [P, 2 * KEYS]), sb("attn", [P, 2 * P])
        negmax, total, rtotal = sb("negmax", [P, 2]), sb("total", [P, 2]), sb("rtotal", [P, 2])
        attnT = sb("attnT", [KEYS, P])
        flip = Flip(k, sem, "h", ps[0])
        tile_mask, mask_placed = sb("tile_mask", [P, 2 * KEYS]), sem("mask_placed")
        zeros = sb("zeros", [P, D])
        CHUNKS = 8
        chunk_loaded = [sem(f"chunk_loaded{c}") for c in range(CHUNKS)]
        tiles_loaded = sem("tiles_loaded")
        rest_loaded = sem("rest_loaded")
        scored = sem("scored")
        soft = sem("soft")
        exped = sem("exped")
        attended = sem("attended")
        a_turned, a_copied = sem("a_turned"), sem("a_copied")
        mixed = sem("mixed")
        x_done = sem("x_done")
        SOFT = 4
        ctxT = k.part("ctxT").rearrange("p (c b j) -> p c b j", c=DC, b=B)
        ctx_rows = k.part("ctx").rearrange("p (b d) -> p b d", b=B)

        with nc.Block() as block:

            @block.sync
            def _(sp):
                sp.dma_start(k.sec0[:, :], k.d_sec0).then_inc(k.loaded0, 16)

                for c in range(CHUNKS):
                    n = TILES // CHUNKS
                    rows = slice(c * n * P, (c + 1) * n * P)
                    sp.dma_start(x[:, c * n * D:(c + 1) * n * D].rearrange("p (t d) -> p t d", d=D),
                                 k.d_x[rows, :].rearrange("(t p) d -> p t d", p=P)).then_inc(chunk_loaded[c], 16)
                    sp.dma_start(mask[:, c * n * KEYS:(c + 1) * n * KEYS].rearrange("p (t j) -> p t j", j=KEYS),
                                 k.d_mask[rows, :].rearrange("(t p) j -> p t j", p=P)).then_inc(chunk_loaded[c], 16)
                for c in range(CHUNKS):
                    sp.wait_ge(chunk_loaded[c], 32)
                    sp.sem_inc(tiles_loaded, TILES // CHUNKS)
                sp.wait_ge(k.set_up, 5)
                for r in range(T, SORTED, P):
                    sp.dma_start(k.d_rows_in[r:r + P, :], zeros[:, :]).then_inc(rest_loaded, 16)
                sp.dma_start(k.rows[:, :], k.d_rows.partition_broadcast(P)).then_inc(rest_loaded, 16)
                sp.dma_start(k.secA[:, 0:offsets(SEC1)[1]], k.d_sec1).then_inc(rest_loaded, 16)
                sp.dma_start(k.sec2[:, :], k.d_sec2).then_inc(rest_loaded, 16)
                sp.dma_start(k.sec65[:, :], k.d_sec65).then_inc(rest_loaded, 16)
                sp.wait_ge(rest_loaded, 64 + (SORTED - T) // P * 16)

            @block.gpsimd
            def _(pool):
                nc.gpsimd.memset(k.neghalf, -0.5).then_inc(k.set_up, 1)
                nc.gpsimd.memset(k.ones[:, :], 1.0).then_inc(k.set_up, 1)
                nc.gpsimd.memset(k.eps, LN_EPS).then_inc(k.set_up, 1)
                nc.gpsimd.memset(zeros[:, :], 0.0).then_inc(k.set_up, 1)
                pool.wait_ge(k.set_up, 5)

                def place_mask(t, q, _):
                    pool.wait_ge(tiles_loaded, t + 1)
                    at_least(pool, soft, (t - 2) * SOFT + 3)
                    nc.gpsimd.tensor_copy(tile_mask[:, q * KEYS:(q + 1) * KEYS],
                                          mask[:, cols(t, KEYS)]).then_inc(mask_placed, 1)
                over_tiles(pool, lambda u: run_lagged(u, [(0, lambda t, q, _: ln.power(pool, t, q)), (1, place_mask)]), 1)

            @block.vector
            def _(dve):
                nc.vector.memset(attn[:, :], 0.0).then_inc(k.set_up, 1)
                dve.wait_ge(k.set_up, 5)
                dve.wait_ge(k.loaded0, 16)
                nc.vector.tensor_copy(k.ident16[:, :], k.ident)
                nc.vector.tensor_copy(k.causal, k.part("causal").rearrange("p (a j) -> p a j", a=2))

                def stats(t, q, _):
                    dve.wait_ge(tiles_loaded, t + 1)
                    ln.stats(dve, x[:, cols(t)], t, q)

                def apply(t, q, _):
                    at_least(dve, flip.turned, t - 1)
                    ln.apply(dve, h[:, q * D:(q + 1) * D], x[:, cols(t)], t, q)

                def soften(t, q, _):
                    s = logit[:, q * KEYS:(q + 1) * KEYS]
                    m = tile_mask[:, q * KEYS:(q + 1) * KEYS]
                    dve.wait_ge(mask_placed, t + 1)
                    dve.wait_ge(scored, t + 1)
                    at_least(dve, exped, t - 1)
                    nc.vector.tensor_scalar(s, ps[2 + q][:, 0:KEYS], D ** -0.5, None, ALU.mult).then_inc(soft, 1)
                    nc.vector.tensor_scalar(use_mask[:, :], m, -1.0, None, ALU.is_lt).then_inc(soft, 1)
                    wait_apart(nc, dve, soft, t * SOFT + 2, k.spare)
                    nc.vector.copy_predicated(s, use_mask[:, :], m).then_inc(soft, 1)
                    dve.wait_ge(soft, t * SOFT + 3)
                    nc.vector.tensor_reduce(negmax[:, q:q + 1], s, AX, ALU.max, negate=True).then_inc(soft, 1)

                def weigh(t, q, _):
                    dve.wait_ge(exped, t + 1)
                    nc.vector.reciprocal(rtotal[:, q:q + 1], total[:, q:q + 1]).then_inc(attended, 1)
                    dve.wait_ge(attended, t * 2 + 1)
                    at_least(dve, a_turned, t - 1)
                    nc.vector.tensor_scalar(attn[:, q * P:q * P + KEYS], prob[:, q * KEYS:(q + 1) * KEYS],
                                            rtotal[:, q:q + 1], 0.0, ALU.mult, ALU.max).then_inc(attended, 1)

                def add(t, q, _):
                    dve.wait_ge(mixed, t + 1)
                    nc.vector.tensor_tensor(x[:, cols(t)], ps[6 + q][:, 0:D], x[:, cols(t)], ALU.add).then_inc(x_done, 1)
                over_tiles(dve, lambda u: run_lagged(u, [(1, apply), (3, weigh), (2, soften), (0, stats), (5, add)]), 5)

            @block.scalar
            def _(act):
                def copy_h(t, q, _):
                    at_least(act, scored, t - 1)
                    flip.copy(act, hT[:, q * D:(q + 1) * D], t)

                def copy_attention(t, q, _):
                    act.wait_ge(a_turned, t + 1)
                    at_least(act, mixed, t)
                    nc.scalar.activation(attnT[:, :], ps[4][0:KEYS, 0:P], ACT.Copy).then_inc(a_copied, 1)

                def exponential(t, q, _):
                    act.wait_ge(soft, t * SOFT + 4)
                    at_least(act, attended, (t - 1) * 2)
                    nc.scalar.activation(prob[:, q * KEYS:(q + 1) * KEYS], logit[:, q * KEYS:(q + 1) * KEYS],
                                         ACT.Exp, bias=negmax[:, q:q + 1],
                                         accum_out=total[:, q:q + 1]).then_inc(exped, 1)
                over_tiles(act, lambda u: run_lagged(u, [(1, copy_h), (4, copy_attention), (2, exponential)]), 4)

            @block.tensor
            def _(pe):
                pe.wait_ge(k.loaded0, 16)
                pe.wait_ge(k.set_up, 5)

                def turn_h(t, q, _):
                    pe.wait_ge(ln.done, t + 1)
                    flip.turn(pe, lambda c: h[:, q * D + c * P:q * D + (c + 1) * P], t)

                def turn_attention(t, q, _):
                    pe.wait_ge(attended, t * 2 + 2)
                    at_least(pe, a_copied, t)
                    nc.tensor.transpose(ps[4][:, 0:P], attn[:, q * P:(q + 1) * P], k.ident).then_inc(a_turned, 1)

                def score(t, q, _):
                    pe.wait_ge(flip.copied, t + 1)
                    at_least(pe, soft, (t - 2) * SOFT + 1)
                    for c in range(DC):
                        last = nc.tensor.matmul(ps[2 + q][:, 0:KEYS], hT[:, q * D + c * P:q * D + (c + 1) * P],
                                                ctxT[:, c, bass.ds(t // TPB, 1), 0:KEYS],
                                                start=(c == 0), stop=(c == DC - 1))
                    last.then_inc(scored, 1)

                def mix(t, q, _):
                    pe.wait_ge(a_copied, t + 1)
                    at_least(pe, x_done, t - 1)
                    nc.tensor.matmul(ps[6 + q][:, 0:D], attnT[:, :], ctx_rows[0:KEYS, bass.ds(t // TPB, 1), :],
                                     start=True, stop=True).then_inc(mixed, 1)
                over_tiles(pe, lambda u: run_lagged(u, [(1, turn_h), (4, turn_attention), (1, score), (4, mix)]), 4)



def head_attention(k, name, heads, table, buf, bq, bk, bv, bo, src, normalised, causal=False, loads=()):
    nc, ps, ident = k.nc, k.ps, k.ident
    hd = D // heads
    hpc = heads // DC
    pairs = heads // 2
    W = 2 * hd + 2
    SC = hpc * KEYS
    part = lambda n: part_of(table, buf, n).rearrange("p (c o) -> p c o", c=DC)
    wq, wk, wv, wo = part("wq"), part("wk"), part("wv"), part("wo")
    hmask = k.part("hmask16" if heads == 16 else "hmask8")
    vmask = k.part("vmask")
    ctxT = k.part("ctxT").rearrange("p (c b j) -> p c b j", c=DC, b=B)
    bq, bk = k.part(bq), k.part(bk)
    bv, bo = part_of(ROWS, k.rows, bv), part_of(ROWS, k.rows, bo)
    with ExitStack() as ctx:
        sb, sem = stage_tools(ctx, k, name)
        kT = sb("kT", [P, DC * B * KEYS])
        kbd = sb("kbd", [P, B * DC * SC])
        v = sb("v", [P, B * D])
        vbd = sb("vbd", [P, B * pairs * W])
        h = sb("h", [P, 2 * D])
        hT, qT = sb("hT", [P, 2 * D]), sb("qT", [P, 2 * D])
        p = sb("p", [P, 2 * DC * SC])
        pT = sb("pT", [P, 2 * DC * SC])
        mx, rs = sb("mx", [P, heads]), sb("rs", [P, heads])
        o, oT = sb("o", [P, D]), sb("oT", [P, D])
        ln = Norm(k, sb, sem, "ln") if normalised else None
        h_set = ln.done if normalised else sem("h_set")
        flip, oflip = Flip(k, sem, "h", ps[4]), Flip(k, sem, "o", ps[7])
        kv_made, kv_set = sem("kv_made"), sem("kv_set")
        q_made, q_set = sem("q_made"), sem("q_set")
        scored = sem("scored")
        shifted = sem("shifted")
        exped = sem("exped")
        p_turned, p_copied = sem("p_turned"), sem("p_copied")
        mixed = sem("mixed")
        scaled = sem("scaled")
        projected = sem("projected")
        biased = sem("biased")
        added = sem("added")
        more_loaded = sem("more_loaded")
        v3 = vbd[:, :].rearrange("p (b j w) -> p b j w", b=B, j=pairs)
        k4 = kbd[:, :].rearrange("p (b c s) -> p b c s", b=B, c=DC)
        KV = 2 + B * DC + B + B + 1

        with nc.Block() as block:

            @block.sync
            def _(sp):
                for to, of in loads:
                    sp.dma_start(to, of).then_inc(more_loaded, 16)
                if loads:
                    sp.wait_ge(more_loaded, 16 * len(loads))

            @block.tensor
            def _(pe):
                for m in range(DC):
                    for c in range(DC):
                        nc_last = nc.tensor.matmul(ps[m][:, 0:B * KEYS], wk[:, c, m * P:(m + 1) * P],
                                                   ctxT[:, c, :, 0:KEYS], start=(c == 0), stop=(c == DC - 1))
                    nc_last.then_inc(kv_made, 1)
                for b in range(B):
                    for c in range(DC):
                        nc_last = nc.tensor.matmul(ps[2 + b][:, 0:D], ctxT[:, c, b, :], wv[:, c, :],
                                                   start=(c == 0), stop=(c == DC - 1))
                    nc_last.then_inc(kv_made, 1)
                pe.wait_ge(kv_set, KV)

                def mix(t, q, n):
                    pe.wait_ge(p_copied, t * 2 + 2)
                    at_least(pe, scaled, t * 2)
                    for j in range(pairs):
                        last = nc.tensor.matmul(ps[6][:, j * W:(j + 1) * W],
                                                pT[:, q * DC * SC + j * P:q * DC * SC + (j + 1) * P],
                                                v3[:, bass.ds(t // TPB, 1), j, :], start=True, stop=True)
                    last.then_inc(mixed, 1)

                def turn_h(t, q, n):
                    pe.wait_ge(h_set, t + 1)
                    flip.turn(pe, lambda c: h[:, q * D + c * P:q * D + (c + 1) * P], t)

                def score(t, q, n):
                    for c in range(DC):
                        pe.wait_ge(q_set, t * 2 + c + 1)
                        at_least(pe, shifted, (t - 1) * 4 + c + 3)
                        last = nc.tensor.matmul(ps[c][:, 0:SC], qT[:, q * D + c * P:q * D + (c + 1) * P],
                                                k4[:, bass.ds(t // TPB, 1), c, :], start=True, stop=not causal)
                        if causal:
                            first = t % TPB
                            later = min(first, 1) if isinstance(first, int) else (first + TPB - 1) // TPB
                            last = nc.tensor.matmul(ps[c][:, 0:SC], k.ident16[:, :],
                                                    k.causal[:, bass.ds(later, 1), :].to_broadcast([P, hpc, KEYS]),
                                                    start=False, stop=True)
                        last.then_inc(scored, 1)

                def turn_o(t, q, n):
                    pe.wait_ge(scaled, t * 2 + 2)
                    at_least(pe, added, t)
                    oflip.turn(pe, lambda c: o[:, c * P:(c + 1) * P], t)

                def project_q(t, q, n):
                    pe.wait_ge(flip.copied, t + 1)
                    at_least(pe, q_set, t * 2)
                    for m in range(DC):
                        for c in range(DC):
                            last = nc.tensor.matmul(ps[5][:, m * P:(m + 1) * P], wq[:, c, m * P:(m + 1) * P],
                                                    hT[:, q * D + c * P:q * D + (c + 1) * P],
                                                    start=(c == 0), stop=(c == DC - 1))
                    last.then_inc(q_made, 1)

                def turn_p(t, q, n):
                    for c in range(DC):
                        pe.wait_ge(exped, t * 2 + c + 1)
                        at_least(pe, p_copied, (t - 1) * 2 + c + 1)
                        for j in range(hpc // 2):
                            at = (q * DC + c) * SC + j * P
                            last = nc.tensor.transpose(ps[2 + c][:, j * P:(j + 1) * P], p[:, at:at + P], ident)
                        last.then_inc(p_turned, 1)

                def project_o(t, q, n):
                    pe.wait_ge(oflip.copied, t + 1)
                    for c in range(DC):
                        last = nc.tensor.matmul(ps[7][:, D:2 * D], oT[:, c * P:(c + 1) * P], wo[:, c, :],
                                                start=(c == 0), stop=(c == DC - 1))
                    last.then_inc(projected, 1)

                over_tiles(pe, lambda u: run_lagged(u, [(4, mix), (1, turn_h), (2, score), (3, turn_p), (4, turn_o),
                                                        (1, project_q), (4, project_o)]), 4)

            @block.gpsimd
            def _(pool):
                def power(t, q, n):
                    ln.power(pool, t, q)

                def add_bias(t, q, n):
                    pool.wait_ge(h_set, t + 1)
                    nc.gpsimd.tensor_tensor(src[:, cols(t)], src[:, cols(t)], bo, ALU.add).then_inc(biased, 1)
                over_tiles(pool, lambda u: run_lagged(u, [(0, power)] * normalised + [(2, add_bias)]), 2)

            @block.vector
            def _(dve):
                for m in range(DC):
                    dve.wait_ge(kv_made, m + 1)
                    nc.vector.tensor_scalar(kT[:, m * D:(m + 1) * D], ps[m][:, 0:B * KEYS], bk[:, m:m + 1], None,
                                            ALU.add).then_inc(kv_set, 1)
                dve.wait_ge(kv_set, DC)
                for b in range(B):
                    for m in range(DC):
                        at = m * D + b * KEYS
                        nc.vector.tensor_tensor(
                            k4[:, b, m, :].rearrange("p (h j) -> p h j", h=hpc),
                            kT[:, at:at + KEYS].unsqueeze(1).to_broadcast([P, hpc, KEYS]),
                            hmask[:, 0:hpc].unsqueeze(2).to_broadcast([P, hpc, KEYS]), ALU.mult).then_inc(kv_set, 1)
                for b in range(B):
                    dve.wait_ge(kv_made, DC + b + 1)
                    nc.vector.tensor_tensor(v[:, b * D:(b + 1) * D], ps[2 + b][:, 0:D], bv, ALU.add).then_inc(kv_set, 1)
                dve.wait_ge(kv_set, DC + B * DC + B)
                for b in range(B):
                    nc.vector.tensor_tensor(
                        v3[:, b, :, 0:2 * hd].rearrange("p j (s d) -> p j s d", s=2),
                        v[:, b * D:(b + 1) * D].rearrange("p (j s d) -> p j s d", s=2, d=hd),
                        vmask.unsqueeze(1).unsqueeze(3).to_broadcast([P, pairs, 2, hd]), ALU.mult).then_inc(kv_set, 1)
                nc.vector.tensor_copy(vbd[:, :].rearrange("p (n w) -> p n w", w=W)[:, :, 2 * hd:W],
                                      vmask.unsqueeze(1).to_broadcast([P, B * pairs, 2])).then_inc(kv_set, 1)

                def scale_heads(t, q, n):
                    heads_ps = ps[6][:, 0:pairs * W].rearrange("p (j w) -> p j w", w=W)
                    dve.wait_ge(mixed, t + 1)
                    at_least(dve, scaled, t * 2)
                    nc.vector.reciprocal(rs[:, :].rearrange("p (j s) -> p j s", s=2),
                                         heads_ps[:, :, 2 * hd:W]).then_inc(scaled, 1)
                    dve.wait_ge(scaled, t * 2 + 1)
                    at_least(dve, oflip.turned, t)
                    nc.vector.tensor_tensor(
                        o[:, :].rearrange("p (j s d) -> p j s d", s=2, d=hd),
                        heads_ps[:, :, 0:2 * hd].rearrange("p j (s d) -> p j s d", s=2),
                        rs[:, :].rearrange("p (j s) -> p j s", s=2).unsqueeze(3).to_broadcast([P, pairs, 2, hd]),
                        ALU.mult).then_inc(scaled, 1)

                def shift(t, q, n):
                    s3 = [ps[c][:, 0:SC].rearrange("p (h j) -> p h j", j=KEYS) for c in range(DC)]
                    for c in range(DC):
                        dve.wait_ge(scored, t * 2 + c + 1)
                        at_least(dve, shifted, t * 4 + c - 1)
                        nc.vector.tensor_reduce(mx[:, c * hpc:(c + 1) * hpc], s3[c], AX, ALU.max).then_inc(shifted, 1)
                    for c in range(DC):
                        dve.wait_ge(shifted, t * 4 + c + 1)
                        at_least(dve, p_turned, (t - 2) * 2 + c + 1)
                        at = (q * DC + c) * SC
                        nc.vector.tensor_tensor(p[:, at:at + SC].rearrange("p (h j) -> p h j", j=KEYS), s3[c],
                                                mx[:, c * hpc:(c + 1) * hpc].unsqueeze(2).to_broadcast([P, hpc, KEYS]),
                                                ALU.subtract).then_inc(shifted, 1)

                def stats(t, q, n):
                    ln.stats(dve, src[:, cols(t)], t, q)

                def add(t, q, n):
                    dve.wait_ge(projected, t + 1)
                    dve.wait_ge(biased, t + 1)
                    nc.vector.tensor_tensor(src[:, cols(t)], ps[7][:, D:2 * D], src[:, cols(t)],
                                            ALU.add).then_inc(added, 1)

                def apply(t, q, n):
                    at_least(dve, flip.turned, t - 1)
                    if normalised:
                        ln.apply(dve, h[:, q * D:(q + 1) * D], src[:, cols(t)], t, q)
                    else:
                        nc.vector.tensor_copy(h[:, q * D:(q + 1) * D], src[:, cols(t)]).then_inc(h_set, 1)
                over_tiles(dve, lambda u: run_lagged(u, [(1, apply), (4, scale_heads), (2, shift)]
                                                     + [(0, stats)] * normalised + [(4, add)]), 4)

            @block.scalar
            def _(act):
                def copy_h(t, q, n):
                    at_least(act, q_made, t - 1)
                    flip.copy(act, hT[:, q * D:(q + 1) * D], t)

                def copy_o(t, q, n):
                    at_least(act, projected, t)
                    oflip.copy(act, oT[:, :], t)

                def set_q(t, q, n):
                    act.wait_ge(q_made, t + 1)
                    at_least(act, scored, (t - 1) * 2)
                    for m in range(DC):
                        nc.scalar.activation(qT[:, q * D + m * P:q * D + (m + 1) * P], ps[5][:, m * P:(m + 1) * P],
                                             ACT.Identity, bias=bq[:, m:m + 1]).then_inc(q_set, 1)

                def copy_p(t, q, n):
                    at_least(act, mixed, t - 1)
                    for c in range(DC):
                        act.wait_ge(p_turned, t * 2 + c + 1)
                        at = (q * DC + c) * SC
                        nc.scalar.activation(pT[:, at:at + SC], ps[2 + c][:, 0:SC], ACT.Copy).then_inc(p_copied, 1)

                def exponential(t, q, n):
                    for c in range(DC):
                        act.wait_ge(shifted, t * 4 + c + 3)
                        at = (q * DC + c) * SC
                        nc.scalar.activation(p[:, at:at + SC], p[:, at:at + SC], ACT.Exp,
                                             scale=hd ** -0.5).then_inc(exped, 1)
                over_tiles(act, lambda u: run_lagged(u, [(1, copy_h), (3, copy_p), (4, copy_o), (1, set_q),
                                                         (2, exponential)]), 4)



def balanced_scores(k, rows, scores):
    nc, x, ps = k.nc, k.x, k.ps
    gain, shift = part_of(ROWS, k.rows, "ln_g0"), part_of(ROWS, k.rows, "ln_b0")
    centroids = k.part("centroids").rearrange("p (c e) -> p c e", c=DC)
    by_expert = scores[:, :].rearrange("p (e t) -> p e t", t=TILES)
    with ExitStack() as ctx:
        sb, sem = stage_tools(ctx, k, "bs")
        outer, inner = Norm(k, sb, sem, "outer"), Norm(k, sb, sem, "inner")
        n, hT = sb("n", [P, 2 * D]), sb("hT", [P, 2 * D])
        flip = Flip(k, sem, "n", ps[0])
        x_added = sem("x_added")
        affine = sem("affine")
        kept = sem("kept")
        scored, score_set = sem("scored"), sem("score_set")

        with nc.Block() as block:

            @block.vector
            def _(dve):
                def stats(t, q, _):
                    outer.stats(dve, x[:, cols(t)], t, q)

                def apply(t, q, _):
                    outer.apply(dve, rows[:, cols(t)], x[:, cols(t)], t, q)
                    wait_apart(nc, dve, outer.done, t + 1, k.spare)
                    inner.stats(dve, rows[:, cols(t)], t, q)

                def apply_inner(t, q, _):
                    dve.wait_ge(x_added, t + 1)
                    at_least(dve, affine, t * 2 - 2)
                    at_least(dve, flip.turned, t - 1)
                    at_least(dve, kept, t - 1)
                    inner.apply(dve, n[:, q * D:(q + 1) * D], rows[:, cols(t)], t, q)

                def add_h(t, q, _):
                    dve.wait_ge(outer.done, t + 1)
                    nc.vector.tensor_tensor(x[:, cols(t)], x[:, cols(t)], rows[:, cols(t)], ALU.add).then_inc(x_added, 1)
                over_tiles(dve, lambda u: run_lagged(u, [(0, stats), (3, apply_inner), (1, apply), (1, add_h)]), 3)

            @block.gpsimd
            def _(pool):
                def power(t, q, _):
                    outer.power(pool, t, q)

                def power_inner(t, q, _):
                    inner.power(pool, t, q)

                def scale(t, q, _):
                    part = n[:, q * D:(q + 1) * D]
                    pool.wait_ge(inner.done, t + 1)
                    nc.gpsimd.tensor_tensor(part, part, gain, ALU.mult).then_inc(affine, 1)
                    pool.wait_ge(affine, t * 2 + 1)
                    nc.gpsimd.tensor_tensor(part, part, shift, ALU.add).then_inc(affine, 1)
                over_tiles(pool, lambda u: run_lagged(u, [(0, power), (4, scale), (2, power_inner)]), 4)

            @block.scalar
            def _(act):
                def keep(t, q, _):
                    act.wait_ge(affine, t * 2 + 2)
                    nc.scalar.activation(rows[:, cols(t)], n[:, q * D:(q + 1) * D], ACT.Copy).then_inc(kept, 1)

                def copy(t, q, _):
                    at_least(act, scored, t - 1)
                    flip.copy(act, hT[:, q * D:(q + 1) * D], t)

                def set_scores(t, q, _):
                    act.wait_ge(scored, t + 1)
                    nc.scalar.activation(by_expert[:, :, bass.ds(t, 1)], ps[2 + q][:, 0:EXPERTS].unsqueeze(2),
                                         ACT.Copy).then_inc(score_set, 1)
                over_tiles(act, lambda u: run_lagged(u, [(5, set_scores), (4, keep), (4, copy)]), 5)

            @block.tensor
            def _(pe):
                def turn(t, q, _):
                    pe.wait_ge(affine, t * 2 + 2)
                    flip.turn(pe, lambda c: n[:, q * D + c * P:q * D + (c + 1) * P], t)

                def score(t, q, _):
                    pe.wait_ge(flip.copied, t + 1)
                    at_least(pe, score_set, t - 1)
                    for c in range(DC):
                        last = nc.tensor.matmul(ps[2 + q][:, 0:EXPERTS], hT[:, q * D + c * P:q * D + (c + 1) * P],
                                                centroids[:, c, :], start=(c == 0), stop=(c == DC - 1))
                    last.then_inc(scored, 1)
                over_tiles(pe, lambda u: run_lagged(u, [(4, turn), (4, score)]), 4)


def balanced_assignment(k, scores):
    nc, ps = k.nc, k.ps
    NIB, ROUNDS = 15, 8
    SHARE = T // EXPERTS
    onehot = k.onehot[:, :].rearrange("p (e t) -> p e t", t=TILES)
    by_expert = scores[:, :].rearrange("p (e t) -> p e t", t=TILES)
    with ExitStack() as ctx:
        sb, sem = stage_tools(ctx, k, "ba")
        left, taken = sb("left", [P, TILES]), sb("taken", [P, TILES])
        nibble = sb("nibble", [P, NIB], I32)
        steps = sb("steps", [P, ROUNDS * NIB], I32)
        prefix, digit, fixed = sb("prefix", [P, 1], I32), sb("digit", [P, 1], I32), sb("fixed", [P, 1], I32)
        cand, sign, bits = sb("cand", [P, NIB], I32), sb("sign", [P, NIB], I32), sb("bits", [P, NIB], I32)
        above = sb("above", [P, NIB * TILES])
        count, over, digitf = sb("count", [P, NIB]), sb("over", [P, NIB]), sb("digitf", [P, 1])
        equal, before = sb("equal", [P, TILES + 1]), sb("before", [P, TILES + 1])
        scan = sb("scan", [P, TILES])
        gt, ranks_ok, limit = sb("gt", [P, TILES]), sb("ranks_ok", [P, TILES]), sb("limit", [P, 1])
        chain = sem("chain")
        counted, summed = sem("counted"), sem("summed")
        ranked_in, ranked = sem("ranked_in"), sem("ranked")
        EXPERT = 95

        def ordered_to_float(step, bits, cand, sign):
            step(nc.vector.tensor_scalar(sign, cand, -1, 31, ALU.bitwise_xor, ALU.arith_shift_right))
            step(nc.vector.scalar_tensor_tensor(bits, sign, -2 ** 31, cand, ALU.bitwise_or, ALU.bitwise_xor))

        with nc.Block() as block:

            @block.vector
            def _(dve):
                done = [0]

                def step(ins, e=0):
                    done[0] += 1
                    ins.then_inc(chain, 1)
                    dve.wait_ge(chain, e * EXPERT + done[0])

                step(nc.vector.tensor_copy(nibble[:, :], k.part("nibble")))
                for r in range(ROUNDS):
                    step(nc.vector.tensor_scalar(steps[:, r * NIB:(r + 1) * NIB], nibble[:, :], 28 - 4 * r, None,
                                                 ALU.logical_shift_left))
                step(nc.vector.memset(taken[:, :], 0.0))
                step(nc.vector.memset(equal[:, :], 0.0))
                head = done[0]

                def expert(e):
                    done[0] = head

                    def st(ins):
                        step(ins, e)
                    st(nc.vector.scalar_tensor_tensor(left[:, :], taken[:, :], -3e38,
                                                      by_expert[:, bass.ds(e, 1), :].squeeze(1), ALU.mult, ALU.add))
                    st(nc.vector.memset(prefix[:, :], 0))
                    for r in range(ROUNDS):
                        st(nc.vector.tensor_tensor(cand[:, :], steps[:, r * NIB:(r + 1) * NIB],
                                                   prefix[:, :].to_broadcast([P, NIB]), ALU.bitwise_or))
                        ordered_to_float(st, bits[:, :], cand[:, :], sign[:, :])
                        st(nc.vector.tensor_tensor(
                            above[:, :].rearrange("p (c t) -> p c t", t=TILES),
                            left[:, :].unsqueeze(1).to_broadcast([P, NIB, TILES]),
                            bits[:, :].bitcast(FP32).unsqueeze(2).to_broadcast([P, NIB, TILES]), ALU.is_ge))
                        nc.vector.tensor_reduce(count[:, :], above[:, :].rearrange("p (c t) -> p c t", t=TILES),
                                                AX, ALU.add).then_inc(counted, 1)
                        dve.wait_ge(summed, e * ROUNDS + r + 1)
                        st(nc.vector.tensor_scalar(over[:, :], ps[0][:, 0:NIB], SHARE - 0.5, None, ALU.is_ge))
                        st(nc.vector.tensor_reduce(digitf[:, :], over[:, :], AX, ALU.add))
                        st(nc.vector.tensor_copy(digit[:, :], digitf[:, :]))
                        st(nc.vector.tensor_scalar(fixed[:, :], digit[:, :], 28 - 4 * r, None, ALU.logical_shift_left))
                        st(nc.vector.tensor_tensor(prefix[:, :], prefix[:, :], fixed[:, :], ALU.bitwise_or))
                    ordered_to_float(st, bits[:, 0:1], prefix[:, :], sign[:, 0:1])
                    lowest = bits[:, 0:1].bitcast(FP32)
                    st(nc.vector.tensor_scalar(gt[:, :], left[:, :], lowest, None, ALU.is_gt))
                    st(nc.vector.tensor_scalar(equal[:, 0:TILES], left[:, :], lowest, None, ALU.is_equal))
                    st(nc.vector.tensor_reduce(before[:, TILES:TILES + 1], gt[:, :], AX, ALU.add))
                    src, dst = equal[:, 0:TILES], scan[:, :]
                    for s in (1, 2, 4, 8, 16):
                        st(nc.vector.tensor_copy(dst[:, 0:s], src[:, 0:s]))
                        st(nc.vector.tensor_tensor(dst[:, s:TILES], src[:, s:TILES], src[:, 0:TILES - s], ALU.add))
                        src, dst = dst, (before[:, 0:TILES] if s in (1, 4) else scan[:, :])
                    nc.vector.tensor_tensor(before[:, 0:TILES], src, equal[:, 0:TILES],
                                            ALU.subtract).then_inc(ranked_in, 1)
                    dve.wait_ge(ranked, e + 1)
                    st(nc.vector.tensor_scalar(limit[:, :], ps[1][:, TILES:TILES + 1], -1.0, float(SHARE),
                                               ALU.mult, ALU.add))
                    st(nc.vector.tensor_scalar(ranks_ok[:, :], ps[1][:, 0:TILES], limit[:, :], None, ALU.is_lt))
                    st(nc.vector.tensor_tensor(ranks_ok[:, :], ranks_ok[:, :], equal[:, 0:TILES], ALU.mult))
                    st(nc.vector.tensor_tensor(gt[:, :], gt[:, :], ranks_ok[:, :], ALU.add))
                    st(nc.vector.tensor_copy(onehot[:, bass.ds(e, 1), :].squeeze(1), gt[:, :]))
                    st(nc.vector.tensor_tensor(taken[:, :], taken[:, :], gt[:, :], ALU.add))
                    assert done[0] - head == EXPERT, done[0] - head
                    done[0] = head

                expert(0)
                with dve.Fori(1, EXPERTS - 1) as e:
                    expert(e)
                nc.vector.tensor_scalar(onehot[:, EXPERTS - 1, :], taken[:, :], -1.0, 1.0, ALU.mult, ALU.add)

            @block.tensor
            def _(pe):
                def expert(e):
                    for r in range(ROUNDS):
                        pe.wait_ge(counted, e * ROUNDS + r + 1)
                        nc.tensor.matmul(ps[0][:, 0:NIB], k.ones[:, :], count[:, :], start=True,
                                         stop=True).then_inc(summed, 1)
                    pe.wait_ge(ranked_in, e + 1)
                    nc.tensor.matmul(ps[1][:, 0:TILES + 1], k.part("tri"), equal[:, :], start=True, stop=False)
                    nc.tensor.matmul(ps[1][:, 0:TILES + 1], k.ones[:, :], before[:, :], start=False,
                                     stop=True).then_inc(ranked, 1)
                expert(0)
                with pe.Fori(1, EXPERTS - 1) as e:
                    expert(e)


def place(k, rows, name, padded):
    nc, ps = k.nc, k.ps
    NG = SORTED // GROUP
    with ExitStack() as ctx:
        sb, sem = stage_tools(ctx, k, name)
        bufs = [sb(f"scan{i}", [P, EXPERTS * TILES]) for i in range(2)]
        before, spread = sb("before", [P, EXPERTS * TILES]), sb("spread", [P, EXPERTS * TILES])
        totals, posf, base = sb("totals", [P, EXPERTS]), sb("posf", [P, TILES]), sb("base", [P, EXPERTS])
        size, sizei, at_or_past = sb("size", [P, EXPERTS]), sb("sizei", [P, EXPERTS], I32), sb("past", [P, NG * 7])
        groupf = sb("groupf", [P, NG])
        chain, scanned, ranked, placed, sent = sem("chain"), sem("scanned"), sem("ranked"), sem("placed"), sem("sent")
        three = lambda a: a[:, :].rearrange("p (e t) -> p e t", t=TILES)

        with nc.Block() as block:

            @block.vector
            def _(dve):
                done = [0]

                def step(ins):
                    done[0] += 1
                    ins.then_inc(chain, 1)
                    dve.wait_ge(chain, done[0])
                src = three(k.onehot)
                for i, s in enumerate((1, 2, 4, 8, 16)):
                    dst = three(bufs[i % 2])
                    step(nc.vector.tensor_copy(dst[:, :, 0:s], src[:, :, 0:s]))
                    step(nc.vector.tensor_tensor(dst[:, :, s:TILES], src[:, :, s:TILES], src[:, :, 0:TILES - s], ALU.add))
                    src = dst
                step(nc.vector.tensor_copy(totals[:, :].unsqueeze(2), src[:, :, TILES - 1:TILES]))
                nc.vector.tensor_tensor(three(before), src, three(k.onehot), ALU.subtract).then_inc(scanned, 1)
                dve.wait_ge(ranked, 1)
                if padded:
                    step(nc.vector.tensor_scalar(sizei[:, :], ps[1][:, 0:EXPERTS], GROUP - 1.0, None, ALU.add))
                    step(nc.vector.tensor_scalar(sizei[:, :], sizei[:, :], -GROUP, None, ALU.bitwise_and))
                    step(nc.vector.tensor_copy(size[:, :], sizei[:, :]))
                    step(nc.vector.memset(base[:, :], 0.0))
                    for e in range(1, EXPERTS):
                        step(nc.vector.tensor_tensor(base[:, e:e + 1], base[:, e - 1:e], size[:, e - 1:e], ALU.add))
                    step(nc.vector.tensor_tensor(
                        at_or_past[:, :].rearrange("p (g e) -> p g e", e=7),
                        k.part("tstart")[:, 0:NG].unsqueeze(2).to_broadcast([P, NG, 7]),
                        base[:, 1:EXPERTS].unsqueeze(1).to_broadcast([P, NG, 7]), ALU.is_ge))
                    step(nc.vector.tensor_reduce(groupf[:, :], at_or_past[:, :].rearrange("p (g e) -> p g e", e=7),
                                                 AX, ALU.add))
                    step(nc.vector.tensor_copy(k.tile_expert[:, 0:NG], groupf[:, :]))
                    first = base[:, :]
                else:
                    first = k.part("base0")
                step(nc.vector.tensor_tensor(three(spread), ps[0][:, 0:EXPERTS * TILES].rearrange("p (e t) -> p e t", t=TILES),
                                             first.unsqueeze(2).to_broadcast([P, EXPERTS, TILES]), ALU.add))
                step(nc.vector.tensor_tensor(spread[:, :], spread[:, :], k.onehot[:, :], ALU.mult))
                step(nc.vector.tensor_reduce(posf[:, :], spread[:, :].rearrange("p (e t) -> p t e", t=TILES), AX, ALU.add))
                nc.vector.tensor_copy(k.pos[:, :], posf[:, :]).then_inc(placed, 1)

            @block.tensor
            def _(pe):
                pe.wait_ge(scanned, 1)
                nc.tensor.matmul(ps[0][:, 0:EXPERTS * TILES], k.part("tri"), k.onehot[:, :], start=True, stop=False)
                nc.tensor.matmul(ps[0][:, 0:EXPERTS * TILES], k.ones[:, :], before[:, :], start=False, stop=True)
                nc.tensor.matmul(ps[1][:, 0:EXPERTS], k.ones[:, :], totals[:, :], start=True,
                                 stop=True).then_inc(ranked, 1)

            @block.gpsimd
            def _(pool):
                pool.wait_ge(placed, 1)
                for t in range(TILES):
                    nc.gpsimd.indirect_dma_start(
                        out=k.d_rows_in, out_offset=bass.IndirectOffsetOnAxis(ap=k.pos[:, t:t + 1], axis=0),
                        in_=rows[:, t * D:(t + 1) * D], in_offset=None).then_inc(sent, 16)
                pool.wait_ge(sent, 16 * TILES)


def expert_ffn(k, name, w1, w2, func, tiles, sub, biased):
    nc, ps, ident = k.nc, k.ps, k.ident
    A = GROUP // P
    UN = 2 * sub
    with ExitStack() as ctx:
        sb, sem = stage_tools(ctx, k, name)
        w1s, w2s = sb("w1", [P, 2 * DC * F]), sb("w2", [P, 2 * FC * D])
        rows, rowsT = sb("rows", [P, 2 * A * D]), sb("rowsT", [P, 2 * DC * GROUP])
        hid, res = sb("hid", [P, FC * GROUP]), sb("res", [P, 2 * A * D])
        b2 = sb("b2", [P, 2 * D]) if biased else None
        b1, eb1, b1_set = sb("b1", [P, FC]), k.part("eb1"), sem("b1_set")
        weights_loaded = [sem("weights_loaded0"), sem("weights_loaded1")]
        rows_loaded = [sem("rows_loaded0"), sem("rows_loaded1")]
        res_stored = [sem("res_stored0"), sem("res_stored1")]
        turned, copied = sem("turned"), sem("copied")
        hid_made, hid_set = sem("hid_made"), sem("hid_set")
        res_made, res_set = sem("res_made"), sem("res_set")
        PAIRS = FC // 2

        def tile(u, i, lag):
            t = u * UN + (i - lag)
            if isinstance(t, int) and not 0 <= t < tiles:
                return None
            r = (i - lag) % UN
            back = (i - lag - r) // UN
            pair = u * sub + back * sub + r // 2
            return t, r % 2, r // sub % 2, pair, u + back, r

        def over(eng, steps):
            def body(u):
                for i in range(UN):
                    for lag, step in steps:
                        if (at := tile(u, i, lag)) is not None:
                            step(*at)
            lag = max(s[0] for s in steps)
            head = 2 if sub == 2 else 3
            for u in range(head):
                body(u)
            with eng.Fori(head, tiles // UN) as u:
                body(u)
            for u in range(tiles // UN, (tiles + lag + UN - 1) // UN):
                body(u)

        with nc.Block() as block:

            @block.gpsimd
            def _(pool):
                def load(t, q, g, pair, gp, r):
                    if r % sub == 0:
                        expert = gp * 2 + g if biased else pool.value_load(
                            k.tile_expert[0:1, t:t + 1] if isinstance(t, int) else k.tile_expert[0:1, bass.ds(t, 1)],
                            min_val=0, max_val=EXPERTS - 1)
                        at_least(pool, res_made, t - sub)
                        pool.dma_start(w1s[:, g * DC * F:(g + 1) * DC * F], w1[bass.ds(expert, 1)].squeeze(0))\
                            .then_inc(weights_loaded[g], 16)
                        pool.dma_start(w2s[:, g * FC * D:(g + 1) * FC * D], w2[bass.ds(expert, 1)].squeeze(0))\
                            .then_inc(weights_loaded[g], 16)
                        if biased:
                            at_least(pool, res_set, (t - sub) * A)
                            pool.dma_start(b2[:, g * D:(g + 1) * D], k.d_b2a[bass.ds(expert, 1)].squeeze(0)
                                           .partition_broadcast(P)).then_inc(weights_loaded[g], 16)
                    at_least(pool, turned, t - 1)
                    pool.dma_start(rows[:, q * A * D:(q + 1) * A * D].rearrange("p (a d) -> p a d", d=D),
                                   k.d_rows_in[bass.ds(t * GROUP, GROUP), :].rearrange("(a p) d -> p a d", p=P))\
                        .then_inc(rows_loaded[q], 16)

                over(pool, [(0, load)])

            @block.tensor
            def _(pe):
                def turn(t, q, g, pair, gp, r):
                    pe.wait_ge(rows_loaded[q], pair * 16 + 16)
                    at_least(pe, copied, t)
                    for a in range(A):
                        for c in range(DC):
                            at = q * A * D + a * D + c * P
                            last = nc.tensor.transpose(ps[0][:, c * GROUP + a * P:c * GROUP + (a + 1) * P],
                                                       rows[:, at:at + P], ident)
                    last.then_inc(turned, 1)

                def hidden(t, q, g, j):
                    at_least(pe, hid_set, t * PAIRS + j - 2)
                    for i in range(2):
                        f = 2 * j + i
                        for c in range(DC):
                            at = (g * DC + c) * F + f * P
                            last = nc.tensor.matmul(ps[1 + j % 3][:, i * GROUP:(i + 1) * GROUP], w1s[:, at:at + P],
                                                    rowsT[:, (q * DC + c) * GROUP:(q * DC + c + 1) * GROUP],
                                                    start=(c == 0), stop=(c == DC - 1))
                    last.then_inc(hid_made, 1)

                def result(t, q, g, j):
                    pe.wait_ge(hid_set, t * PAIRS + j + 1)
                    for f in (2 * j, 2 * j + 1):
                        for a in range(A):
                            at = f * GROUP + a * P
                            last = nc.tensor.matmul(ps[4 + 2 * q + a][:, 0:D], hid[:, at:at + P],
                                                    w2s[:, (g * FC + f) * D:(g * FC + f + 1) * D],
                                                    start=(f == 0), stop=(f == FC - 1))
                    return last

                def first(t, q, g, pair, gp, r):
                    if r % sub == 0:
                        pe.wait_ge(weights_loaded[g], (gp + 1) * (48 if biased else 32))
                    pe.wait_ge(copied, t + 1)
                    hidden(t, q, g, 0)
                    hidden(t, q, g, 1)
                    at_least(pe, res_set, (t - 1) * A)
                    for j in range(PAIRS - 1):
                        result(t, q, g, j)
                        if j + 2 < PAIRS:
                            hidden(t, q, g, j + 2)

                def last_pair(t, q, g, pair, gp, r):
                    result(t, q, g, PAIRS - 1).then_inc(res_made, 1)
                over(pe, [(1, first), (0, turn), (1, last_pair)])

            @block.scalar
            def _(act):
                def copy(t, q, g, pair, gp, r):
                    act.wait_ge(turned, t + 1)
                    at_least(act, hid_made, (t - 1) * PAIRS)
                    nc.scalar.activation(rowsT[:, q * DC * GROUP:(q + 1) * DC * GROUP], ps[0][:, :],
                                         ACT.Copy).then_inc(copied, 1)

                def gelu(t, q, g, pair, gp, r):
                    if biased and r % sub == 0:
                        at_least(act, hid_set, t * PAIRS)
                        nc.scalar.activation(b1[:, :], eb1[:, bass.ds((gp * 2 + g) * FC, FC)], ACT.Copy)\
                            .then_inc(b1_set, 1)
                        act.wait_ge(b1_set, gp * 2 + g + 1)
                    at_least(act, res_made, t)
                    for j in range(PAIRS):
                        act.wait_ge(hid_made, t * PAIRS + j + 1)
                        bank = ps[1 + j % 3]
                        if biased:
                            for i in range(2):
                                f = 2 * j + i
                                last = nc.scalar.activation(hid[:, f * GROUP:(f + 1) * GROUP],
                                                            bank[:, i * GROUP:(i + 1) * GROUP], func,
                                                            bias=b1[:, f:f + 1])
                        else:
                            last = nc.scalar.activation(hid[:, 2 * j * GROUP:2 * (j + 1) * GROUP], bank[:, :], func)
                        last.then_inc(hid_set, 1)
                def store(t, q, g, pair, gp, r):
                    act.wait_ge(res_set, t * A + A)
                    act.dma_start(k.d_rows_out[bass.ds(t * GROUP, GROUP), :].rearrange("(a p) d -> p a d", p=P),
                                   res[:, q * A * D:(q + 1) * A * D].rearrange("p (a d) -> p a d", d=D))\
                        .then_inc(res_stored[q], 16)
                over(act, [(2, store), (1, gelu), (0, copy)])
                act.wait_ge(res_stored[0], (tiles + 1) // 2 * 16)
                act.wait_ge(res_stored[1], tiles // 2 * 16)

            @block.vector
            def _(dve):
                def take(t, q, g, pair, gp, r):
                    dve.wait_ge(res_made, t + 1)
                    at_least(dve, res_stored[q], pair * 16)
                    for a in range(A):
                        to = res[:, (q * A + a) * D:(q * A + a + 1) * D]
                        if biased:
                            nc.vector.tensor_tensor(to, ps[4 + 2 * q + a][:, 0:D], b2[:, g * D:(g + 1) * D],
                                                    ALU.add).then_inc(res_set, 1)
                        else:
                            nc.vector.tensor_copy(to, ps[4 + 2 * q + a][:, 0:D]).then_inc(res_set, 1)
                over(dve, [(1, take)])


def collect(k, name, gate, used):
    nc, x = k.nc, k.x
    RING = 8
    with ExitStack() as ctx:
        sb, sem = stage_tools(ctx, k, name)
        got = sb("got", [P, RING * D])
        arrived = [sem(f"arrived{i}") for i in range(RING)]
        added = sem("added")

        with nc.Block() as block:

            @block.gpsimd
            def _(pool):
                for t in range(TILES):
                    r = t % RING
                    at_least(pool, added, t - RING + 1)
                    nc.gpsimd.indirect_dma_start(
                        out=got[:, r * D:(r + 1) * D], out_offset=None, in_=k.d_rows_out[0:used, :],
                        in_offset=bass.IndirectOffsetOnAxis(ap=k.pos[:, t:t + 1], axis=0)).then_inc(arrived[r], 16)

            @block.vector
            def _(dve):
                for t in range(TILES):
                    r = t % RING
                    dve.wait_ge(arrived[r], 16 * (t // RING + 1))
                    part = got[:, r * D:(r + 1) * D]
                    to = x[:, t * D:(t + 1) * D]
                    if gate is None:
                        nc.vector.tensor_tensor(to, part, to, ALU.add).then_inc(added, 1)
                    else:
                        nc.vector.scalar_tensor_tensor(to, part, gate[:, t:t + 1], to, ALU.mult,
                                                       ALU.add).then_inc(added, 1)


def layer0_ffn(k):
    with ExitStack() as ctx:
        rows = ctx.enter_context(k.nc.sbuf_tensor("rows0", [P, TILES * D], FP32))
        scores = ctx.enter_context(k.nc.sbuf_tensor("scores0", [P, EXPERTS * TILES], FP32))
        balanced_scores(k, rows, scores)
        balanced_assignment(k, scores)
        place(k, rows, "pl0", False)
    expert_ffn(k, "e0", k.d_w1a, k.d_w2a, ACT.Gelu_apprx_tanh, T // GROUP, 2, True)
    collect(k, "co0", None, T)



def route_top1(k, rows):
    nc, x, ps = k.nc, k.x, k.ps
    wr = k.part("wr").rearrange("p (c e) -> p c e", c=DC)
    onehot = k.onehot[:, :].rearrange("p (e t) -> p e t", t=TILES)
    with ExitStack() as ctx:
        sb, sem = stage_tools(ctx, k, "r1")
        ln = Norm(k, sb, sem, "ln")
        h, hT = sb("h", [P, 2 * D]), sb("hT", [P, 2 * D])
        logits, best = sb("logits", [P, TILES * EXPERTS]), sb("best", [P, TILES * 8])
        same, seen, lead = sb("same", [P, EXPERTS * TILES]), sb("seen", [P, TILES]), sb("lead", [P, TILES])
        flip = Flip(k, sem, "h", ps[0])
        kept, scored, logit_set = sem("kept"), sem("scored"), sem("logit_set")
        chain, led = sem("chain"), sem("led")

        with nc.Block() as block:

            @block.vector
            def _(dve):
                def stats(t, q, _):
                    ln.stats(dve, x[:, cols(t)], t, q)

                def apply(t, q, _):
                    at_least(dve, flip.turned, t - 1)
                    at_least(dve, kept, t - 1)
                    ln.apply(dve, h[:, q * D:(q + 1) * D], x[:, cols(t)], t, q)
                over_tiles(dve, lambda u: run_lagged(u, [(0, stats), (1, apply)]), 1)
                done = [0]

                def step(ins):
                    done[0] += 1
                    ins.then_inc(chain, 1)
                    dve.wait_ge(chain, done[0])
                dve.wait_ge(logit_set, TILES)
                for t in range(TILES):
                    last = nc.vector.max(best[:, t * 8:(t + 1) * 8], logits[:, t * EXPERTS:(t + 1) * EXPERTS])
                step(last)
                by_rank = best[:, :].rearrange("p (t r) -> p r t", r=8)
                nc.vector.tensor_tensor(lead[:, :], by_rank[:, 0, :], by_rank[:, 1, :], ALU.subtract).then_inc(led, 1)
                step(nc.vector.tensor_tensor(
                    same[:, :].rearrange("p (e t) -> p e t", t=TILES),
                    logits[:, :].rearrange("p (t e) -> p e t", e=EXPERTS),
                    by_rank[:, 0:1, :].to_broadcast([P, EXPERTS, TILES]), ALU.is_equal))
                step(nc.vector.memset(seen[:, :], 0.0))
                for e in range(EXPERTS):
                    mine = same[:, e * TILES:(e + 1) * TILES]
                    step(nc.vector.tensor_tensor(onehot[:, e, :], mine, seen[:, :], ALU.is_gt))
                    step(nc.vector.tensor_tensor(seen[:, :], seen[:, :], mine, ALU.max))

            @block.gpsimd
            def _(pool):
                over_tiles(pool, lambda u: run_lagged(u, [(0, lambda t, q, _: ln.power(pool, t, q))]), 0)

            @block.scalar
            def _(act):
                def keep(t, q, _):
                    act.wait_ge(ln.done, t + 1)
                    nc.scalar.activation(rows[:, cols(t)], h[:, q * D:(q + 1) * D], ACT.Copy).then_inc(kept, 1)

                def copy(t, q, _):
                    at_least(act, scored, t - 1)
                    flip.copy(act, hT[:, q * D:(q + 1) * D], t)

                def set_logits(t, q, _):
                    act.wait_ge(scored, t + 1)
                    nc.scalar.activation(logits[:, cols(t, EXPERTS)], ps[2 + q][:, 0:EXPERTS],
                                         ACT.Copy).then_inc(logit_set, 1)
                over_tiles(act, lambda u: run_lagged(u, [(2, set_logits), (1, keep), (1, copy)]), 2)
                act.wait_ge(led, 1)
                nc.scalar.activation(k.gate1[:, :], lead[:, :], ACT.Sigmoid)

            @block.tensor
            def _(pe):
                def turn(t, q, _):
                    pe.wait_ge(ln.done, t + 1)
                    flip.turn(pe, lambda c: h[:, q * D + c * P:q * D + (c + 1) * P], t)

                def score(t, q, _):
                    pe.wait_ge(flip.copied, t + 1)
                    at_least(pe, logit_set, t - 1)
                    for c in range(DC):
                        last = nc.tensor.matmul(ps[2 + q][:, 0:EXPERTS], hT[:, q * D + c * P:q * D + (c + 1) * P],
                                                wr[:, c, :], start=(c == 0), stop=(c == DC - 1))
                    last.then_inc(scored, 1)
                over_tiles(pe, lambda u: run_lagged(u, [(1, turn), (1, score)]), 1)


def layer1_ffn(k):
    with ExitStack() as ctx:
        rows = ctx.enter_context(k.nc.sbuf_tensor("rows1", [P, TILES * D], FP32))
        route_top1(k, rows)
        place(k, rows, "pl1", True)
    expert_ffn(k, "e1", k.d_w1b, k.d_w2b, ACT.Gelu, SORTED // GROUP, 1, False)
    collect(k, "co1", k.gate1, SORTED)



def diagonal_attention(k, y):
    nc, x, ps = k.nc, k.x, k.ps
    part = lambda n: part_of(SEC2, k.sec2, n).rearrange("p (c o) -> p c o", c=DC)
    row = lambda n: part_of(ROWS, k.rows, n)
    vs, os = part("vs"), part("os")
    bv = k.part("bvs2")
    with ExitStack() as ctx:
        sb, sem = stage_tools(ctx, k, "da")
        pre, post = Norm(k, sb, sem, "pre"), Norm(k, sb, sem, "post")
        h, hT, vT = sb("h", [P, 2 * D]), sb("hT", [P, 2 * D]), sb("vT", [P, 2 * D])
        z = sb("z", [P, 2 * D])
        flip = Flip(k, sem, "h", ps[0])
        v_made, v_set = sem("v_made"), sem("v_set")
        projected = sem("projected")
        biased, added, affine = sem("biased"), sem("added"), sem("affine")
        sec3_loaded = sem("sec3_loaded")

        with nc.Block() as block:

            @block.sync
            def _(sp):
                sp.dma_start(k.secA[:, :], k.d_sec3).then_inc(sec3_loaded, 16)
                sp.wait_ge(sec3_loaded, 16)

            @block.vector
            def _(dve):
                def stats(t, q, _):
                    pre.stats(dve, x[:, cols(t)], t, q)

                def apply(t, q, _):
                    at_least(dve, flip.turned, t - 1)
                    at_least(dve, biased, t - 1)
                    pre.apply(dve, h[:, q * D:(q + 1) * D], x[:, cols(t)], t, q)

                def bias(t, q, _):
                    dve.wait_ge(pre.done, t + 1)
                    nc.vector.tensor_tensor(y[:, cols(t)], h[:, q * D:(q + 1) * D], row("bos2"), ALU.add).then_inc(biased, 1)

                def add(t, q, _):
                    dve.wait_ge(projected, t + 1)
                    dve.wait_ge(biased, t + 1)
                    nc.vector.tensor_tensor(y[:, cols(t)], ps[3 + q][:, 0:D], y[:, cols(t)], ALU.add).then_inc(added, 1)
                    wait_apart(nc, dve, added, t + 1, k.spare)
                    post.stats(dve, y[:, cols(t)], t, q)

                def apply_post(t, q, _):
                    at_least(dve, affine, t * 2 - 2)
                    post.apply(dve, z[:, q * D:(q + 1) * D], y[:, cols(t)], t, q)
                over_tiles(dve, lambda u: run_lagged(u, [(0, stats), (1, apply), (1, bias), (4, apply_post), (2, add)]), 4)

            @block.gpsimd
            def _(pool):
                def scale(t, q, _):
                    part = z[:, q * D:(q + 1) * D]
                    pool.wait_ge(post.done, t + 1)
                    nc.gpsimd.tensor_tensor(part, part, row("g1"), ALU.mult).then_inc(affine, 1)
                    pool.wait_ge(affine, t * 2 + 1)
                    nc.gpsimd.tensor_tensor(y[:, cols(t)], part, row("b1"), ALU.add).then_inc(affine, 1)
                over_tiles(pool, lambda u: run_lagged(u, [(0, lambda t, q, _: pre.power(pool, t, q)), (5, scale),
                                                          (3, lambda t, q, _: post.power(pool, t, q))]), 5)

            @block.scalar
            def _(act):
                def copy(t, q, _):
                    at_least(act, v_made, t - 1)
                    flip.copy(act, hT[:, q * D:(q + 1) * D], t)

                def set_v(t, q, _):
                    act.wait_ge(v_made, t + 1)
                    at_least(act, projected, t - 1)
                    for m in range(DC):
                        nc.scalar.activation(vT[:, q * D + m * P:q * D + (m + 1) * P], ps[1 + q][:, m * P:(m + 1) * P],
                                             ACT.Identity, bias=bv[:, m:m + 1]).then_inc(v_set, 1)
                over_tiles(act, lambda u: run_lagged(u, [(1, copy), (1, set_v)]), 1)

            @block.tensor
            def _(pe):
                def project(t, q, _):
                    pe.wait_ge(v_set, t * 2 + 2)
                    at_least(pe, added, t - 1)
                    for c in range(DC):
                        last = nc.tensor.matmul(ps[3 + q][:, 0:D], vT[:, q * D + c * P:q * D + (c + 1) * P], os[:, c, :],
                                                start=(c == 0), stop=(c == DC - 1))
                    last.then_inc(projected, 1)

                def turn(t, q, _):
                    pe.wait_ge(pre.done, t + 1)
                    flip.turn(pe, lambda c: h[:, q * D + c * P:q * D + (c + 1) * P], t)

                def values(t, q, _):
                    pe.wait_ge(flip.copied, t + 1)
                    at_least(pe, v_set, t * 2 - 2)
                    for m in range(DC):
                        for c in range(DC):
                            last = nc.tensor.matmul(ps[1 + q][:, m * P:(m + 1) * P], vs[:, c, m * P:(m + 1) * P],
                                                    hT[:, q * D + c * P:q * D + (c + 1) * P],
                                                    start=(c == 0), stop=(c == DC - 1))
                    last.then_inc(v_made, 1)
                over_tiles(pe, lambda u: run_lagged(u, [(1, turn), (2, project), (1, values)]), 2)


def feed_forward(k, y):
    nc, x, ps = k.nc, k.x, k.ps
    row = lambda n: part_of(ROWS, k.rows, n)
    lin1 = part_of(SEC2, k.sec2, "lin1").rearrange("p (c f) -> p c f", c=DC)
    lin2 = part_of(SEC2, k.sec2, "lin2").rearrange("p (f d) -> p f d", f=FC)
    b1 = k.part("lin1_b")
    HALF = FC // 2
    with ExitStack() as ctx:
        sb, sem = stage_tools(ctx, k, "ff")
        pre, post = Norm(k, sb, sem, "pre"), Norm(k, sb, sem, "post")
        h, hT, hid = sb("h", [P, 2 * D]), sb("hT", [P, 2 * D]), sb("hid", [P, 2 * F])
        z = sb("z", [P, 2 * D])
        flip = Flip(k, sem, "h", ps[0])
        affine = sem("affine")
        hid_made = sem("hid_made")
        act_set, dve_set = sem("act_set"), sem("dve_set")
        projected, added = sem("projected"), sem("added")
        affine3 = sem("affine3")

        with nc.Block() as block:

            @block.vector
            def _(dve):
                def stats(t, q, _):
                    pre.stats(dve, y[:, cols(t)], t, q)

                def apply(t, q, _):
                    at_least(dve, flip.turned, t - 1)
                    at_least(dve, affine, (t - 1) * 3)
                    pre.apply(dve, h[:, q * D:(q + 1) * D], y[:, cols(t)], t, q)

                def hidden(t, q, _):
                    dve.wait_ge(hid_made, t * 2 + 2)
                    at_least(dve, projected, t - 1)
                    for j in range(HALF):
                        f = HALF + j
                        last = nc.vector.tensor_scalar(hid[:, q * F + f * P:q * F + (f + 1) * P], ps[2][:, j * P:(j + 1) * P],
                                                       b1[:, f:f + 1], 0.0, ALU.add, ALU.max)
                    last.then_inc(dve_set, 1)

                def add(t, q, _):
                    dve.wait_ge(projected, t + 1)
                    dve.wait_ge(affine, t * 3 + 3)
                    nc.vector.tensor_tensor(y[:, cols(t)], ps[3 + q][:, 0:D], y[:, cols(t)], ALU.add).then_inc(added, 1)
                    wait_apart(nc, dve, added, t + 1, k.spare)
                    post.stats(dve, y[:, cols(t)], t, q)

                def apply_post(t, q, _):
                    at_least(dve, affine3, t * 3 - 3)
                    post.apply(dve, z[:, q * D:(q + 1) * D], y[:, cols(t)], t, q)
                over_tiles(dve, lambda u: run_lagged(u, [(1, apply), (0, stats), (5, apply_post), (2, hidden), (3, add)]), 5)

            @block.gpsimd
            def _(pool):
                def scale(t, q, _):
                    part = h[:, q * D:(q + 1) * D]
                    pool.wait_ge(pre.done, t + 1)
                    nc.gpsimd.tensor_tensor(part, part, row("g2"), ALU.mult).then_inc(affine, 1)
                    pool.wait_ge(affine, t * 3 + 1)
                    nc.gpsimd.tensor_tensor(part, part, row("b2"), ALU.add).then_inc(affine, 1)
                    pool.wait_ge(affine, t * 3 + 2)
                    nc.gpsimd.tensor_tensor(y[:, cols(t)], part, row("lin2_b"), ALU.add).then_inc(affine, 1)

                def finish(t, q, _):
                    part = z[:, q * D:(q + 1) * D]
                    pool.wait_ge(post.done, t + 1)
                    nc.gpsimd.tensor_tensor(part, part, row("g3"), ALU.mult).then_inc(affine3, 1)
                    pool.wait_ge(affine3, t * 3 + 1)
                    nc.gpsimd.tensor_tensor(part, part, row("b3"), ALU.add).then_inc(affine3, 1)
                    pool.wait_ge(affine3, t * 3 + 2)
                    nc.gpsimd.tensor_tensor(x[:, cols(t)], part, x[:, cols(t)], ALU.add).then_inc(affine3, 1)
                over_tiles(pool, lambda u: run_lagged(u, [(1, scale), (0, lambda t, q, _: pre.power(pool, t, q)),
                                                          (5, finish), (4, lambda t, q, _: post.power(pool, t, q))]), 5)

            @block.scalar
            def _(act):
                def copy(t, q, _):
                    at_least(act, hid_made, t * 2 - 2)
                    flip.copy(act, hT[:, q * D:(q + 1) * D], t)

                def hidden(t, q, _):
                    act.wait_ge(hid_made, t * 2 + 1)
                    at_least(act, projected, t - 1)
                    for f in range(HALF):
                        last = nc.scalar.activation(hid[:, q * F + f * P:q * F + (f + 1) * P], ps[1][:, f * P:(f + 1) * P],
                                                    ACT.Relu, bias=b1[:, f:f + 1])
                    last.then_inc(act_set, 1)
                over_tiles(act, lambda u: run_lagged(u, [(1, copy), (2, hidden)]), 2)

            @block.tensor
            def _(pe):
                def turn(t, q, _):
                    pe.wait_ge(affine, t * 3 + 2)
                    flip.turn(pe, lambda c: h[:, q * D + c * P:q * D + (c + 1) * P], t)

                def hidden(t, q, _):
                    pe.wait_ge(flip.copied, t + 1)
                    for half, read in ((0, act_set), (1, dve_set)):
                        at_least(pe, read, t)
                        for j in range(HALF):
                            f = half * HALF + j
                            for c in range(DC):
                                last = nc.tensor.matmul(ps[1 + half][:, j * P:(j + 1) * P], lin1[:, c, f * P:(f + 1) * P],
                                                        hT[:, q * D + c * P:q * D + (c + 1) * P],
                                                        start=(c == 0), stop=(c == DC - 1))
                        last.then_inc(hid_made, 1)

                def project(t, q, _):
                    at_least(pe, added, t - 1)
                    for f in range(FC):
                        if f % HALF == 0:
                            pe.wait_ge((act_set, dve_set)[f // HALF], t + 1)
                        last = nc.tensor.matmul(ps[3 + q][:, 0:D], hid[:, q * F + f * P:q * F + (f + 1) * P], lin2[:, f, :],
                                                start=(f == 0), stop=(f == FC - 1))
                    last.then_inc(projected, 1)
                over_tiles(pe, lambda u: run_lagged(u, [(2, hidden), (1, turn), (3, project)]), 3)



def quantised_product(k, y):
    nc, x, ps = k.nc, k.x, k.ps
    row = lambda n: part_of(ROWS, k.rows, n)
    w = part_of(SEC2, k.sec2, "tern")
    MAGIC = 1.5 * 2 ** 23
    QMAX = 127.0
    with ExitStack() as ctx:
        sb, sem = stage_tools(ctx, k, "qp")
        outer, inner = Norm(k, sb, sem, "outer"), Norm(k, sb, sem, "inner")
        peak, z = sb("peak", [P, TILES]), sb("z", [P, 2 * D])
        absw, keep, sign = sb("absw", [P, DC * D]), sb("keep", [P, DC * D]), sb("sign", [P, DC * D])
        tern = sb("tern", [P, DC * D], BF16)
        sums, delta, alpha = sb("sums", [P, 2]), sb("delta", [P, 1]), sb("alpha", [P, 1])
        top, topT, scale = sb("top", [P, P]), sb("topT", [P, 1]), sb("scale", [P, 1])
        inv, out_scale = sb("inv", [P, 1]), sb("out_scale", [P, 1])
        affine, chain = sem("affine"), sem("chain")
        asked, given = sem("asked"), sem("given")
        peaked = sem("peaked")
        with nc.Block() as block:

            @block.vector
            def _(dve):
                def stats(t, q, _):
                    outer.stats(dve, x[:, cols(t)], t, q)

                def apply(t, q, _):
                    outer.apply(dve, y[:, cols(t)], x[:, cols(t)], t, q)
                    wait_apart(nc, dve, outer.done, t + 1, k.spare)
                    inner.stats(dve, y[:, cols(t)], t, q)

                def apply_inner(t, q, _):
                    at_least(dve, affine, t * 2 - 2)
                    inner.apply(dve, z[:, q * D:(q + 1) * D], y[:, cols(t)], t, q)

                def peak_of(t, q, _):
                    dve.wait_ge(affine, t * 2 + 2)
                    nc.vector.tensor_reduce(peak[:, bass.ds(t, 1)], y[:, cols(t)], AX, ALU.max,
                                            apply_absolute_value=True).then_inc(peaked, 1)
                over_tiles(dve, lambda u: run_lagged(u, [(1, apply), (0, stats), (2, apply_inner), (3, peak_of)]), 3)
                done = [0]

                def step(ins):
                    done[0] += 1
                    ins.then_inc(chain, 1)
                    dve.wait_ge(chain, done[0])
                step(nc.vector.tensor_scalar(absw[:, :], w, -1.0, None, ALU.mult))
                step(nc.vector.tensor_tensor(absw[:, :], absw[:, :], w, ALU.max))
                nc.vector.tensor_reduce(sums[:, 0:1], absw[:, :], AX, ALU.add).then_inc(asked, 1)
                dve.wait_ge(given, 1)
                step(nc.vector.tensor_scalar(delta[:, :], ps[0][:, 0:1], 1.0 / (D * D), 0.7, ALU.mult, ALU.mult))
                step(nc.vector.tensor_scalar(keep[:, :], absw[:, :], delta[:, :], None, ALU.is_gt))
                step(nc.vector.tensor_tensor(absw[:, :], absw[:, :], keep[:, :], ALU.mult))
                step(nc.vector.tensor_reduce(sums[:, 0:1], absw[:, :], AX, ALU.add))
                nc.vector.tensor_reduce(sums[:, 1:2], keep[:, :], AX, ALU.add).then_inc(asked, 1)
                step(nc.vector.tensor_scalar(sign[:, :], w, 0.0, None, ALU.is_gt))
                step(nc.vector.tensor_scalar(absw[:, :], w, 0.0, None, ALU.is_lt))
                step(nc.vector.tensor_tensor(sign[:, :], sign[:, :], absw[:, :], ALU.subtract))
                step(nc.vector.tensor_tensor(tern[:, :], sign[:, :], keep[:, :], ALU.mult))
                dve.wait_ge(given, 2)
                step(nc.vector.tensor_scalar(alpha[:, :], ps[0][:, 1:2], 1.0, None, ALU.max))
                step(nc.vector.reciprocal(alpha[:, :], alpha[:, :]))
                step(nc.vector.tensor_tensor(alpha[:, :], alpha[:, :], ps[0][:, 0:1], ALU.mult))
                dve.wait_ge(peaked, TILES)
                step(nc.vector.tensor_reduce(topT[:, :], peak[:, :], AX, ALU.max))
                nc.vector.tensor_copy(top[:, :], topT[:, :].to_broadcast([P, P])).then_inc(asked, 1)
                dve.wait_ge(given, 3)
                step(nc.vector.tensor_reduce(scale[:, :], ps[1][:, 0:P], AX, ALU.max))
                step(nc.vector.tensor_scalar(scale[:, :], scale[:, :], 1e-8, 1.0 / QMAX, ALU.max, ALU.mult))
                step(nc.vector.reciprocal(inv[:, :], scale[:, :]))
                step(nc.vector.tensor_tensor(out_scale[:, :], scale[:, :], alpha[:, :], ALU.mult))

            @block.gpsimd
            def _(pool):
                def affine_of(t, q, _):
                    part = z[:, q * D:(q + 1) * D]
                    pool.wait_ge(inner.done, t + 1)
                    nc.gpsimd.tensor_tensor(part, part, row("gamma"), ALU.mult).then_inc(affine, 1)
                    pool.wait_ge(affine, t * 2 + 1)
                    nc.gpsimd.tensor_tensor(y[:, cols(t)], part, row("beta"), ALU.add).then_inc(affine, 1)
                over_tiles(pool, lambda u: run_lagged(u, [(0, lambda t, q, _: outer.power(pool, t, q)),
                                                          (1, lambda t, q, _: inner.power(pool, t, q)), (2, affine_of)]), 2)

            @block.tensor
            def _(pe):
                pe.wait_ge(asked, 1)
                nc.tensor.matmul(ps[0][:, 0:1], k.ones[:, :], sums[:, 0:1], start=True, stop=True).then_inc(given, 1)
                pe.wait_ge(asked, 2)
                nc.tensor.matmul(ps[0][:, 0:2], k.ones[:, :], sums[:, :], start=True, stop=True).then_inc(given, 1)
                pe.wait_ge(asked, 3)
                nc.tensor.transpose(ps[1][:, 0:P], top[:, :], k.ident).then_inc(given, 1)

        n, whole = sb("n", [P, 2 * D]), sb("whole", [P, 2 * D], BF16)
        wholeT = sb("wholeT", [P, 2 * D], BF16)
        rounded = sem("rounded")
        turned, copied, made, added = sem("turned"), sem("copied"), sem("made"), sem("added")
        turned_bank = ps[0][:, 0:P].bitcast(BF16)
        with nc.Block() as block:

            @block.vector
            def _(dve):
                def quantise(t, q, _):
                    part = n[:, q * D:(q + 1) * D]
                    at_least(dve, rounded, t * 3 - 3)
                    nc.vector.tensor_scalar(part, y[:, cols(t)], inv[:, :], MAGIC, ALU.mult, ALU.add).then_inc(rounded, 1)
                    dve.wait_ge(rounded, t * 3 + 1)
                    nc.vector.tensor_scalar(part, part, MAGIC + QMAX, MAGIC - QMAX, ALU.min, ALU.max).then_inc(rounded, 1)
                    dve.wait_ge(rounded, t * 3 + 2)
                    at_least(dve, turned, t - 1)
                    nc.vector.tensor_scalar(whole[:, q * D:(q + 1) * D], part, -MAGIC, None, ALU.add).then_inc(rounded, 1)

                def add(t, q, _):
                    dve.wait_ge(made, t + 1)
                    nc.vector.scalar_tensor_tensor(x[:, cols(t)], ps[1 + q][:, 0:D], out_scale[:, :], x[:, cols(t)],
                                                   ALU.mult, ALU.add).then_inc(added, 1)
                over_tiles(dve, lambda u: run_lagged(u, [(0, quantise), (1, add)]), 1)

            @block.scalar
            def _(act):
                def copy(t, q, _):
                    act.wait_ge(turned, t + 1)
                    at_least(act, made, t - 1)
                    nc.scalar.activation(wholeT[:, q * D:(q + 1) * D], turned_bank, ACT.Copy).then_inc(copied, 1)
                over_tiles(act, lambda u: run_lagged(u, [(0, copy)]), 0)

            @block.tensor
            def _(pe):
                def turn(t, q, _):
                    pe.wait_ge(rounded, t * 3 + 3)
                    at_least(pe, copied, t)
                    for c in range(DC):
                        last = nc.tensor.transpose(turned_bank[:, c * P:(c + 1) * P],
                                                   whole[:, q * D + c * P:q * D + (c + 1) * P], k.ident16[:, :])
                    last.then_inc(turned, 1)

                def product(t, q, _):
                    pe.wait_ge(copied, t + 1)
                    at_least(pe, added, t - 1)
                    for c in range(DC):
                        last = nc.tensor.matmul(ps[1 + q][:, 0:D], wholeT[:, q * D + c * P:q * D + (c + 1) * P],
                                                tern[:, c * D:(c + 1) * D], start=(c == 0), stop=(c == DC - 1))
                    last.then_inc(made, 1)
                over_tiles(pe, lambda u: run_lagged(u, [(0, turn), (0, product)]), 0)


def layer2(k):
    with ExitStack() as ctx:
        y = ctx.enter_context(k.nc.sbuf_tensor("y2", [P, TILES * D], FP32))
        diagonal_attention(k, y)
        head_attention(k, "h2", 8, SEC2, k.sec2, "bq2", "bk2", "bv2", "bo2", y, False)
        feed_forward(k, y)
        quantised_product(k, y)



def gated_experts(k):
    nc, x, ps, ident = k.nc, k.x, k.ps, k.ident
    part3 = lambda n, c: part_of(SEC3, k.secA, n).rearrange("p (c o) -> p c o", c=c)
    part65 = lambda n: part_of(SEC65, k.sec65, n)
    row = lambda n: part_of(ROWS, k.rows, n)
    enc, s2c, we2, dec = part3("enc", DC), part3("s2c", 4), part3("we2", 16), part3("dec", 4)
    rw1, rw2, we1, c2s = part65("rw1"), part65("rw2"), part65("we1"), part65("c2s")
    enc_b, s2c_b = k.part("enc_b"), k.part("s2c_b")
    M, H, HC = 64, 512, 4
    E = EXPERTS
    EC = E * 2
    with ExitStack() as ctx:
        sb, sem = stage_tools(ctx, k, "ge")
        pre, post = Norm(k, sb, sem, "pre"), Norm(k, sb, sem, "post")
        h, hT = sb("h", [P, 2 * D]), sb("hT", [P, 2 * D])
        encT, contT, routeT = sb("encT", [P, 2 * H]), sb("contT", [M + 1, 2 * P]), sb("routeT", [M + 1, 2 * P])
        logits, best, lead, z = sb("logits", [P, E]), sb("best", [P, 8]), sb("lead", [P, E]), sb("z", [P, 2 * E])
        higher, same, rank = sb("higher", [P, E * E]), sb("same", [P, E * E]), sb("rank", [P, 2 * E])
        gate = sb("gate", [P, 2 * E])
        hid = sb("hid", [P, EC * P])
        outs, moe = sb("outs", [P, E * M]), sb("moe", [P, 2 * P])
        moeT, spikeT = sb("moeT", [M + 1, 2 * P]), sb("spikeT", [P, 2 * H])
        decoded, res = sb("decoded", [P, 2 * D]), sb("res", [P, 2 * D])
        flip = Flip(k, sem, "h", ps[0])
        ready = sem("ready")
        enc_made, enc_set = sem("enc_made"), sem("enc_set")
        cont_made, cont_set = sem("cont_made"), sem("cont_set")
        route_made, route_set = sem("route_made"), sem("route_set")
        logit_made = sem("logit_made")
        gating = sem("gating")
        z_sig = sem("z_sig")
        hid_made, hid_set = sem("hid_made"), sem("hid_set")
        outs_made = sem("outs_made")
        combined = sem("combined")
        moe_turned, moe_copied = sem("moe_turned"), sem("moe_copied")
        spike_made, spike_set = sem("spike_made"), sem("spike_set")
        dec_made, dec_biased, dec_set = sem("dec_made"), sem("dec_biased"), sem("dec_set")
        finished = sem("finished")
        GATING = 11

        with nc.Block() as block:

            @block.tensor
            def _(pe):
                pe.wait_ge(ready, 4)

                def turn(t, q, _):
                    pe.wait_ge(pre.done, t + 1)
                    flip.turn(pe, lambda c: h[:, q * D + c * P:q * D + (c + 1) * P], t)

                def encode(t, q, _):
                    pe.wait_ge(flip.copied, t + 1)
                    at_least(pe, enc_set, t * HC)
                    for m in range(HC):
                        for c in range(DC):
                            last = nc.tensor.matmul(ps[1][:, m * P:(m + 1) * P], enc[:, c, m * P:(m + 1) * P],
                                                    hT[:, q * D + c * P:q * D + (c + 1) * P],
                                                    start=(c == 0), stop=(c == DC - 1))
                    last.then_inc(enc_made, 1)

                def condense(t, q, _):
                    pe.wait_ge(enc_set, t * HC + HC)
                    at_least(pe, gating, (t - 1) * GATING + 1)
                    for m in range(HC):
                        last = nc.tensor.matmul(ps[2][0:M, 0:P], s2c[:, m, :], encT[:, q * H + m * P:q * H + (m + 1) * P],
                                                start=(m == 0), stop=(m == HC - 1))
                    last.then_inc(cont_made, 1)

                def route(t, q, _):
                    pe.wait_ge(cont_set, t + 1)
                    nc.tensor.matmul(ps[2][0:M, P:2 * P], rw1, contT[:, q * P:(q + 1) * P], start=True,
                                     stop=True).then_inc(route_made, 1)

                def score(t, q, _):
                    pe.wait_ge(route_set, t + 1)
                    nc.tensor.matmul(ps[2][:, 2 * P:2 * P + E], routeT[:, q * P:(q + 1) * P], rw2, start=True,
                                     stop=True).then_inc(logit_made, 1)

                def hidden(t, q, j):
                    at_least(pe, hid_set, t * 4 + j - 1)
                    for i in range(4):
                        f = 4 * j + i
                        last = nc.tensor.matmul(ps[3 + j % 2][:, i * P:(i + 1) * P], we1[:, f * P:(f + 1) * P],
                                                contT[:, q * P:(q + 1) * P], start=True, stop=True)
                    last.then_inc(hid_made, 1)

                def out(t, q, j):
                    pe.wait_ge(hid_set, t * 4 + j + 1)
                    if j == 0:
                        at_least(pe, combined, (t - 1) * 3 + 1)
                    for e in (2 * j, 2 * j + 1):
                        for i in range(2):
                            f = 2 * e + i
                            last = nc.tensor.matmul(ps[5][:, e * M:(e + 1) * M], hid[:, f * P:(f + 1) * P], we2[:, f, :],
                                                    start=(i == 0), stop=(i == 1))
                    return last

                def experts(t, q, _):
                    hidden(t, q, 0)
                    hidden(t, q, 1)
                    for j in range(4):
                        last = out(t, q, j)
                        if j < 2:
                            hidden(t, q, j + 2)
                    last.then_inc(outs_made, 1)

                def turn_moe(t, q, _):
                    pe.wait_ge(combined, t * 3 + 3)
                    at_least(pe, dec_biased, t)
                    nc.tensor.transpose(ps[7][:, 0:P], moe[:, q * P:(q + 1) * P], ident).then_inc(moe_turned, 1)

                def spike(t, q, _):
                    pe.wait_ge(moe_copied, t + 1)
                    at_least(pe, spike_set, t)
                    for m in range(HC):
                        last = nc.tensor.matmul(ps[6][:, m * P:(m + 1) * P], c2s[:, m * P:(m + 1) * P],
                                                moeT[:, q * P:(q + 1) * P], start=True, stop=True)
                    last.then_inc(spike_made, 1)

                def decode(t, q, _):
                    pe.wait_ge(spike_set, t + 1)
                    for m in range(HC):
                        last = nc.tensor.matmul(ps[7][:, D:2 * D], spikeT[:, q * H + m * P:q * H + (m + 1) * P], dec[:, m, :],
                                                start=(m == 0), stop=(m == HC - 1))
                    last.then_inc(dec_made, 1)
                over_tiles(pe, lambda u: run_lagged(u, [(3, experts), (4, turn_moe), (1, turn), (2, condense), (4, spike),
                                                        (1, encode), (2, route), (4, decode), (2, score)]), 4)

            @block.scalar
            def _(act):
                def copy(t, q, _):
                    at_least(act, enc_made, t - 1)
                    flip.copy(act, hT[:, q * D:(q + 1) * D], t)

                def set_enc(t, q, _):
                    act.wait_ge(enc_made, t + 1)
                    at_least(act, cont_made, t - 1)
                    for m in range(HC):
                        nc.scalar.activation(encT[:, q * H + m * P:q * H + (m + 1) * P], ps[1][:, m * P:(m + 1) * P],
                                             ACT.Sigmoid, bias=enc_b[:, m:m + 1]).then_inc(enc_set, 1)

                def set_cont(t, q, _):
                    act.wait_ge(cont_made, t + 1)
                    at_least(act, outs_made, t - 1)
                    nc.scalar.activation(contT[0:M, q * P:(q + 1) * P], ps[2][0:M, 0:P], ACT.Identity,
                                         bias=s2c_b[0:M, :]).then_inc(cont_set, 1)

                def set_route(t, q, _):
                    act.wait_ge(route_made, t + 1)
                    at_least(act, logit_made, t - 1)
                    nc.scalar.activation(routeT[0:M, q * P:(q + 1) * P], ps[2][0:M, P:2 * P], ACT.Tanh).then_inc(route_set, 1)

                def gate_sig(t, q, _):
                    act.wait_ge(gating, t * GATING + 5)
                    nc.scalar.activation(z[:, q * E:(q + 1) * E], z[:, q * E:(q + 1) * E], ACT.Sigmoid).then_inc(z_sig, 1)

                def hidden(t, q, _):
                    at_least(act, outs_made, t)
                    for j in range(4):
                        act.wait_ge(hid_made, t * 4 + j + 1)
                        nc.scalar.activation(hid[:, 4 * j * P:4 * (j + 1) * P], ps[3 + j % 2][:, :], ACT.Relu).then_inc(hid_set, 1)

                def copy_moe(t, q, _):
                    act.wait_ge(moe_turned, t + 1)
                    at_least(act, spike_made, t - 1)
                    nc.scalar.activation(moeT[0:M, q * P:(q + 1) * P], ps[7][0:M, 0:P], ACT.Copy).then_inc(moe_copied, 1)

                def set_spike(t, q, _):
                    act.wait_ge(spike_made, t + 1)
                    at_least(act, dec_made, t - 1)
                    nc.scalar.activation(spikeT[:, q * H:(q + 1) * H], ps[6][:, :], ACT.Sigmoid).then_inc(spike_set, 1)

                def set_dec(t, q, _):
                    act.wait_ge(dec_biased, t + 1)
                    nc.scalar.activation(decoded[:, q * D:(q + 1) * D], decoded[:, q * D:(q + 1) * D],
                                         ACT.Sigmoid).then_inc(dec_set, 1)
                over_tiles(act, lambda u: run_lagged(u, [(5, set_dec), (3, hidden), (3, gate_sig), (4, copy_moe), (1, copy),
                                                         (2, set_cont), (4, set_spike), (2, set_route), (1, set_enc)]), 5)

            @block.vector
            def _(dve):
                nc.vector.memset(contT[M:M + 1, :], 1.0).then_inc(ready, 1)
                nc.vector.memset(routeT[M:M + 1, :], 1.0).then_inc(ready, 1)
                nc.vector.memset(moeT[M:M + 1, :], 1.0).then_inc(ready, 1)
                nc.vector.memset(moe[:, :], 0.0).then_inc(ready, 1)
                dve.wait_ge(ready, 4)

                def stats(t, q, _):
                    pre.stats(dve, x[:, cols(t)], t, q)

                def apply(t, q, _):
                    at_least(dve, flip.turned, t - 1)
                    pre.apply(dve, h[:, q * D:(q + 1) * D], x[:, cols(t)], t, q)

                def gates(t, q, _):
                    def step(ins, n):
                        ins.then_inc(gating, 1)
                        dve.wait_ge(gating, t * GATING + n)
                    zt = z[:, q * E:(q + 1) * E]
                    square = lambda a: a[:, :].rearrange("p (e f) -> p e f", f=E)
                    mine = logits[:, :].unsqueeze(2).to_broadcast([P, E, E])
                    other = logits[:, :].unsqueeze(1).to_broadcast([P, E, E])
                    at_least(dve, gating, t * GATING)
                    dve.wait_ge(logit_made, t + 1)
                    step(nc.vector.tensor_copy(logits[:, :], ps[2][:, 2 * P:2 * P + E]), 1)
                    step(nc.vector.memset(best[:, :], 0.0), 2)
                    wait_apart(nc, dve, gating, t * GATING + 2, k.spare)
                    step(nc.vector.max(best[:, :], logits[:, :]), 3)
                    step(nc.vector.tensor_scalar(lead[:, :], logits[:, :], best[:, 0:1], None, ALU.subtract), 4)
                    at_least(dve, gating, (t - 1) * GATING)
                    step(nc.vector.scalar_tensor_tensor(zt, logits[:, :], best[:, 1:2], lead[:, :], ALU.subtract,
                                                        ALU.add), 5)
                    step(nc.vector.tensor_tensor(square(higher), other, mine, ALU.is_gt), 6)
                    step(nc.vector.tensor_tensor(square(same), other, mine, ALU.is_equal), 7)
                    step(nc.vector.tensor_tensor(same[:, :], same[:, :], k.part("lower"), ALU.mult), 8)
                    step(nc.vector.tensor_tensor(higher[:, :], higher[:, :], same[:, :], ALU.add), 9)
                    step(nc.vector.tensor_reduce(rank[:, q * E:(q + 1) * E], square(higher), AX, ALU.add), 10)
                    dve.wait_ge(z_sig, t + 1)
                    step(nc.vector.scalar_tensor_tensor(gate[:, q * E:(q + 1) * E], rank[:, q * E:(q + 1) * E], 1.5, zt,
                                                        ALU.is_lt, ALU.mult), 11)

                def combine(t, q, _):
                    dve.wait_ge(outs_made, t + 1)
                    nc.vector.tensor_tensor(outs[:, :], ps[5][:, :], row("be2"), ALU.add).then_inc(combined, 1)
                    dve.wait_ge(combined, t * 3 + 1)
                    dve.wait_ge(gating, t * GATING + GATING)
                    o3 = outs[:, :].rearrange("p (e m) -> p e m", m=M)
                    nc.vector.tensor_tensor(o3, o3, gate[:, q * E:(q + 1) * E].unsqueeze(2).to_broadcast([P, E, M]),
                                            ALU.mult).then_inc(combined, 1)
                    dve.wait_ge(combined, t * 3 + 2)
                    at_least(dve, moe_turned, t - 1)
                    nc.vector.tensor_reduce(moe[:, q * P:q * P + M], outs[:, :].rearrange("p (e m) -> p m e", m=M),
                                            AX, ALU.add).then_inc(combined, 1)

                def bias_dec(t, q, _):
                    dve.wait_ge(dec_made, t + 1)
                    at_least(dve, post.done, t - 1)
                    nc.vector.tensor_tensor(decoded[:, q * D:(q + 1) * D], ps[7][:, D:2 * D], row("dec_b"),
                                            ALU.add).then_inc(dec_biased, 1)

                def post_stats(t, q, _):
                    dve.wait_ge(dec_set, t + 1)
                    post.stats(dve, decoded[:, q * D:(q + 1) * D], t, q)

                def post_apply(t, q, _):
                    at_least(dve, finished, t * 3 - 3)
                    post.apply(dve, res[:, q * D:(q + 1) * D], decoded[:, q * D:(q + 1) * D], t, q)
                over_tiles(dve, lambda u: run_lagged(u, [(1, apply), (6, post_apply), (0, stats), (3, gates),
                                                         (5, post_stats), (3, combine), (4, bias_dec)]), 6)

            @block.gpsimd
            def _(pool):
                def finish(t, q, _):
                    part = res[:, q * D:(q + 1) * D]
                    pool.wait_ge(post.done, t + 1)
                    nc.gpsimd.tensor_tensor(part, part, row("ln_g3"), ALU.mult).then_inc(finished, 1)
                    pool.wait_ge(finished, t * 3 + 1)
                    nc.gpsimd.tensor_tensor(part, part, row("ln_b3"), ALU.add).then_inc(finished, 1)
                    pool.wait_ge(finished, t * 3 + 2)
                    nc.gpsimd.tensor_tensor(x[:, cols(t)], part, x[:, cols(t)], ALU.add).then_inc(finished, 1)
                over_tiles(pool, lambda u: run_lagged(u, [(0, lambda t, q, _: pre.power(pool, t, q)),
                                                          (5, lambda t, q, _: post.power(pool, t, q)), (6, finish)]), 6)


def layer3(k):
    head_attention(k, "h3", 16, SEC3, k.secA, "bq3", "bk3", "bv3", "bo3", k.x, True)
    gated_experts(k)


def store(k):
    with ExitStack() as ctx:
        sb, sem = stage_tools(ctx, k, "st")
        stored = sem("stored")
        with k.nc.Block() as block:
            @block.sync
            def _(sp):
                for c in range(4):
                    n = T // 4
                    sp.dma_start(k.d_out[c * n:(c + 1) * n, :].rearrange("(t p) d -> p t d", p=P),
                                 k.x[:, c * 8 * D:(c + 1) * 8 * D].rearrange("p (t d) -> p t d", d=D)).then_inc(stored, 16)
                sp.wait_ge(stored, 64)


def stages(k):
    context_attention(k)
    layer0_ffn(k)
    head_attention(k,
    'h1',
    16,
    SEC1,
    k.secA,
    'bq1',
    'bk1',
    'bv1',
    'bo1',
    k.x,
    True,
    causal=True)
    layer1_ffn(k)
    layer2(k)
    layer3(k)
    store(k)



def build(nc, args, out):
    k = Kit()
    k.nc = nc
    (k.d_x, k.d_mask, k.d_sec0, k.d_sec1, k.d_sec2, k.d_sec3, k.d_sec65, k.d_rows,
     k.d_w1a, k.d_w2a, k.d_b2a, k.d_w1b, k.d_w2b) = args
    k.d_out = out
    k.d_rows_in = nc.dram_tensor("rows_by_expert", [SORTED, D], FP32).ap()
    k.d_rows_out = nc.dram_tensor("expert_results", [SORTED, D], FP32).ap()
    with ExitStack() as ctx:
        sb = lambda n, s, d=FP32: ctx.enter_context(nc.sbuf_tensor(n, s, d))
        k.x = sb("x", [P, TILES * D])
        k.sec0 = sb("sec0", [P, offsets(SEC0)[1]])
        k.secA = sb("secA", [P, offsets(SEC3)[1]])
        k.sec2 = sb("sec2", [P, offsets(SEC2)[1]])
        k.sec65 = sb("sec65", [65, offsets(SEC65)[1]])
        k.rows = sb("rows", [P, offsets(ROWS)[1]])
        k.neghalf, k.eps, k.spare = [sb(n, [P, 1])[:, 0:1] for n in ("neghalf", "eps", "spare")]
        k.ones = sb("ones", [P, P])
        k.ident16 = sb("ident16", [P, P], BF16)
        k.causal = sb("causal16", [P, 2 * KEYS], BF16)[:, :].rearrange("p (a j) -> p a j", a=2)
        k.pos = sb("pos", [P, TILES], I32)
        k.tile_expert = sb("tile_expert", [P, 24], I32)
        k.onehot = sb("onehot", [P, EXPERTS * TILES])
        k.gate1 = sb("gate1", [P, TILES])
        k.packs = [(SEC0, k.sec0)]
        k.ident = k.part("ident")
        k.ps = [ctx.enter_context(nc.psum_tensor(f"bank{i}", [P, 512], FP32)) for i in range(8)]
        k.loaded0 = ctx.enter_context(nc.semaphore("sec0_loaded"))
        k.set_up = ctx.enter_context(nc.semaphore("constants_set"))
        stages(k)



def kernel(**inputs):
    import concourse.bacc as _bacc
    from concourse.bass_utils import run_bass_kernel_spmd as _run
    i = {n: np.asarray(a) for n, a in inputs.items()}

    def kmajor(w):
        return w.reshape(-1, P, w.shape[-1]).transpose(1, 0, 2).reshape(P, -1)

    def col(v):
        return v.reshape(-1, P).T

    def pack(table, parts, rows=P):
        parts = [np.asarray(parts[n]).reshape(rows, -1) for n, _ in table]
        assert [a.shape[1] for a in parts] == [w for _, w in table]
        return np.ascontiguousarray(np.concatenate(parts, axis=1))

    f32 = np.float32
    p = np.arange(P)
    ctx = i["ctx_1024"]
    ctxT = ctx.transpose(2, 0, 1).reshape(DC, P, B, KEYS).transpose(1, 0, 2, 3)
    qkv_w, qkv_b = i["L2_xattn_qkv_w"], i["L2_xattn_qkv_b"]
    inw, inb = i["L2_xattn_in_proj_w"], i["L2_xattn_in_proj_b"]
    sec0 = dict(
        ident=np.eye(P, dtype=f32), tri=(p[:, None] < p[None, :]).astype(f32),
        hmask16=(p[:, None] // 16 == np.arange(8)[None]).astype(f32),
        hmask8=(p[:, None] // 32 == np.arange(4)[None]).astype(f32),
        vmask=(p[:, None] // KEYS == np.arange(2)[None]).astype(f32),
        ctxT=np.concatenate([ctxT, ctxT], axis=3),
        ctx=np.concatenate([ctx, ctx], axis=1).transpose(1, 0, 2),
        centroids=kmajor(i["L0_ffn_centroids"].T), wr=kmajor(i["L1_ffn_Wr"]),
        bq1=col(i["L1_xattn_bq"]), bk1=col(i["L1_xattn_bk"]), bvs2=col(qkv_b[2 * D:]),
        bq2=col(inb[:D]), bk2=col(inb[D:2 * D]), lin1_b=col(i["L2_xattn_lin1_b"]),
        bq3=col(i["L3_xattn_bq"]), bk3=col(i["L3_xattn_bk"]), enc_b=col(i["L3_ffn_enc_b"]),
        s2c_b=np.concatenate([i["L3_ffn_s2c_b"]] * 2), eb1=col(i["L0_ffn_b1"].reshape(-1)), nibble=np.broadcast_to(np.arange(1, 16, dtype=f32), (P, 15)),
        base0=np.broadcast_to(np.arange(EXPERTS, dtype=f32) * (T // EXPERTS), (P, EXPERTS)),
        tstart=np.broadcast_to(np.arange(24, dtype=f32) * GROUP, (P, 24)),
        lower=np.broadcast_to((np.arange(8)[None, :] < np.arange(8)[:, None]).astype(f32).reshape(1, 64), (P, 64)),
        causal=np.where((p[:, None, None] < np.arange(KEYS)) & (np.arange(2)[:, None] == 0), f32(-1e30), f32(0)))
    sec1 = dict(wq=kmajor(i["L1_xattn_Wq"].T), wk=kmajor(i["L1_xattn_Wk"].T), wv=kmajor(i["L1_xattn_Wv"].T),
                wo=kmajor(i["L1_xattn_Wo"].T))
    sec2 = dict(vs=kmajor(qkv_w[2 * D:].T), os=kmajor(i["L2_xattn_sa_out_w"].T), wq=kmajor(inw[:D].T),
                wk=kmajor(inw[D:2 * D].T), wv=kmajor(inw[2 * D:].T), wo=kmajor(i["L2_xattn_mha_out_w"].T),
                lin1=kmajor(i["L2_xattn_lin1_w"].T), lin2=kmajor(i["L2_xattn_lin2_w"].T),
                tern=kmajor(i["L2_ffn_weight"].T))
    sec3 = dict(wq=kmajor(i["L3_xattn_Wq"]), wk=kmajor(i["L3_xattn_Wk"]), wv=kmajor(i["L3_xattn_Wv"]),
                wo=kmajor(i["L3_xattn_Wo"]), enc=kmajor(i["L3_ffn_enc_W"]), s2c=kmajor(i["L3_ffn_s2c_W"]),
                we2=kmajor(i["L3_ffn_We2"].reshape(-1, 64)), dec=kmajor(i["L3_ffn_dec_W"]))
    we1 = i["L3_ffn_We1"].transpose(1, 0, 2).reshape(64, -1)
    sec65 = dict(rw1=np.concatenate([i["L3_ffn_rW1"], i["L3_ffn_rb1"][None]]),
                 rw2=np.concatenate([i["L3_ffn_rW2"], i["L3_ffn_rb2"][None]]),
                 we1=np.concatenate([we1, i["L3_ffn_be1"].reshape(1, -1)]),
                 c2s=np.concatenate([i["L3_ffn_c2s_W"], i["L3_ffn_c2s_b"][None]]))
    rows = dict(ln_g0=i["L0_ffn_ln_g"], ln_b0=i["L0_ffn_ln_b"], bv1=i["L1_xattn_bv"], bo1=i["L1_xattn_bo"],
                bos2=i["L2_xattn_sa_out_b"], g1=i["L2_xattn_ln1_g"], b1=i["L2_xattn_ln1_b"], bv2=inb[2 * D:],
                bo2=i["L2_xattn_mha_out_b"], g2=i["L2_xattn_ln2_g"], b2=i["L2_xattn_ln2_b"],
                lin2_b=i["L2_xattn_lin2_b"], g3=i["L2_xattn_ln3_g"], b3=i["L2_xattn_ln3_b"],
                gamma=i["L2_ffn_gamma"], beta=i["L2_ffn_beta"], bv3=i["L3_xattn_bv"], bo3=i["L3_xattn_bo"],
                dec_b=i["L3_ffn_dec_b"], ln_g3=i["L3_ffn_ln_g"], ln_b3=i["L3_ffn_ln_b"], be2=i["L3_ffn_be2"])

    def experts(w):
        return np.ascontiguousarray(w.reshape(EXPERTS, -1, P, w.shape[-1]).transpose(0, 2, 1, 3).reshape(EXPERTS, P, -1))

    arrays = dict(
        x=i["x"].reshape(T, D), mask=i["mask_BxSxS2_fk0"].reshape(T, KEYS), sec0=pack(SEC0, sec0),
        sec1=pack(SEC1, sec1), sec2=pack(SEC2, sec2), sec3=pack(SEC3, sec3), sec65=pack(SEC65, sec65, 65),
        rows=pack(ROWS, rows, 1).reshape(-1), w1a=experts(i["L0_ffn_w1"]), w2a=experts(i["L0_ffn_w2"]),
        b2a=i["L0_ffn_b2"], w1b=experts(i["L1_ffn_W1"]), w2b=experts(i["L1_ffn_W2"]))
    nc = _bacc.Bacc("TRN2", target_bir_lowering=False, num_devices=1)
    args = [nc.dram_tensor("in_" + n, a.shape, FP32, kind="ExternalInput").ap() for n, a in arrays.items()]
    out = nc.dram_tensor("out", (T, D), FP32, kind="ExternalOutput").ap()
    build(nc, args, out)
    r = _run(nc, [{"in_" + n: np.ascontiguousarray(a) for n, a in arrays.items()}], core_ids=[0])
    return r.results[0]["out"].reshape(B, S, D)
```

```python
import numpy as np
import concourse.bass as bass
from concourse import mybir
from contextlib import ExitStack

FP32 = mybir.dt.float32
BF16 = mybir.dt.bfloat16
I32 = mybir.dt.int32
U32 = mybir.dt.uint32
ALU = mybir.AluOpType
ACT = mybir.ActivationFunctionType
AX = mybir.AxisListType.X

P = 128
B, S, D, KEYS = 4, 1024, 256, 64
T = B * S
TILES = T // P
TPB = S // P
DC = D // P
EXPERTS, F = 8, 1024
FC = F // P
LN_EPS = 1e-5



def lagged(u, par, lag, tiles=TILES):
    t = u * 2 + (par - lag)
    q = (par - lag) % 2
    if isinstance(t, int) and not 0 <= t < tiles:
        return None
    return t, q, u + (par - lag - q) // 2


def over_tiles(eng, body, lag, tiles=TILES):
    head = (lag + 4) // 2
    for u in range(head):
        body(u)
    with eng.Fori(head, tiles // 2) as u:
        body(u)
    for u in range(tiles // 2, (tiles + lag + 1) // 2):
        body(u)


def wait_apart(nc, dve, sem, value, spare):
    at_least(dve, sem, value)
    if not isinstance(value, int):
        nc.vector.memset(spare, 0.0)


def at_least(eng, sem, value):
    if not (isinstance(value, int) and value <= 0):
        eng.wait_ge(sem, value)


def cols(t, w=D):
    return bass.ds(t * w, w)


def offsets(table):
    at, out = 0, {}
    for name, width in table:
        out[name] = (at, width)
        at += width
    return out, at


SEC0 = [("ident", P), ("tri", P), ("hmask16", 8), ("hmask8", 4), ("vmask", 2), ("ctxT", DC * B * P),
        ("ctx", B * D), ("centroids", DC * EXPERTS), ("wr", DC * EXPERTS),
        ("bq1", DC), ("bk1", DC), ("bvs2", DC), ("bq2", DC), ("bk2", DC), ("lin1_b", FC), ("bq3", DC), ("bk3", DC),
        ("enc_b", 4), ("s2c_b", 1), ("eb1", EXPERTS * FC), ("base0", EXPERTS), ("tstart", 24), ("nibble", 15), ("lower", 64),
        ("causal", 2 * KEYS)]
PROJ = [("wq", DC * D), ("wk", DC * D), ("wv", DC * D), ("wo", DC * D)]
SEC1 = PROJ
SEC2 = [("vs", DC * D), ("os", DC * D)] + PROJ + [("lin1", DC * F), ("lin2", FC * D), ("tern", DC * D)]
SEC3 = PROJ + [("enc", DC * 512), ("s2c", 4 * 64), ("we2", 16 * 64), ("dec", 4 * D)]
SEC65 = [("rw1", 64), ("rw2", EXPERTS), ("we1", EXPERTS * 256), ("c2s", 512)]
ROWS = [(n, D) for n in ("ln_g0", "ln_b0", "bv1", "bo1", "bos2", "g1", "b1", "bv2", "bo2", "g2", "b2", "lin2_b",
                         "g3", "b3", "gamma", "beta", "bv3", "bo3", "dec_b", "ln_g3", "ln_b3")] \
    + [("be2", EXPERTS * 64)]


class Kit:

    def part(self, name):
        for table, buf in self.packs:
            at, _ = offsets(table)
            if name in at:
                return buf[:, at[name][0]:at[name][0] + at[name][1]]
        raise KeyError(name)


class Norm:

    def __init__(self, k, sb, sem, name):
        self.nc, self.neghalf, self.eps, self.spare = k.nc, k.neghalf, k.eps, k.spare
        self.st, self.mv, self.rstd = sb(name + "_st", [P, 12]), sb(name + "_mv", [P, 4]), sb(name + "_rstd", [P, 2])
        self.stats_done = sem(name + "_stats_done")
        self.rstd_done = sem(name + "_rstd_done")
        self.done = sem(name + "_done")

    def stats(self, dve, src, t, q):
        self.nc.vector.bn_stats(self.st[:, 6 * q:6 * q + 6], src).then_inc(self.stats_done, 1)
        wait_apart(self.nc, dve, self.stats_done, t * 2 + 1, self.spare)
        self.nc.vector.bn_aggr(self.mv[:, 2 * q:2 * q + 2], self.st[:, 6 * q:6 * q + 6]).then_inc(self.stats_done, 1)

    def power(self, pool, t, q):
        pool.wait_ge(self.stats_done, t * 2 + 2)
        at_least(pool, self.done, t - 1)
        self.nc.gpsimd.tensor_tensor(self.rstd[:, q:q + 1], self.mv[:, 2 * q + 1:2 * q + 2], self.eps,
                                     ALU.add).then_inc(self.rstd_done, 1)
        pool.wait_ge(self.rstd_done, t * 2 + 1)
        self.nc.gpsimd.tensor_tensor(self.rstd[:, q:q + 1], self.rstd[:, q:q + 1], self.neghalf,
                                     ALU.pow).then_inc(self.rstd_done, 1)

    def apply(self, dve, out, src, t, q):
        dve.wait_ge(self.rstd_done, t * 2 + 2)
        self.nc.vector.tensor_scalar(out, src, self.mv[:, 2 * q:2 * q + 1], self.rstd[:, q:q + 1],
                                     ALU.subtract, ALU.mult).then_inc(self.done, 1)


class Flip:

    def __init__(self, k, sem, name, bank):
        self.nc, self.ident, self.bank = k.nc, k.ident, bank
        self.turned, self.copied = sem(name + "_turned"), sem(name + "_copied")

    def turn(self, pe, src, t, pieces=DC):
        at_least(pe, self.copied, t)
        for c in range(pieces):
            last = self.nc.tensor.transpose(self.bank[:, c * P:(c + 1) * P], src(c), self.ident)
        last.then_inc(self.turned, 1)

    def copy(self, act, dst, t, pieces=DC):
        act.wait_ge(self.turned, t + 1)
        self.nc.scalar.activation(dst, self.bank[:, 0:pieces * P], ACT.Copy).then_inc(self.copied, 1)


def stage_tools(ctx, k, name):
    used = []

    def sb(n, shape, dtype=FP32):
        return ctx.enter_context(k.nc.sbuf_tensor(f"{name}_{n}", shape, dtype))

    def sem(n):
        used.append(k.nc.alloc_semaphore(f"{name}_{n}"))
        return used[-1]

    def clear():
        k.nc.clear_and_free_semaphores(used)
        k.nc.all_engine_barrier(sem_only=True)
    ctx.callback(clear)
    return sb, sem


def part_of(table, buf, name):
    at, _ = offsets(table)
    return buf[:, at[name][0]:at[name][0] + at[name][1]]


def run_lagged(u, steps, tiles=TILES):
    for par in range(2):
        for lag, step in steps:
            if (at := lagged(u, par, lag, tiles)) is not None:
                step(*at)

GROUP = 256
SORTED = T + (EXPERTS - 1) * GROUP



def context_attention(k, rows, scores):
    nc, x, ps = k.nc, k.x, k.ps
    with ExitStack() as ctx:
        sb, sem = stage_tools(ctx, k, "ca")
        ln = Norm(k, sb, sem, "ln")
        h, hT = sb("h", [P, 2 * D]), sb("hT", [P, 2 * D])
        mask, use_mask = sb("mask", [P, TILES * KEYS]), sb("use_mask", [P, KEYS], I32)
        logit, prob, attn = sb("logit", [P, 2 * KEYS]), sb("prob", [P, 2 * KEYS]), sb("attn", [P, 2 * P])
        negmax, total, rtotal = sb("negmax", [P, 2]), sb("total", [P, 2]), sb("rtotal", [P, 2])
        attnT = sb("attnT", [KEYS, P])
        flip = Flip(k, sem, "h", ps[0])
        tile_mask, mask_placed = sb("tile_mask", [P, 2 * KEYS]), sem("mask_placed")
        zeros = sb("zeros", [P, D])
        CHUNKS = 8
        chunk_loaded = [sem(f"chunk_loaded{c}") for c in range(CHUNKS)]
        tiles_loaded = sem("tiles_loaded")
        rest_loaded = sem("rest_loaded")
        scored = sem("scored")
        soft = sem("soft")
        exped = sem("exped")
        attended = sem("attended")
        a_turned, a_copied = sem("a_turned"), sem("a_copied")
        mixed = sem("mixed")
        x_done = sem("x_done")
        SOFT = 4
        gain, shift = part_of(ROWS, k.rows, "ln_g0"), part_of(ROWS, k.rows, "ln_b0")
        centroids = k.part("centroids").rearrange("p (c e) -> p c e", c=DC)
        by_expert = scores[:, :].rearrange("p (e t) -> p e t", t=TILES)
        outer, inner = Norm(k, sb, sem, "outer"), Norm(k, sb, sem, "inner")
        n, nT = sb("n", [P, 2 * D]), sb("nT", [P, 2 * D])
        nflip = Flip(k, sem, "n", ps[1])
        rows_loaded = sem("rows_loaded")
        x_added = sem("x_added")
        affine = sem("affine")
        kept = sem("kept")
        rated, score_set = sem("rated"), sem("score_set")
        ctxT = k.part("ctxT").rearrange("p (c b j) -> p c b j", c=DC, b=B)
        ctx_rows = k.part("ctx").rearrange("p (b d) -> p b d", b=B)

        with nc.Block() as block:

            @block.sync
            def _(sp):
                sp.dma_start(k.sec0[:, :], k.d_sec0).then_inc(k.loaded0, 16)

                for c in range(CHUNKS):
                    each = TILES // CHUNKS
                    part = slice(c * each * P, (c + 1) * each * P)
                    sp.dma_start(x[:, c * each * D:(c + 1) * each * D].rearrange("p (t d) -> p t d", d=D),
                                 k.d_x[part, :].rearrange("(t p) d -> p t d", p=P)).then_inc(chunk_loaded[c], 16)
                    sp.dma_start(mask[:, c * each * KEYS:(c + 1) * each * KEYS].rearrange("p (t j) -> p t j", j=KEYS),
                                 k.d_mask[part, :].rearrange("(t p) j -> p t j", p=P)).then_inc(chunk_loaded[c], 16)
                for c in range(CHUNKS):
                    sp.wait_ge(chunk_loaded[c], 32)
                    sp.sem_inc(tiles_loaded, TILES // CHUNKS)
                sp.dma_start(k.rows[:, :], k.d_rows.partition_broadcast(P)).then_inc(rows_loaded, 16)
                sp.wait_ge(k.set_up, 5)
                for r in range(T, SORTED, P):
                    sp.dma_start(k.d_rows_in[r:r + P, :], zeros[:, :]).then_inc(rest_loaded, 16)
                sp.dma_start(k.secA[:, 0:offsets(SEC1)[1]], k.d_sec1).then_inc(rest_loaded, 16)
                sp.dma_start(k.sec2[:, :], k.d_sec2).then_inc(rest_loaded, 16)
                sp.dma_start(k.sec65[:, :], k.d_sec65).then_inc(rest_loaded, 16)
                sp.wait_ge(rest_loaded, 48 + (SORTED - T) // P * 16)

            @block.gpsimd
            def _(pool):
                nc.gpsimd.memset(k.neghalf, -0.5).then_inc(k.set_up, 1)
                nc.gpsimd.memset(k.ones[:, :], 1.0).then_inc(k.set_up, 1)
                nc.gpsimd.memset(k.eps, LN_EPS).then_inc(k.set_up, 1)
                nc.gpsimd.memset(zeros[:, :], 0.0).then_inc(k.set_up, 1)
                pool.wait_ge(k.set_up, 5)

                def place_mask(t, q, _):
                    pool.wait_ge(tiles_loaded, t + 1)
                    at_least(pool, soft, (t - 2) * SOFT + 3)
                    nc.gpsimd.tensor_copy(tile_mask[:, q * KEYS:(q + 1) * KEYS],
                                          mask[:, cols(t, KEYS)]).then_inc(mask_placed, 1)

                def scale(t, q, _):
                    part = n[:, q * D:(q + 1) * D]
                    if isinstance(t, int) and t == 0:
                        pool.wait_ge(rows_loaded, 16)
                    pool.wait_ge(inner.done, t + 1)
                    nc.gpsimd.tensor_tensor(part, part, gain, ALU.mult).then_inc(affine, 1)
                    pool.wait_ge(affine, t * 2 + 1)
                    nc.gpsimd.tensor_tensor(part, part, shift, ALU.add).then_inc(affine, 1)

                def add_h(t, q, _):
                    pool.wait_ge(outer.done, t + 1)
                    nc.gpsimd.tensor_tensor(x[:, cols(t)], x[:, cols(t)], rows[:, cols(t)], ALU.add).then_inc(x_added, 1)
                over_tiles(pool, lambda u: run_lagged(u, [(7, lambda t, q, _: inner.power(pool, t, q)), (9, scale),
                                                          (0, lambda t, q, _: ln.power(pool, t, q)), (1, place_mask),
                                                          (7, add_h), (5, lambda t, q, _: outer.power(pool, t, q))]), 9)

            @block.vector
            def _(dve):
                nc.vector.memset(attn[:, :], 0.0).then_inc(k.set_up, 1)
                dve.wait_ge(k.set_up, 5)
                dve.wait_ge(k.loaded0, 16)
                nc.vector.tensor_copy(k.ident16[:, :], k.ident)
                nc.vector.tensor_copy(k.causal, k.part("causal").rearrange("p (a j) -> p a j", a=2))

                def stats(t, q, _):
                    dve.wait_ge(tiles_loaded, t + 1)
                    ln.stats(dve, x[:, cols(t)], t, q)

                def apply(t, q, _):
                    at_least(dve, flip.turned, t - 1)
                    ln.apply(dve, h[:, q * D:(q + 1) * D], x[:, cols(t)], t, q)

                def soften(t, q, _):
                    s = logit[:, q * KEYS:(q + 1) * KEYS]
                    m = tile_mask[:, q * KEYS:(q + 1) * KEYS]
                    dve.wait_ge(mask_placed, t + 1)
                    dve.wait_ge(scored, t + 1)
                    at_least(dve, exped, t - 1)
                    nc.vector.tensor_scalar(s, ps[2 + q][:, 0:KEYS], D ** -0.5, None, ALU.mult).then_inc(soft, 1)
                    nc.vector.tensor_scalar(use_mask[:, :], m, -1.0, None, ALU.is_lt).then_inc(soft, 1)
                    wait_apart(nc, dve, soft, t * SOFT + 2, k.spare)
                    nc.vector.copy_predicated(s, use_mask[:, :], m).then_inc(soft, 1)
                    dve.wait_ge(soft, t * SOFT + 3)
                    nc.vector.tensor_reduce(negmax[:, q:q + 1], s, AX, ALU.max, negate=True).then_inc(soft, 1)

                def weigh(t, q, _):
                    dve.wait_ge(exped, t + 1)
                    nc.vector.reciprocal(rtotal[:, q:q + 1], total[:, q:q + 1]).then_inc(attended, 1)
                    dve.wait_ge(attended, t * 2 + 1)
                    at_least(dve, a_turned, t - 1)
                    nc.vector.tensor_scalar(attn[:, q * P:q * P + KEYS], prob[:, q * KEYS:(q + 1) * KEYS],
                                            rtotal[:, q:q + 1], 0.0, ALU.mult, ALU.max).then_inc(attended, 1)

                def add(t, q, _):
                    dve.wait_ge(mixed, t + 1)
                    nc.vector.tensor_tensor(x[:, cols(t)], ps[6 + q][:, 0:D], x[:, cols(t)], ALU.add).then_inc(x_done, 1)

                def outer_stats(t, q, _):
                    wait_apart(nc, dve, x_done, t + 1, k.spare)
                    outer.stats(dve, x[:, cols(t)], t, q)

                def outer_apply(t, q, _):
                    outer.apply(dve, rows[:, cols(t)], x[:, cols(t)], t, q)
                    wait_apart(nc, dve, outer.done, t + 1, k.spare)
                    inner.stats(dve, rows[:, cols(t)], t, q)

                def inner_apply(t, q, _):
                    dve.wait_ge(x_added, t + 1)
                    at_least(dve, affine, t * 2 - 2)
                    at_least(dve, nflip.turned, t - 1)
                    at_least(dve, kept, t - 1)
                    inner.apply(dve, n[:, q * D:(q + 1) * D], rows[:, cols(t)], t, q)
                over_tiles(dve, lambda u: run_lagged(u, [(1, apply), (8, inner_apply), (3, weigh), (2, soften), (0, stats),
                                                         (6, outer_apply), (5, add), (5, outer_stats)]), 8)

            @block.scalar
            def _(act):
                def copy_h(t, q, _):
                    at_least(act, scored, t - 1)
                    flip.copy(act, hT[:, q * D:(q + 1) * D], t)

                def copy_attention(t, q, _):
                    act.wait_ge(a_turned, t + 1)
                    at_least(act, mixed, t)
                    nc.scalar.activation(attnT[:, :], ps[4][0:KEYS, 0:P], ACT.Copy).then_inc(a_copied, 1)

                def exponential(t, q, _):
                    act.wait_ge(soft, t * SOFT + 4)
                    at_least(act, attended, (t - 1) * 2)
                    nc.scalar.activation(prob[:, q * KEYS:(q + 1) * KEYS], logit[:, q * KEYS:(q + 1) * KEYS],
                                         ACT.Exp, bias=negmax[:, q:q + 1],
                                         accum_out=total[:, q:q + 1]).then_inc(exped, 1)

                def keep(t, q, _):
                    act.wait_ge(affine, t * 2 + 2)
                    nc.scalar.activation(rows[:, cols(t)], n[:, q * D:(q + 1) * D], ACT.Copy).then_inc(kept, 1)

                def copy_n(t, q, _):
                    at_least(act, rated, t - 1)
                    nflip.copy(act, nT[:, q * D:(q + 1) * D], t)

                def set_scores(t, q, _):
                    act.wait_ge(rated, t + 1)
                    nc.scalar.activation(by_expert[:, :, bass.ds(t, 1)], ps[5][:, 0:EXPERTS].unsqueeze(2),
                                         ACT.Copy).then_inc(score_set, 1)
                over_tiles(act, lambda u: run_lagged(u, [(10, set_scores), (1, copy_h), (4, copy_attention), (2, exponential),
                                                         (9, keep), (9, copy_n)]), 10)

            @block.tensor
            def _(pe):
                pe.wait_ge(k.loaded0, 16)
                pe.wait_ge(k.set_up, 5)

                def turn_h(t, q, _):
                    pe.wait_ge(ln.done, t + 1)
                    flip.turn(pe, lambda c: h[:, q * D + c * P:q * D + (c + 1) * P], t)

                def turn_attention(t, q, _):
                    pe.wait_ge(attended, t * 2 + 2)
                    at_least(pe, a_copied, t)
                    nc.tensor.transpose(ps[4][:, 0:P], attn[:, q * P:(q + 1) * P], k.ident).then_inc(a_turned, 1)

                def score(t, q, _):
                    pe.wait_ge(flip.copied, t + 1)
                    at_least(pe, soft, (t - 2) * SOFT + 1)
                    for c in range(DC):
                        last = nc.tensor.matmul(ps[2 + q][:, 0:KEYS], hT[:, q * D + c * P:q * D + (c + 1) * P],
                                                ctxT[:, c, bass.ds(t // TPB, 1), 0:KEYS],
                                                start=(c == 0), stop=(c == DC - 1))
                    last.then_inc(scored, 1)

                def mix(t, q, _):
                    pe.wait_ge(a_copied, t + 1)
                    at_least(pe, x_done, t - 1)
                    nc.tensor.matmul(ps[6 + q][:, 0:D], attnT[:, :], ctx_rows[0:KEYS, bass.ds(t // TPB, 1), :],
                                     start=True, stop=True).then_inc(mixed, 1)

                def turn_n(t, q, _):
                    pe.wait_ge(affine, t * 2 + 2)
                    nflip.turn(pe, lambda c: n[:, q * D + c * P:q * D + (c + 1) * P], t)

                def rate(t, q, _):
                    pe.wait_ge(nflip.copied, t + 1)
                    at_least(pe, score_set, t)
                    for c in range(DC):
                        last = nc.tensor.matmul(ps[5][:, 0:EXPERTS], nT[:, q * D + c * P:q * D + (c + 1) * P],
                                                centroids[:, c, :], start=(c == 0), stop=(c == DC - 1))
                    last.then_inc(rated, 1)
                over_tiles(pe, lambda u: run_lagged(u, [(1, turn_h), (4, turn_attention), (1, score), (4, mix),
                                                        (9, turn_n), (9, rate)]), 9)



def head_attention(k, name, heads, table, buf, bq, bk, bv, bo, src, normalised, causal=False, loads=(), ahead=None):
    nc, ps, ident = k.nc, k.ps, k.ident
    hd = D // heads
    hpc = heads // DC
    pairs = heads // 2
    W = 2 * hd + 2
    SC = hpc * KEYS
    part = lambda n: part_of(table, buf, n).rearrange("p (c o) -> p c o", c=DC)
    wq, wk, wv, wo = part("wq"), part("wk"), part("wv"), part("wo")
    hmask = k.part("hmask16" if heads == 16 else "hmask8")
    vmask = k.part("vmask")
    ctxT = k.part("ctxT").rearrange("p (c b j) -> p c b j", c=DC, b=B)
    bq, bk = k.part(bq), k.part(bk)
    bv, bo = part_of(ROWS, k.rows, bv), part_of(ROWS, k.rows, bo)
    with ExitStack() as ctx:
        sb, sem = stage_tools(ctx, k, name)
        kT = sb("kT", [P, DC * B * KEYS])
        kbd = sb("kbd", [P, B * DC * SC])
        v = sb("v", [P, B * D])
        vbd = sb("vbd", [P, B * pairs * W])
        h = sb("h", [P, 2 * D])
        hT, qT = sb("hT", [P, 2 * D]), sb("qT", [P, 2 * D])
        p = sb("p", [P, 2 * DC * SC])
        pT = sb("pT", [P, 2 * DC * SC])
        mx, rs = sb("mx", [P, heads]), sb("rs", [P, heads])
        o, oT = sb("o", [P, D]), sb("oT", [P, D])
        ln = Norm(k, sb, sem, "ln") if normalised else None
        h_set = ln.done if normalised else sem("h_set")
        flip, oflip = Flip(k, sem, "h", ps[4]), Flip(k, sem, "o", ps[7])
        kv_made, kv_set = sem("kv_made"), sem("kv_set")
        q_made, q_set = sem("q_made"), sem("q_set")
        scored = sem("scored")
        shifted = sem("shifted")
        exped = sem("exped")
        p_turned, p_copied = sem("p_turned"), sem("p_copied")
        mixed = sem("mixed")
        scaled = sem("scaled")
        projected = sem("projected")
        biased = sem("biased")
        added = sem("added")
        more_loaded = sem("more_loaded")
        v3 = vbd[:, :].rearrange("p (b j w) -> p b j w", b=B, j=pairs)
        k4 = kbd[:, :].rearrange("p (b c s) -> p b c s", b=B, c=DC)
        one_bank = SC * DC <= 512
        score_bank = [ps[0][:, c * SC:(c + 1) * SC] if one_bank else ps[c][:, 0:SC] for c in range(DC)]
        p_bank = [ps[2][:, c * SC:(c + 1) * SC] if one_bank else ps[2 + c][:, 0:SC] for c in range(DC)]
        q_bank = ps[4][:, D:2 * D] if ahead else ps[5][:, 0:D]
        upto = lambda c: DC if one_bank else c + 1
        behind = DIAGONAL_LAG if ahead else 0
        first_gpsimd = lambda eng: []
        first_vector = first_scalar = first_tensor = lambda eng: ([], [])
        if ahead:
            first_vector, first_gpsimd, first_scalar, first_tensor, src_set = ahead(k, sb, sem, src)
        KV = 2 + B * DC + B + B + 1

        with nc.Block() as block:

            @block.sync
            def _(sp):
                for to, of in loads:
                    sp.dma_start(to, of).then_inc(more_loaded, 16)
                if loads:
                    sp.wait_ge(more_loaded, 16 * len(loads))

            @block.tensor
            def _(pe):
                for m in range(DC):
                    for c in range(DC):
                        nc_last = nc.tensor.matmul(ps[m][:, 0:B * KEYS], wk[:, c, m * P:(m + 1) * P],
                                                   ctxT[:, c, :, 0:KEYS], start=(c == 0), stop=(c == DC - 1))
                    nc_last.then_inc(kv_made, 1)
                for b in range(B):
                    for c in range(DC):
                        nc_last = nc.tensor.matmul(ps[2 + b][:, 0:D], ctxT[:, c, b, :], wv[:, c, :],
                                                   start=(c == 0), stop=(c == DC - 1))
                    nc_last.then_inc(kv_made, 1)
                pe.wait_ge(kv_set, KV)

                def mix(t, q, n):
                    pe.wait_ge(p_copied, t * 2 + 2)
                    at_least(pe, scaled, t * 2)
                    for j in range(pairs):
                        last = nc.tensor.matmul(ps[6][:, j * W:(j + 1) * W],
                                                pT[:, q * DC * SC + j * P:q * DC * SC + (j + 1) * P],
                                                v3[:, bass.ds(t // TPB, 1), j, :], start=True, stop=True)
                    last.then_inc(mixed, 1)

                def turn_h(t, q, n):
                    pe.wait_ge(h_set, t + 1)
                    at_least(pe, q_set, t * 2)
                    flip.turn(pe, lambda c: h[:, q * D + c * P:q * D + (c + 1) * P], t)

                def score(t, q, n):
                    for c in range(DC):
                        pe.wait_ge(q_set, t * 2 + c + 1)
                        at_least(pe, shifted, (t - 1) * 4 + 2 + upto(c))
                        last = nc.tensor.matmul(score_bank[c], qT[:, q * D + c * P:q * D + (c + 1) * P],
                                                k4[:, bass.ds(t // TPB, 1), c, :], start=True, stop=not causal)
                        if causal:
                            first = t % TPB
                            later = min(first, 1) if isinstance(first, int) else (first + TPB - 1) // TPB
                            last = nc.tensor.matmul(score_bank[c], k.ident16[:, :],
                                                    k.causal[:, bass.ds(later, 1), :].to_broadcast([P, hpc, KEYS]),
                                                    start=False, stop=True)
                        last.then_inc(scored, 1)

                def turn_o(t, q, n):
                    pe.wait_ge(scaled, t * 2 + 2)
                    at_least(pe, added, t)
                    oflip.turn(pe, lambda c: o[:, c * P:(c + 1) * P], t)

                def project_q(t, q, n):
                    pe.wait_ge(flip.copied, t + 1)
                    at_least(pe, q_set, t * 2)
                    for m in range(DC):
                        for c in range(DC):
                            last = nc.tensor.matmul(q_bank[:, m * P:(m + 1) * P], wq[:, c, m * P:(m + 1) * P],
                                                    hT[:, q * D + c * P:q * D + (c + 1) * P],
                                                    start=(c == 0), stop=(c == DC - 1))
                    last.then_inc(q_made, 1)

                def turn_p(t, q, n):
                    for c in range(DC):
                        pe.wait_ge(exped, t * 2 + c + 1)
                        at_least(pe, p_copied, (t - 1) * 2 + upto(c))
                        for j in range(hpc // 2):
                            at = (q * DC + c) * SC + j * P
                            last = nc.tensor.transpose(p_bank[c][:, j * P:(j + 1) * P], p[:, at:at + P], ident)
                        last.then_inc(p_turned, 1)

                def project_o(t, q, n):
                    pe.wait_ge(oflip.copied, t + 1)
                    for c in range(DC):
                        last = nc.tensor.matmul(ps[7][:, D:2 * D], oT[:, c * P:(c + 1) * P], wo[:, c, :],
                                                start=(c == 0), stop=(c == DC - 1))
                    last.then_inc(projected, 1)

                early, late = first_tensor(pe)
                steps = [(behind + 4, mix), (behind + 1, turn_h), (behind + 2, score)] + early \
                    + [(behind + 3, turn_p), (behind + 4, turn_o)] + late \
                    + [(behind + 1, project_q), (behind + 4, project_o)]
                over_tiles(pe, lambda u: run_lagged(u, steps), behind + 4)

            @block.gpsimd
            def _(pool):
                def power(t, q, n):
                    ln.power(pool, t, q)

                def add_bias(t, q, n):
                    pool.wait_ge(h_set, t + 1)
                    nc.gpsimd.tensor_tensor(src[:, cols(t)], src[:, cols(t)], bo, ALU.add).then_inc(biased, 1)
                steps = first_gpsimd(pool) + [(0, power)] * normalised + [(behind + 2, add_bias)]
                over_tiles(pool, lambda u: run_lagged(u, steps), behind + 2)

            @block.vector
            def _(dve):
                for m in range(DC):
                    dve.wait_ge(kv_made, m + 1)
                    nc.vector.tensor_scalar(kT[:, m * D:(m + 1) * D], ps[m][:, 0:B * KEYS], bk[:, m:m + 1], None,
                                            ALU.add).then_inc(kv_set, 1)
                dve.wait_ge(kv_set, DC)
                for b in range(B):
                    for m in range(DC):
                        at = m * D + b * KEYS
                        nc.vector.tensor_tensor(
                            k4[:, b, m, :].rearrange("p (h j) -> p h j", h=hpc),
                            kT[:, at:at + KEYS].unsqueeze(1).to_broadcast([P, hpc, KEYS]),
                            hmask[:, 0:hpc].unsqueeze(2).to_broadcast([P, hpc, KEYS]), ALU.mult).then_inc(kv_set, 1)
                for b in range(B):
                    dve.wait_ge(kv_made, DC + b + 1)
                    nc.vector.tensor_tensor(v[:, b * D:(b + 1) * D], ps[2 + b][:, 0:D], bv, ALU.add).then_inc(kv_set, 1)
                dve.wait_ge(kv_set, DC + B * DC + B)
                for b in range(B):
                    nc.vector.tensor_tensor(
                        v3[:, b, :, 0:2 * hd].rearrange("p j (s d) -> p j s d", s=2),
                        v[:, b * D:(b + 1) * D].rearrange("p (j s d) -> p j s d", s=2, d=hd),
                        vmask.unsqueeze(1).unsqueeze(3).to_broadcast([P, pairs, 2, hd]), ALU.mult).then_inc(kv_set, 1)
                nc.vector.tensor_copy(vbd[:, :].rearrange("p (n w) -> p n w", w=W)[:, :, 2 * hd:W],
                                      vmask.unsqueeze(1).to_broadcast([P, B * pairs, 2])).then_inc(kv_set, 1)

                def scale_heads(t, q, n):
                    heads_ps = ps[6][:, 0:pairs * W].rearrange("p (j w) -> p j w", w=W)
                    dve.wait_ge(mixed, t + 1)
                    at_least(dve, scaled, t * 2)
                    nc.vector.reciprocal(rs[:, :].rearrange("p (j s) -> p j s", s=2),
                                         heads_ps[:, :, 2 * hd:W]).then_inc(scaled, 1)
                    dve.wait_ge(scaled, t * 2 + 1)
                    at_least(dve, oflip.turned, t)
                    nc.vector.tensor_tensor(
                        o[:, :].rearrange("p (j s d) -> p j s d", s=2, d=hd),
                        heads_ps[:, :, 0:2 * hd].rearrange("p j (s d) -> p j s d", s=2),
                        rs[:, :].rearrange("p (j s) -> p j s", s=2).unsqueeze(3).to_broadcast([P, pairs, 2, hd]),
                        ALU.mult).then_inc(scaled, 1)

                def shift(t, q, n):
                    s3 = [score_bank[c].rearrange("p (h j) -> p h j", j=KEYS) for c in range(DC)]
                    for c in range(DC):
                        dve.wait_ge(scored, t * 2 + upto(c))
                        at_least(dve, shifted, t * 4 + c - 1)
                        nc.vector.tensor_reduce(mx[:, c * hpc:(c + 1) * hpc], s3[c], AX, ALU.max).then_inc(shifted, 1)
                    for c in range(DC):
                        dve.wait_ge(shifted, t * 4 + c + 1)
                        at_least(dve, p_turned, (t - 2) * 2 + c + 1)
                        at = (q * DC + c) * SC
                        nc.vector.tensor_tensor(p[:, at:at + SC].rearrange("p (h j) -> p h j", j=KEYS), s3[c],
                                                mx[:, c * hpc:(c + 1) * hpc].unsqueeze(2).to_broadcast([P, hpc, KEYS]),
                                                ALU.subtract).then_inc(shifted, 1)

                def stats(t, q, n):
                    ln.stats(dve, src[:, cols(t)], t, q)

                def add(t, q, n):
                    dve.wait_ge(projected, t + 1)
                    dve.wait_ge(biased, t + 1)
                    nc.vector.tensor_tensor(src[:, cols(t)], ps[7][:, D:2 * D], src[:, cols(t)],
                                            ALU.add).then_inc(added, 1)

                def apply(t, q, n):
                    at_least(dve, flip.turned, t - 1)
                    if normalised:
                        ln.apply(dve, h[:, q * D:(q + 1) * D], src[:, cols(t)], t, q)
                    else:
                        dve.wait_ge(src_set, t * 2 + 2)
                        nc.vector.tensor_copy(h[:, q * D:(q + 1) * D], src[:, cols(t)]).then_inc(h_set, 1)
                early, late = first_vector(dve)
                steps = [(behind + 1, apply)] + [(0, stats)] * normalised + [(behind + 5, add)] + early \
                    + [(behind + 4, scale_heads), (behind + 2, shift)] + late
                over_tiles(dve, lambda u: run_lagged(u, steps), behind + 5)

            @block.scalar
            def _(act):
                def copy_h(t, q, n):
                    at_least(act, q_made, t - 1)
                    flip.copy(act, hT[:, q * D:(q + 1) * D], t)

                def copy_o(t, q, n):
                    at_least(act, projected, t)
                    oflip.copy(act, oT[:, :], t)

                def set_q(t, q, n):
                    act.wait_ge(q_made, t + 1)
                    at_least(act, scored, (t - 1) * 2)
                    for m in range(DC):
                        nc.scalar.activation(qT[:, q * D + m * P:q * D + (m + 1) * P], q_bank[:, m * P:(m + 1) * P],
                                             ACT.Identity, bias=bq[:, m:m + 1]).then_inc(q_set, 1)

                def copy_p(t, q, n):
                    at_least(act, mixed, t - 1)
                    for c in range(DC):
                        act.wait_ge(p_turned, t * 2 + upto(c))
                        at = (q * DC + c) * SC
                        nc.scalar.activation(pT[:, at:at + SC], p_bank[c], ACT.Copy).then_inc(p_copied, 1)

                def exponential(t, q, n):
                    for c in range(DC):
                        act.wait_ge(shifted, t * 4 + c + 3)
                        at = (q * DC + c) * SC
                        nc.scalar.activation(p[:, at:at + SC], p[:, at:at + SC], ACT.Exp,
                                             scale=hd ** -0.5).then_inc(exped, 1)
                early, late = first_scalar(act)
                steps = [(behind + 1, copy_h)] + early + [(behind + 3, copy_p), (behind + 4, copy_o)] + late \
                    + [(behind + 1, set_q), (behind + 2, exponential)]
                over_tiles(act, lambda u: run_lagged(u, steps), behind + 4)



def balanced_assignment(k, scores):
    nc, ps = k.nc, k.ps
    NIB, ROUNDS = 15, 8
    SHARE = T // EXPERTS
    onehot = k.onehot[:, :].rearrange("p (e t) -> p e t", t=TILES)
    by_expert = scores[:, :].rearrange("p (e t) -> p e t", t=TILES)
    with ExitStack() as ctx:
        sb, sem = stage_tools(ctx, k, "ba")
        left, taken = sb("left", [P, TILES]), sb("taken", [P, TILES])
        nibble = sb("nibble", [P, NIB], I32)
        steps = sb("steps", [P, ROUNDS * NIB], I32)
        prefix, digit, fixed = sb("prefix", [P, 1], I32), sb("digit", [P, 1], I32), sb("fixed", [P, 1], I32)
        first_bits, sign, bits = sb("first_bits", [P, NIB], I32), sb("sign", [P, NIB], I32), sb("bits", [P, NIB], I32)
        above = sb("above", [P, NIB * TILES])
        count, over = sb("count", [P, NIB]), sb("over", [P, NIB])
        equal, before = sb("equal", [P, TILES + 1]), sb("before", [P, TILES + 1])
        PAD = TILES // 2
        scans = [sb(f"scan{i}", [P, PAD + TILES]) for i in range(2)]
        gt, ranks_ok, limit = sb("gt", [P, TILES]), sb("ranks_ok", [P, TILES]), sb("limit", [P, 1])
        chain = sem("chain")
        counted, summed = sem("counted"), sem("summed")
        ranked_in, ranked = sem("ranked_in"), sem("ranked")
        EXPERT = ROUNDS * 5 + 17

        def ordered_to_float(step, bits, cand, sign):
            step(nc.vector.tensor_scalar(sign, cand, -1, 31, ALU.bitwise_xor, ALU.arith_shift_right))
            step(nc.vector.scalar_tensor_tensor(bits, sign, -2 ** 31, cand, ALU.bitwise_or, ALU.bitwise_xor))

        with nc.Block() as block:

            @block.vector
            def _(dve):
                done = [0]

                def step(ins, e=0):
                    done[0] += 1
                    ins.then_inc(chain, 1)
                    dve.wait_ge(chain, e * EXPERT + done[0])

                step(nc.vector.tensor_copy(nibble[:, :], k.part("nibble")))
                for r in range(ROUNDS):
                    step(nc.vector.tensor_scalar(steps[:, r * NIB:(r + 1) * NIB], nibble[:, :], 28 - 4 * r, None,
                                                 ALU.logical_shift_left))
                ordered_to_float(step, first_bits[:, :], steps[:, 0:NIB], sign[:, :])
                for scan in scans:
                    step(nc.vector.memset(scan[:, :], 0.0))
                step(nc.vector.memset(taken[:, :], 0.0))
                step(nc.vector.memset(equal[:, :], 0.0))
                head = done[0]

                def expert(e):
                    done[0] = head

                    def st(ins):
                        step(ins, e)
                    st(nc.vector.scalar_tensor_tensor(left[:, :], taken[:, :], -3e38,
                                                      by_expert[:, bass.ds(e, 1), :].squeeze(1), ALU.mult, ALU.add))
                    for r in range(ROUNDS):
                        if r:
                            st(nc.vector.tensor_tensor(bits[:, :], steps[:, r * NIB:(r + 1) * NIB],
                                                       prefix[:, :].to_broadcast([P, NIB]), ALU.bitwise_xor))
                        st(nc.vector.tensor_tensor(
                            above[:, :].rearrange("p (c t) -> p c t", t=TILES),
                            left[:, :].unsqueeze(1).to_broadcast([P, NIB, TILES]),
                            (bits if r else first_bits)[:, :].bitcast(FP32).unsqueeze(2).to_broadcast([P, NIB, TILES]),
                            ALU.is_ge))
                        nc.vector.tensor_reduce(count[:, :], above[:, :].rearrange("p (c t) -> p c t", t=TILES),
                                                AX, ALU.add).then_inc(counted, 1)
                        dve.wait_ge(summed, e * ROUNDS + r + 1)
                        st(nc.vector.tensor_scalar(over[:, :], ps[0][:, 0:NIB], SHARE - 0.5, None, ALU.is_ge))
                        with nc.allow_low_precision(reason="a count of up to 15, exact"):
                            st(nc.vector.tensor_reduce(digit[:, :], over[:, :], AX, ALU.add))
                        if r == 0:
                            st(nc.vector.tensor_scalar(fixed[:, :], digit[:, :], 28, None, ALU.logical_shift_left))
                            ordered_to_float(st, prefix[:, :], fixed[:, :], sign[:, 0:1])
                        else:
                            st(nc.vector.scalar_tensor_tensor(prefix[:, :], digit[:, :], 28 - 4 * r, prefix[:, :],
                                                              ALU.logical_shift_left, ALU.bitwise_xor))
                    lowest = prefix[:, :].bitcast(FP32)
                    st(nc.vector.tensor_scalar(gt[:, :], left[:, :], lowest, None, ALU.is_gt))
                    st(nc.vector.tensor_scalar(equal[:, 0:TILES], left[:, :], lowest, None, ALU.is_equal))
                    st(nc.vector.tensor_reduce(before[:, TILES:TILES + 1], gt[:, :], AX, ALU.add))
                    st(nc.vector.tensor_copy(scans[0][:, PAD:], equal[:, 0:TILES]))
                    for i, s in enumerate((1, 2, 4, 8, 16)):
                        old, new = scans[i % 2], scans[1 - i % 2]
                        st(nc.vector.tensor_tensor(new[:, PAD:], old[:, PAD:], old[:, PAD - s:PAD + TILES - s], ALU.add))
                    src = new[:, PAD:]
                    nc.vector.tensor_tensor(before[:, 0:TILES], src, equal[:, 0:TILES],
                                            ALU.subtract).then_inc(ranked_in, 1)
                    dve.wait_ge(ranked, e + 1)
                    st(nc.vector.tensor_scalar(limit[:, :], ps[1][:, TILES:TILES + 1], -1.0, float(SHARE),
                                               ALU.mult, ALU.add))
                    st(nc.vector.tensor_scalar(ranks_ok[:, :], ps[1][:, 0:TILES], limit[:, :], None, ALU.is_lt))
                    st(nc.vector.tensor_tensor(ranks_ok[:, :], ranks_ok[:, :], equal[:, 0:TILES], ALU.mult))
                    st(nc.vector.tensor_tensor(gt[:, :], gt[:, :], ranks_ok[:, :], ALU.add))
                    st(nc.vector.tensor_copy(onehot[:, bass.ds(e, 1), :].squeeze(1), gt[:, :]))
                    st(nc.vector.tensor_tensor(taken[:, :], taken[:, :], gt[:, :], ALU.add))
                    assert done[0] - head == EXPERT, done[0] - head
                    done[0] = head

                expert(0)
                with dve.Fori(1, EXPERTS - 1) as e:
                    expert(e)
                nc.vector.tensor_scalar(onehot[:, EXPERTS - 1, :], taken[:, :], -1.0, 1.0, ALU.mult, ALU.add)

            @block.tensor
            def _(pe):
                def expert(e):
                    for r in range(ROUNDS):
                        pe.wait_ge(counted, e * ROUNDS + r + 1)
                        nc.tensor.matmul(ps[0][:, 0:NIB], k.ones[:, :], count[:, :], start=True,
                                         stop=True).then_inc(summed, 1)
                    pe.wait_ge(ranked_in, e + 1)
                    nc.tensor.matmul(ps[1][:, 0:TILES + 1], k.part("tri"), equal[:, :], start=True, stop=False)
                    nc.tensor.matmul(ps[1][:, 0:TILES + 1], k.ones[:, :], before[:, :], start=False,
                                     stop=True).then_inc(ranked, 1)
                expert(0)
                with pe.Fori(1, EXPERTS - 1) as e:
                    expert(e)


def place(k, rows, name, padded):
    nc, ps = k.nc, k.ps
    NG = SORTED // GROUP
    with ExitStack() as ctx:
        sb, sem = stage_tools(ctx, k, name)
        PAD = TILES // 2
        bufs = [sb(f"scan{i}", [P, EXPERTS * (PAD + TILES)]) for i in range(2)]
        before, spread = sb("before", [P, EXPERTS * TILES]), sb("spread", [P, EXPERTS * TILES])
        totals, posf, base = sb("totals", [P, EXPERTS]), sb("posf", [P, TILES]), sb("base", [P, EXPERTS])
        size, sizei, at_or_past = sb("size", [P, EXPERTS]), sb("sizei", [P, EXPERTS], I32), sb("past", [P, NG * 7])
        groupf = sb("groupf", [P, NG])
        chain, scanned, ranked, placed, sent = sem("chain"), sem("scanned"), sem("ranked"), sem("placed"), sem("sent")
        three = lambda a: a[:, :].rearrange("p (e t) -> p e t", t=TILES)

        with nc.Block() as block:

            @block.vector
            def _(dve):
                done = [0]

                def step(ins):
                    done[0] += 1
                    ins.then_inc(chain, 1)
                    dve.wait_ge(chain, done[0])
                wide = [a[:, :].rearrange("p (e t) -> p e t", t=PAD + TILES) for a in bufs]
                for buf in bufs:
                    step(nc.vector.memset(buf[:, :], 0.0))
                step(nc.vector.tensor_copy(wide[0][:, :, PAD:], three(k.onehot)))
                for i, s in enumerate((1, 2, 4, 8, 16)):
                    old, new = wide[i % 2], wide[1 - i % 2]
                    step(nc.vector.tensor_tensor(new[:, :, PAD:], old[:, :, PAD:], old[:, :, PAD - s:PAD + TILES - s],
                                                 ALU.add))
                src = new[:, :, PAD:]
                step(nc.vector.tensor_copy(totals[:, :].unsqueeze(2), src[:, :, TILES - 1:TILES]))
                nc.vector.tensor_tensor(three(before), src, three(k.onehot), ALU.subtract).then_inc(scanned, 1)
                dve.wait_ge(ranked, 1)
                if padded:
                    step(nc.vector.tensor_scalar(sizei[:, :], ps[1][:, 0:EXPERTS], GROUP - 1.0, None, ALU.add))
                    step(nc.vector.tensor_scalar(sizei[:, :], sizei[:, :], -GROUP, None, ALU.bitwise_and))
                    step(nc.vector.tensor_copy(size[:, :], sizei[:, :]))
                    step(nc.vector.memset(base[:, :], 0.0))
                    for e in range(1, EXPERTS):
                        step(nc.vector.tensor_tensor(base[:, e:e + 1], base[:, e - 1:e], size[:, e - 1:e], ALU.add))
                    step(nc.vector.tensor_tensor(
                        at_or_past[:, :].rearrange("p (g e) -> p g e", e=7),
                        k.part("tstart")[:, 0:NG].unsqueeze(2).to_broadcast([P, NG, 7]),
                        base[:, 1:EXPERTS].unsqueeze(1).to_broadcast([P, NG, 7]), ALU.is_ge))
                    step(nc.vector.tensor_reduce(groupf[:, :], at_or_past[:, :].rearrange("p (g e) -> p g e", e=7),
                                                 AX, ALU.add))
                    step(nc.vector.tensor_copy(k.tile_expert[:, 0:NG], groupf[:, :]))
                    first = base[:, :]
                else:
                    first = k.part("base0")
                step(nc.vector.tensor_tensor(three(spread), ps[0][:, 0:EXPERTS * TILES].rearrange("p (e t) -> p e t", t=TILES),
                                             first.unsqueeze(2).to_broadcast([P, EXPERTS, TILES]), ALU.add))
                step(nc.vector.tensor_tensor(spread[:, :], spread[:, :], k.onehot[:, :], ALU.mult))
                step(nc.vector.tensor_reduce(posf[:, :], spread[:, :].rearrange("p (e t) -> p t e", t=TILES), AX, ALU.add))
                nc.vector.tensor_copy(k.pos[:, :], posf[:, :]).then_inc(placed, 1)

            @block.tensor
            def _(pe):
                pe.wait_ge(scanned, 1)
                nc.tensor.matmul(ps[0][:, 0:EXPERTS * TILES], k.part("tri"), k.onehot[:, :], start=True, stop=False)
                nc.tensor.matmul(ps[0][:, 0:EXPERTS * TILES], k.ones[:, :], before[:, :], start=False, stop=True)
                nc.tensor.matmul(ps[1][:, 0:EXPERTS], k.ones[:, :], totals[:, :], start=True,
                                 stop=True).then_inc(ranked, 1)

            @block.gpsimd
            def _(pool):
                pool.wait_ge(placed, 1)
                for t in range(TILES):
                    nc.gpsimd.indirect_dma_start(
                        out=k.d_rows_in, out_offset=bass.IndirectOffsetOnAxis(ap=k.pos[:, t:t + 1], axis=0),
                        in_=rows[:, t * D:(t + 1) * D], in_offset=None).then_inc(sent, 16)
                pool.wait_ge(sent, 16 * TILES)


def expert_ffn(k, name, w1, w2, func, tiles, sub, biased):
    nc, ps, ident = k.nc, k.ps, k.ident
    A = GROUP // P
    UN = 2 * sub
    with ExitStack() as ctx:
        sb, sem = stage_tools(ctx, k, name)
        w1s, w2s = sb("w1", [P, 2 * DC * F]), sb("w2", [P, 2 * FC * D])
        rows, rowsT = sb("rows", [P, 2 * A * D]), sb("rowsT", [P, 2 * DC * GROUP])
        hid, res = sb("hid", [P, FC * GROUP]), sb("res", [P, 2 * A * D])
        b2 = sb("b2", [P, 2 * D]) if biased else None
        b1, eb1, b1_set = sb("b1", [P, FC]), k.part("eb1"), sem("b1_set")
        weights_loaded = [sem("weights_loaded0"), sem("weights_loaded1")]
        rows_loaded = [sem("rows_loaded0"), sem("rows_loaded1")]
        res_stored = [sem("res_stored0"), sem("res_stored1")]
        turned, copied = sem("turned"), sem("copied")
        hid_made, hid_set = sem("hid_made"), sem("hid_set")
        res_made, res_set = sem("res_made"), sem("res_set")
        PAIRS = FC // 2

        def tile(u, i, lag):
            t = u * UN + (i - lag)
            if isinstance(t, int) and not 0 <= t < tiles:
                return None
            r = (i - lag) % UN
            back = (i - lag - r) // UN
            pair = u * sub + back * sub + r // 2
            return t, r % 2, r // sub % 2, pair, u + back, r

        def over(eng, steps):
            def body(u):
                for i in range(UN):
                    for lag, step in steps:
                        if (at := tile(u, i, lag)) is not None:
                            step(*at)
            lag = max(s[0] for s in steps)
            head = 2 if sub == 2 else 3
            for u in range(head):
                body(u)
            with eng.Fori(head, tiles // UN) as u:
                body(u)
            for u in range(tiles // UN, (tiles + lag + UN - 1) // UN):
                body(u)

        with nc.Block() as block:

            @block.gpsimd
            def _(pool):
                def load(t, q, g, pair, gp, r):
                    if r % sub == 0:
                        expert = gp * 2 + g if biased else pool.value_load(
                            k.tile_expert[0:1, t:t + 1] if isinstance(t, int) else k.tile_expert[0:1, bass.ds(t, 1)],
                            min_val=0, max_val=EXPERTS - 1)
                        at_least(pool, res_made, t - sub)
                        pool.dma_start(w1s[:, g * DC * F:(g + 1) * DC * F], w1[bass.ds(expert, 1)].squeeze(0))\
                            .then_inc(weights_loaded[g], 16)
                        pool.dma_start(w2s[:, g * FC * D:(g + 1) * FC * D], w2[bass.ds(expert, 1)].squeeze(0))\
                            .then_inc(weights_loaded[g], 16)
                        if biased:
                            at_least(pool, res_set, (t - sub) * A)
                            pool.dma_start(b2[:, g * D:(g + 1) * D], k.d_b2a[bass.ds(expert, 1)].squeeze(0)
                                           .partition_broadcast(P)).then_inc(weights_loaded[g], 16)
                    at_least(pool, turned, t - 1)
                    pool.dma_start(rows[:, q * A * D:(q + 1) * A * D].rearrange("p (a d) -> p a d", d=D),
                                   k.d_rows_in[bass.ds(t * GROUP, GROUP), :].rearrange("(a p) d -> p a d", p=P))\
                        .then_inc(rows_loaded[q], 16)

                over(pool, [(0, load)])

            @block.tensor
            def _(pe):
                def turn(t, q, g, pair, gp, r):
                    pe.wait_ge(rows_loaded[q], pair * 16 + 16)
                    at_least(pe, copied, t)
                    for a in range(A):
                        for c in range(DC):
                            at = q * A * D + a * D + c * P
                            last = nc.tensor.transpose(ps[0][:, c * GROUP + a * P:c * GROUP + (a + 1) * P],
                                                       rows[:, at:at + P], ident)
                    last.then_inc(turned, 1)

                def hidden(t, q, g, j):
                    at_least(pe, hid_set, t * PAIRS + j - 2)
                    for i in range(2):
                        f = 2 * j + i
                        for c in range(DC):
                            at = (g * DC + c) * F + f * P
                            last = nc.tensor.matmul(ps[1 + j % 3][:, i * GROUP:(i + 1) * GROUP], w1s[:, at:at + P],
                                                    rowsT[:, (q * DC + c) * GROUP:(q * DC + c + 1) * GROUP],
                                                    start=(c == 0), stop=(c == DC - 1))
                    last.then_inc(hid_made, 1)

                def result(t, q, g, j):
                    pe.wait_ge(hid_set, t * PAIRS + j + 1)
                    for f in (2 * j, 2 * j + 1):
                        for a in range(A):
                            at = f * GROUP + a * P
                            last = nc.tensor.matmul(ps[4 + 2 * q + a][:, 0:D], hid[:, at:at + P],
                                                    w2s[:, (g * FC + f) * D:(g * FC + f + 1) * D],
                                                    start=(f == 0), stop=(f == FC - 1))
                    return last

                def first(t, q, g, pair, gp, r):
                    if r % sub == 0:
                        pe.wait_ge(weights_loaded[g], (gp + 1) * (48 if biased else 32))
                    pe.wait_ge(copied, t + 1)
                    hidden(t, q, g, 0)
                    hidden(t, q, g, 1)
                    at_least(pe, res_set, (t - 1) * A)
                    for j in range(PAIRS - 1):
                        result(t, q, g, j)
                        if j + 2 < PAIRS:
                            hidden(t, q, g, j + 2)

                def last_pair(t, q, g, pair, gp, r):
                    result(t, q, g, PAIRS - 1).then_inc(res_made, 1)
                over(pe, [(1, first), (0, turn), (1, last_pair)])

            @block.scalar
            def _(act):
                def copy(t, q, g, pair, gp, r):
                    act.wait_ge(turned, t + 1)
                    at_least(act, hid_made, (t - 1) * PAIRS)
                    nc.scalar.activation(rowsT[:, q * DC * GROUP:(q + 1) * DC * GROUP], ps[0][:, :],
                                         ACT.Copy).then_inc(copied, 1)

                def gelu(t, q, g, pair, gp, r):
                    if biased and r % sub == 0:
                        at_least(act, hid_set, t * PAIRS)
                        nc.scalar.activation(b1[:, :], eb1[:, bass.ds((gp * 2 + g) * FC, FC)], ACT.Copy)\
                            .then_inc(b1_set, 1)
                        act.wait_ge(b1_set, gp * 2 + g + 1)
                    at_least(act, res_made, t)
                    for j in range(PAIRS):
                        act.wait_ge(hid_made, t * PAIRS + j + 1)
                        bank = ps[1 + j % 3]
                        if biased:
                            for i in range(2):
                                f = 2 * j + i
                                last = nc.scalar.activation(hid[:, f * GROUP:(f + 1) * GROUP],
                                                            bank[:, i * GROUP:(i + 1) * GROUP], func,
                                                            bias=b1[:, f:f + 1])
                        else:
                            last = nc.scalar.activation(hid[:, 2 * j * GROUP:2 * (j + 1) * GROUP], bank[:, :], func)
                        last.then_inc(hid_set, 1)
                def store(t, q, g, pair, gp, r):
                    act.wait_ge(res_set, t * A + A)
                    act.dma_start(k.d_rows_out[bass.ds(t * GROUP, GROUP), :].rearrange("(a p) d -> p a d", p=P),
                                   res[:, q * A * D:(q + 1) * A * D].rearrange("p (a d) -> p a d", d=D))\
                        .then_inc(res_stored[q], 16)
                over(act, [(2, store), (1, gelu), (0, copy)])
                act.wait_ge(res_stored[0], (tiles + 1) // 2 * 16)
                act.wait_ge(res_stored[1], tiles // 2 * 16)

            @block.vector
            def _(dve):
                def take(t, q, g, pair, gp, r):
                    dve.wait_ge(res_made, t + 1)
                    at_least(dve, res_stored[q], pair * 16)
                    for a in range(A):
                        to = res[:, (q * A + a) * D:(q * A + a + 1) * D]
                        if biased:
                            nc.vector.tensor_tensor(to, ps[4 + 2 * q + a][:, 0:D], b2[:, g * D:(g + 1) * D],
                                                    ALU.add).then_inc(res_set, 1)
                        else:
                            nc.vector.tensor_copy(to, ps[4 + 2 * q + a][:, 0:D]).then_inc(res_set, 1)
                over(dve, [(1, take)])


def collect(k, name, gate, used, also=None):
    nc, x = k.nc, k.x
    RING = 8
    with ExitStack() as ctx:
        sb, sem = stage_tools(ctx, k, name)
        got = sb("got", [P, RING * D])
        arrived = [sem(f"arrived{i}") for i in range(RING)]
        added = sem("added")
        also_vector, also_tensor = also(k, sb, sem) if also else (None, None)

        with nc.Block() as block:

            @block.tensor
            def _(pe):
                if also:
                    also_tensor(pe)

            @block.gpsimd
            def _(pool):
                for t in range(TILES):
                    r = t % RING
                    at_least(pool, added, t - RING + 1)
                    nc.gpsimd.indirect_dma_start(
                        out=got[:, r * D:(r + 1) * D], out_offset=None, in_=k.d_rows_out[0:used, :],
                        in_offset=bass.IndirectOffsetOnAxis(ap=k.pos[:, t:t + 1], axis=0)).then_inc(arrived[r], 16)

            @block.vector
            def _(dve):
                if also:
                    also_vector(dve)
                for t in range(TILES):
                    r = t % RING
                    dve.wait_ge(arrived[r], 16 * (t // RING + 1))
                    part = got[:, r * D:(r + 1) * D]
                    to = x[:, t * D:(t + 1) * D]
                    if gate is None:
                        nc.vector.tensor_tensor(to, part, to, ALU.add).then_inc(added, 1)
                    else:
                        nc.vector.scalar_tensor_tensor(to, part, gate[:, t:t + 1], to, ALU.mult,
                                                       ALU.add).then_inc(added, 1)


def layer0(k):
    with ExitStack() as ctx:
        rows = ctx.enter_context(k.nc.sbuf_tensor("rows0", [P, TILES * D], FP32))
        scores = ctx.enter_context(k.nc.sbuf_tensor("scores0", [P, EXPERTS * TILES], FP32))
        context_attention(k, rows, scores)
        balanced_assignment(k, scores)
        place(k, rows, "pl0", False)
    expert_ffn(k, "e0", k.d_w1a, k.d_w2a, ACT.Gelu_apprx_tanh, T // GROUP, 2, True)
    collect(k, "co0", None, T)



def route_top1(k, rows):
    nc, x, ps = k.nc, k.x, k.ps
    wr = k.part("wr").rearrange("p (c e) -> p c e", c=DC)
    onehot = k.onehot[:, :].rearrange("p (e t) -> p e t", t=TILES)
    with ExitStack() as ctx:
        sb, sem = stage_tools(ctx, k, "r1")
        ln = Norm(k, sb, sem, "ln")
        h, hT = sb("h", [P, 2 * D]), sb("hT", [P, 2 * D])
        logits, best = sb("logits", [P, TILES * EXPERTS]), sb("best", [P, TILES * 8])
        same, seen, lead = sb("same", [P, EXPERTS * TILES]), sb("seen", [P, TILES]), sb("lead", [P, TILES])
        flip = Flip(k, sem, "h", ps[0])
        kept, scored, logit_set = sem("kept"), sem("scored"), sem("logit_set")
        chain, led = sem("chain"), sem("led")

        with nc.Block() as block:

            @block.vector
            def _(dve):
                def stats(t, q, _):
                    ln.stats(dve, x[:, cols(t)], t, q)

                def apply(t, q, _):
                    at_least(dve, flip.turned, t - 1)
                    at_least(dve, kept, t - 1)
                    ln.apply(dve, h[:, q * D:(q + 1) * D], x[:, cols(t)], t, q)
                over_tiles(dve, lambda u: run_lagged(u, [(0, stats), (1, apply)]), 1)
                done = [0]

                def step(ins):
                    done[0] += 1
                    ins.then_inc(chain, 1)
                    dve.wait_ge(chain, done[0])
                dve.wait_ge(logit_set, TILES)
                for t in range(TILES):
                    last = nc.vector.max(best[:, t * 8:(t + 1) * 8], logits[:, t * EXPERTS:(t + 1) * EXPERTS])
                step(last)
                by_rank = best[:, :].rearrange("p (t r) -> p r t", r=8)
                nc.vector.tensor_tensor(lead[:, :], by_rank[:, 0, :], by_rank[:, 1, :], ALU.subtract).then_inc(led, 1)
                step(nc.vector.tensor_tensor(
                    same[:, :].rearrange("p (e t) -> p e t", t=TILES),
                    logits[:, :].rearrange("p (t e) -> p e t", e=EXPERTS),
                    by_rank[:, 0:1, :].to_broadcast([P, EXPERTS, TILES]), ALU.is_equal))
                step(nc.vector.memset(seen[:, :], 0.0))
                for e in range(EXPERTS):
                    mine = same[:, e * TILES:(e + 1) * TILES]
                    step(nc.vector.tensor_tensor(onehot[:, e, :], mine, seen[:, :], ALU.is_gt))
                    step(nc.vector.tensor_tensor(seen[:, :], seen[:, :], mine, ALU.max))

            @block.gpsimd
            def _(pool):
                over_tiles(pool, lambda u: run_lagged(u, [(0, lambda t, q, _: ln.power(pool, t, q))]), 0)

            @block.scalar
            def _(act):
                def keep(t, q, _):
                    act.wait_ge(ln.done, t + 1)
                    nc.scalar.activation(rows[:, cols(t)], h[:, q * D:(q + 1) * D], ACT.Copy).then_inc(kept, 1)

                def copy(t, q, _):
                    at_least(act, scored, t - 1)
                    flip.copy(act, hT[:, q * D:(q + 1) * D], t)

                def set_logits(t, q, _):
                    act.wait_ge(scored, t + 1)
                    nc.scalar.activation(logits[:, cols(t, EXPERTS)], ps[2 + q][:, 0:EXPERTS],
                                         ACT.Copy).then_inc(logit_set, 1)
                over_tiles(act, lambda u: run_lagged(u, [(2, copy), (5, set_logits), (1, keep)]), 5)
                act.wait_ge(led, 1)
                nc.scalar.activation(k.gate1[:, :], lead[:, :], ACT.Sigmoid)

            @block.tensor
            def _(pe):
                def turn(t, q, _):
                    pe.wait_ge(ln.done, t + 1)
                    flip.turn(pe, lambda c: h[:, q * D + c * P:q * D + (c + 1) * P], t)

                def score(t, q, _):
                    pe.wait_ge(flip.copied, t + 1)
                    at_least(pe, logit_set, t - 1)
                    for c in range(DC):
                        last = nc.tensor.matmul(ps[2 + q][:, 0:EXPERTS], hT[:, q * D + c * P:q * D + (c + 1) * P],
                                                wr[:, c, :], start=(c == 0), stop=(c == DC - 1))
                    last.then_inc(scored, 1)
                over_tiles(pe, lambda u: run_lagged(u, [(4, score), (2, turn)]), 4)


def layer1_ffn(k):
    with ExitStack() as ctx:
        rows = ctx.enter_context(k.nc.sbuf_tensor("rows1", [P, TILES * D], FP32))
        route_top1(k, rows)
        place(k, rows, "pl1", True)
    expert_ffn(k, "e1", k.d_w1b, k.d_w2b, ACT.Gelu, SORTED // GROUP, 1, False)
    collect(k, "co1", k.gate1, SORTED, also=ternary_weights)



DIAGONAL_LAG = 5


def diagonal_attention(k, sb, sem, y):
    nc, x, ps = k.nc, k.x, k.ps
    part = lambda n: part_of(SEC2, k.sec2, n).rearrange("p (c o) -> p c o", c=DC)
    row = lambda n: part_of(ROWS, k.rows, n)
    vs, os = part("vs"), part("os")
    bv = k.part("bvs2")
    pre, post = Norm(k, sb, sem, "pre"), Norm(k, sb, sem, "post")
    h, hT, vT = sb("dh", [P, 2 * D]), sb("dhT", [P, 2 * D]), sb("dvT", [P, 2 * D])
    z = sb("dz", [P, 2 * D])
    flip, v_bank = Flip(k, sem, "dh", ps[1]), ps[1][:, D:2 * D]
    out_bank = [ps[3 + 2 * q][:, 0:D] for q in range(2)]
    v_made, v_set = sem("v_made"), sem("v_set")
    projected = sem("d_projected")
    biased, added = sem("d_biased"), sem("d_added")
    affine = sem("affine")

    def vector(dve):
        def stats(t, q, _):
            pre.stats(dve, x[:, cols(t)], t, q)

        def apply(t, q, _):
            at_least(dve, flip.turned, t - 1)
            at_least(dve, biased, t - 1)
            pre.apply(dve, h[:, q * D:(q + 1) * D], x[:, cols(t)], t, q)

        def bias(t, q, _):
            dve.wait_ge(pre.done, t + 1)
            nc.vector.tensor_tensor(y[:, cols(t)], h[:, q * D:(q + 1) * D], row("bos2"), ALU.add).then_inc(biased, 1)

        def add(t, q, _):
            dve.wait_ge(projected, t + 1)
            dve.wait_ge(biased, t + 1)
            nc.vector.tensor_tensor(y[:, cols(t)], out_bank[q], y[:, cols(t)], ALU.add).then_inc(added, 1)
            wait_apart(nc, dve, added, t + 1, k.spare)
            post.stats(dve, y[:, cols(t)], t, q)

        def apply_post(t, q, _):
            at_least(dve, affine, t * 2 - 2)
            post.apply(dve, z[:, q * D:(q + 1) * D], y[:, cols(t)], t, q)
        return [(1, apply), (4, apply_post)], [(0, stats), (1, bias), (2, add)]

    def gpsimd(pool):
        def scale(t, q, _):
            part = z[:, q * D:(q + 1) * D]
            pool.wait_ge(post.done, t + 1)
            nc.gpsimd.tensor_tensor(part, part, row("g1"), ALU.mult).then_inc(affine, 1)
            pool.wait_ge(affine, t * 2 + 1)
            nc.gpsimd.tensor_tensor(y[:, cols(t)], part, row("b1"), ALU.add).then_inc(affine, 1)
        return [(5, scale), (0, lambda t, q, _: pre.power(pool, t, q)), (3, lambda t, q, _: post.power(pool, t, q))]

    def scalar(act):
        def copy(t, q, _):
            at_least(act, v_made, t - 1)
            flip.copy(act, hT[:, q * D:(q + 1) * D], t)

        def set_v(t, q, _):
            act.wait_ge(v_made, t + 1)
            at_least(act, projected, t - 1)
            for m in range(DC):
                nc.scalar.activation(vT[:, q * D + m * P:q * D + (m + 1) * P], v_bank[:, m * P:(m + 1) * P],
                                     ACT.Identity, bias=bv[:, m:m + 1]).then_inc(v_set, 1)
        return [(1, copy)], [(1, set_v)]

    def tensor(pe):
        def project(t, q, _):
            pe.wait_ge(v_set, t * 2 + 2)
            at_least(pe, added, t - 1)
            for c in range(DC):
                last = nc.tensor.matmul(out_bank[q], vT[:, q * D + c * P:q * D + (c + 1) * P], os[:, c, :],
                                        start=(c == 0), stop=(c == DC - 1))
            last.then_inc(projected, 1)

        def turn(t, q, _):
            pe.wait_ge(pre.done, t + 1)
            at_least(pe, v_set, t * 2)
            flip.turn(pe, lambda c: h[:, q * D + c * P:q * D + (c + 1) * P], t)

        def values(t, q, _):
            pe.wait_ge(flip.copied, t + 1)
            for m in range(DC):
                for c in range(DC):
                    last = nc.tensor.matmul(v_bank[:, m * P:(m + 1) * P], vs[:, c, m * P:(m + 1) * P],
                                            hT[:, q * D + c * P:q * D + (c + 1) * P],
                                            start=(c == 0), stop=(c == DC - 1))
            last.then_inc(v_made, 1)
        return [(1, turn)], [(1, values), (2, project)]
    return vector, gpsimd, scalar, tensor, affine


def feed_forward(k, y, peak):
    nc, x, ps = k.nc, k.x, k.ps
    row = lambda n: part_of(ROWS, k.rows, n)
    lin1 = part_of(SEC2, k.sec2, "lin1").rearrange("p (c f) -> p c f", c=DC)
    lin2 = part_of(SEC2, k.sec2, "lin2").rearrange("p (f d) -> p f d", f=FC)
    b1 = k.part("lin1_b")
    HALF = FC // 2
    with ExitStack() as ctx:
        sb, sem = stage_tools(ctx, k, "ff")
        pre, post = Norm(k, sb, sem, "pre"), Norm(k, sb, sem, "post")
        h, hT, hid = sb("h", [P, 2 * D]), sb("hT", [P, 2 * D]), sb("hid", [P, 2 * F])
        z = sb("z", [P, 2 * D])
        flip = Flip(k, sem, "h", ps[0])
        affine = sem("affine")
        biased = sem("biased")
        hid_made = sem("hid_made")
        act_set, dve_set = sem("act_set"), sem("dve_set")
        projected, added = sem("projected"), sem("added")
        affine3 = sem("affine3")
        x_added = sem("x_added")
        outer, inner, n = Norm(k, sb, sem, "outer"), Norm(k, sb, sem, "inner"), sb("n", [P, 2 * D])
        affine_n = sem("affine_n")
        peaked = sem("peaked")

        with nc.Block() as block:

            @block.vector
            def _(dve):
                def stats(t, q, _):
                    pre.stats(dve, y[:, cols(t)], t, q)

                def apply(t, q, _):
                    at_least(dve, flip.turned, t - 1)
                    at_least(dve, biased, t - 1)
                    pre.apply(dve, h[:, q * D:(q + 1) * D], y[:, cols(t)], t, q)

                def hidden(t, q, _):
                    dve.wait_ge(hid_made, t * 2 + 2)
                    at_least(dve, projected, t - 1)
                    for j in range(HALF):
                        f = HALF + j
                        last = nc.vector.tensor_scalar(hid[:, q * F + f * P:q * F + (f + 1) * P], ps[2][:, j * P:(j + 1) * P],
                                                       b1[:, f:f + 1], 0.0, ALU.add, ALU.max)
                    last.then_inc(dve_set, 1)

                def add(t, q, _):
                    dve.wait_ge(projected, t + 1)
                    dve.wait_ge(biased, t + 1)
                    nc.vector.tensor_tensor(y[:, cols(t)], ps[3 + q][:, 0:D], y[:, cols(t)], ALU.add).then_inc(added, 1)
                    wait_apart(nc, dve, added, t + 1, k.spare)
                    post.stats(dve, y[:, cols(t)], t, q)

                def apply_post(t, q, _):
                    at_least(dve, x_added, t - 1)
                    post.apply(dve, z[:, q * D:(q + 1) * D], y[:, cols(t)], t, q)

                def bias(t, q, _):
                    dve.wait_ge(affine, t * 2 + 2)
                    nc.vector.tensor_tensor(y[:, cols(t)], h[:, q * D:(q + 1) * D], row("lin2_b"), ALU.add)\
                        .then_inc(biased, 1)

                def add_x(t, q, _):
                    dve.wait_ge(affine3, t * 2 + 2)
                    nc.vector.tensor_tensor(x[:, cols(t)], z[:, q * D:(q + 1) * D], x[:, cols(t)], ALU.add)\
                        .then_inc(x_added, 1)

                def outer_stats(t, q, _):
                    wait_apart(nc, dve, x_added, t + 1, k.spare)
                    outer.stats(dve, x[:, cols(t)], t, q)

                def outer_apply(t, q, _):
                    outer.apply(dve, y[:, cols(t)], x[:, cols(t)], t, q)
                    wait_apart(nc, dve, outer.done, t + 1, k.spare)
                    inner.stats(dve, y[:, cols(t)], t, q)

                def inner_apply(t, q, _):
                    at_least(dve, affine_n, t * 2 - 2)
                    inner.apply(dve, n[:, q * D:(q + 1) * D], y[:, cols(t)], t, q)

                def peak_of(t, q, _):
                    dve.wait_ge(affine_n, t * 2 + 2)
                    nc.vector.tensor_reduce(peak[:, bass.ds(t, 1)], y[:, cols(t)], AX, ALU.max,
                                            apply_absolute_value=True).then_inc(peaked, 1)
                over_tiles(dve, lambda u: run_lagged(u, [(1, apply), (0, stats), (5, apply_post), (9, inner_apply),
                                                         (2, hidden), (2, bias), (7, outer_apply), (6, add_x),
                                                         (6, outer_stats), (10, peak_of), (3, add)]), 10)

            @block.gpsimd
            def _(pool):
                def scale(t, q, _):
                    part = h[:, q * D:(q + 1) * D]
                    pool.wait_ge(pre.done, t + 1)
                    nc.gpsimd.tensor_tensor(part, part, row("g2"), ALU.mult).then_inc(affine, 1)
                    pool.wait_ge(affine, t * 2 + 1)
                    nc.gpsimd.tensor_tensor(part, part, row("b2"), ALU.add).then_inc(affine, 1)

                def finish(t, q, _):
                    part = z[:, q * D:(q + 1) * D]
                    pool.wait_ge(post.done, t + 1)
                    nc.gpsimd.tensor_tensor(part, part, row("g3"), ALU.mult).then_inc(affine3, 1)
                    pool.wait_ge(affine3, t * 2 + 1)
                    nc.gpsimd.tensor_tensor(part, part, row("b3"), ALU.add).then_inc(affine3, 1)

                def affine_of(t, q, _):
                    part = n[:, q * D:(q + 1) * D]
                    pool.wait_ge(inner.done, t + 1)
                    nc.gpsimd.tensor_tensor(part, part, row("gamma"), ALU.mult).then_inc(affine_n, 1)
                    pool.wait_ge(affine_n, t * 2 + 1)
                    nc.gpsimd.tensor_tensor(y[:, cols(t)], part, row("beta"), ALU.add).then_inc(affine_n, 1)
                over_tiles(pool, lambda u: run_lagged(u, [(1, scale), (0, lambda t, q, _: pre.power(pool, t, q)),
                                                          (5, finish), (4, lambda t, q, _: post.power(pool, t, q)),
                                                          (8, lambda t, q, _: inner.power(pool, t, q)), (9, affine_of),
                                                          (6, lambda t, q, _: outer.power(pool, t, q))]), 9)

            @block.scalar
            def _(act):
                def copy(t, q, _):
                    at_least(act, hid_made, t * 2 - 2)
                    flip.copy(act, hT[:, q * D:(q + 1) * D], t)

                def hidden(t, q, _):
                    act.wait_ge(hid_made, t * 2 + 1)
                    at_least(act, projected, t - 1)
                    for f in range(HALF):
                        last = nc.scalar.activation(hid[:, q * F + f * P:q * F + (f + 1) * P], ps[1][:, f * P:(f + 1) * P],
                                                    ACT.Relu, bias=b1[:, f:f + 1])
                    last.then_inc(act_set, 1)
                over_tiles(act, lambda u: run_lagged(u, [(1, copy), (2, hidden)]), 2)

            @block.tensor
            def _(pe):
                def turn(t, q, _):
                    pe.wait_ge(affine, t * 2 + 2)
                    flip.turn(pe, lambda c: h[:, q * D + c * P:q * D + (c + 1) * P], t)

                def hidden(t, q, _):
                    pe.wait_ge(flip.copied, t + 1)
                    for half, read in ((0, act_set), (1, dve_set)):
                        at_least(pe, read, t)
                        for j in range(HALF):
                            f = half * HALF + j
                            for c in range(DC):
                                last = nc.tensor.matmul(ps[1 + half][:, j * P:(j + 1) * P], lin1[:, c, f * P:(f + 1) * P],
                                                        hT[:, q * D + c * P:q * D + (c + 1) * P],
                                                        start=(c == 0), stop=(c == DC - 1))
                        last.then_inc(hid_made, 1)

                def project(t, q, _):
                    at_least(pe, added, t - 1)
                    for f in range(FC):
                        if f % HALF == 0:
                            pe.wait_ge((act_set, dve_set)[f // HALF], t + 1)
                        last = nc.tensor.matmul(ps[3 + q][:, 0:D], hid[:, q * F + f * P:q * F + (f + 1) * P], lin2[:, f, :],
                                                start=(f == 0), stop=(f == FC - 1))
                    last.then_inc(projected, 1)
                over_tiles(pe, lambda u: run_lagged(u, [(2, hidden), (1, turn), (3, project)]), 3)



def ternary_weights(k, sb, sem):
    nc, ps = k.nc, k.ps
    w = part_of(SEC2, k.sec2, "tern")
    absw, keep, sign = sb("absw", [P, DC * D]), sb("keep", [P, DC * D]), sb("sign", [P, DC * D])
    sums, delta = sb("sums", [P, 2]), sb("delta", [P, 1])
    chain, asked, given = sem("chain"), sem("asked"), sem("given")

    def vector(dve):
        done = [0]

        def step(ins):
            done[0] += 1
            ins.then_inc(chain, 1)
            dve.wait_ge(chain, done[0])
        step(nc.vector.tensor_scalar(absw[:, :], w, -1.0, None, ALU.mult))
        step(nc.vector.tensor_tensor(absw[:, :], absw[:, :], w, ALU.max))
        nc.vector.tensor_reduce(sums[:, 0:1], absw[:, :], AX, ALU.add).then_inc(asked, 1)
        dve.wait_ge(given, 1)
        step(nc.vector.tensor_scalar(delta[:, :], ps[0][:, 0:1], 1.0 / (D * D), 0.7, ALU.mult, ALU.mult))
        step(nc.vector.tensor_scalar(keep[:, :], absw[:, :], delta[:, :], None, ALU.is_gt))
        step(nc.vector.tensor_tensor(absw[:, :], absw[:, :], keep[:, :], ALU.mult))
        step(nc.vector.tensor_reduce(sums[:, 0:1], absw[:, :], AX, ALU.add))
        nc.vector.tensor_reduce(sums[:, 1:2], keep[:, :], AX, ALU.add).then_inc(asked, 1)
        step(nc.vector.tensor_scalar(sign[:, :], w, 0.0, None, ALU.is_gt))
        step(nc.vector.tensor_scalar(absw[:, :], w, 0.0, None, ALU.is_lt))
        step(nc.vector.tensor_tensor(sign[:, :], sign[:, :], absw[:, :], ALU.subtract))
        step(nc.vector.tensor_tensor(k.tern[:, :], sign[:, :], keep[:, :], ALU.mult))
        dve.wait_ge(given, 2)
        step(nc.vector.tensor_scalar(k.alpha[:, :], ps[0][:, 1:2], 1.0, None, ALU.max))
        step(nc.vector.reciprocal(k.alpha[:, :], k.alpha[:, :]))
        step(nc.vector.tensor_tensor(k.alpha[:, :], k.alpha[:, :], ps[0][:, 0:1], ALU.mult))

    def tensor(pe):
        pe.wait_ge(asked, 1)
        nc.tensor.matmul(ps[0][:, 0:1], k.ones[:, :], sums[:, 0:1], start=True, stop=True).then_inc(given, 1)
        pe.wait_ge(asked, 2)
        nc.tensor.matmul(ps[0][:, 0:2], k.ones[:, :], sums[:, :], start=True, stop=True).then_inc(given, 1)
    return vector, tensor



def quantised_product(k, n_all, peak):
    nc, x, ps = k.nc, k.x, k.ps
    MAGIC = 1.5 * 2 ** 23
    QMAX = 127.0
    with ExitStack() as ctx:
        sb, sem = stage_tools(ctx, k, "qp")
        top, topT, scale = sb("top", [P, P]), sb("topT", [P, 1]), sb("scale", [P, 1])
        inv, out_scale = sb("inv", [P, 1]), sb("out_scale", [P, 1])
        chain = sem("chain")
        asked, given = sem("asked"), sem("given")
        with nc.Block() as block:

            @block.vector
            def _(dve):
                done = [0]

                def step(ins):
                    done[0] += 1
                    ins.then_inc(chain, 1)
                    dve.wait_ge(chain, done[0])
                step(nc.vector.tensor_reduce(topT[:, :], peak[:, :], AX, ALU.max))
                nc.vector.tensor_copy(top[:, :], topT[:, :].to_broadcast([P, P])).then_inc(asked, 1)
                dve.wait_ge(given, 1)
                step(nc.vector.tensor_reduce(scale[:, :], ps[1][:, 0:P], AX, ALU.max))
                step(nc.vector.tensor_scalar(scale[:, :], scale[:, :], 1e-8, 1.0 / QMAX, ALU.max, ALU.mult))
                step(nc.vector.reciprocal(inv[:, :], scale[:, :]))
                step(nc.vector.tensor_tensor(out_scale[:, :], scale[:, :], k.alpha[:, :], ALU.mult))

            @block.tensor
            def _(pe):
                pe.wait_ge(asked, 1)
                nc.tensor.transpose(ps[1][:, 0:P], top[:, :], k.ident).then_inc(given, 1)

        n, whole = sb("n", [P, 2 * D]), sb("whole", [P, 2 * D], BF16)
        wholeT = sb("wholeT", [P, 2 * D], BF16)
        rounded = sem("rounded")
        turned, copied, made, added = sem("turned"), sem("copied"), sem("made"), sem("added")
        turned_bank = ps[0][:, 0:P].bitcast(BF16)
        with nc.Block() as block:

            @block.vector
            def _(dve):
                def quantise(t, q, _):
                    part = n[:, q * D:(q + 1) * D]
                    at_least(dve, rounded, t * 3 - 3)
                    nc.vector.tensor_scalar(part, n_all[:, cols(t)], inv[:, :], MAGIC, ALU.mult, ALU.add).then_inc(rounded, 1)
                    dve.wait_ge(rounded, t * 3 + 1)
                    nc.vector.tensor_scalar(part, part, MAGIC + QMAX, MAGIC - QMAX, ALU.min, ALU.max).then_inc(rounded, 1)
                    dve.wait_ge(rounded, t * 3 + 2)
                    at_least(dve, turned, t - 1)
                    nc.vector.tensor_scalar(whole[:, q * D:(q + 1) * D], part, -MAGIC, None, ALU.add).then_inc(rounded, 1)

                def add(t, q, _):
                    dve.wait_ge(made, t + 1)
                    nc.vector.scalar_tensor_tensor(x[:, cols(t)], ps[1 + q][:, 0:D], out_scale[:, :], x[:, cols(t)],
                                                   ALU.mult, ALU.add).then_inc(added, 1)
                over_tiles(dve, lambda u: run_lagged(u, [(2, add), (0, quantise)]), 2)

            @block.scalar
            def _(act):
                def copy(t, q, _):
                    act.wait_ge(turned, t + 1)
                    at_least(act, made, t - 1)
                    nc.scalar.activation(wholeT[:, q * D:(q + 1) * D], turned_bank, ACT.Copy).then_inc(copied, 1)
                over_tiles(act, lambda u: run_lagged(u, [(0, copy)]), 0)

            @block.tensor
            def _(pe):
                def turn(t, q, _):
                    pe.wait_ge(rounded, t * 3 + 3)
                    at_least(pe, copied, t)
                    for c in range(DC):
                        last = nc.tensor.transpose(turned_bank[:, c * P:(c + 1) * P],
                                                   whole[:, q * D + c * P:q * D + (c + 1) * P], k.ident16[:, :])
                    last.then_inc(turned, 1)

                def product(t, q, _):
                    pe.wait_ge(copied, t + 1)
                    at_least(pe, added, t - 1)
                    for c in range(DC):
                        last = nc.tensor.matmul(ps[1 + q][:, 0:D], wholeT[:, q * D + c * P:q * D + (c + 1) * P],
                                                k.tern[:, c * D:(c + 1) * D], start=(c == 0), stop=(c == DC - 1))
                    last.then_inc(made, 1)
                over_tiles(pe, lambda u: run_lagged(u, [(0, turn), (0, product)]), 0)


def layer2(k):
    with ExitStack() as ctx:
        y = ctx.enter_context(k.nc.sbuf_tensor("y2", [P, TILES * D], FP32))
        head_attention(k, "h2", 8, SEC2, k.sec2, "bq2", "bk2", "bv2", "bo2", y, False,
                       ahead=diagonal_attention, loads=[(k.secA[:, :], k.d_sec3)])
        peak = ctx.enter_context(k.nc.sbuf_tensor("peak", [P, TILES], FP32))
        feed_forward(k, y, peak)
        quantised_product(k, y, peak)



def gated_experts(k):
    nc, x, ps, ident = k.nc, k.x, k.ps, k.ident
    part3 = lambda n, c: part_of(SEC3, k.secA, n).rearrange("p (c o) -> p c o", c=c)
    part65 = lambda n: part_of(SEC65, k.sec65, n)
    row = lambda n: part_of(ROWS, k.rows, n)
    enc, s2c, we2, dec = part3("enc", DC), part3("s2c", 4), part3("we2", 16), part3("dec", 4)
    rw1, rw2, we1, c2s = part65("rw1"), part65("rw2"), part65("we1"), part65("c2s")
    enc_b, s2c_b = k.part("enc_b"), k.part("s2c_b")
    M, H, HC = 64, 512, 4
    E = EXPERTS
    EC = E * 2
    with ExitStack() as ctx:
        sb, sem = stage_tools(ctx, k, "ge")
        pre, post = Norm(k, sb, sem, "pre"), Norm(k, sb, sem, "post")
        h, hT = sb("h", [P, 2 * D]), sb("hT", [P, 2 * D])
        encT, contT, routeT = sb("encT", [P, 2 * H]), sb("contT", [M + 1, 2 * P]), sb("routeT", [M + 1, 2 * P])
        logits, best, lead, z = sb("logits", [P, E]), sb("best", [P, 8]), sb("lead", [P, E]), sb("z", [P, 2 * E])
        higher, same, rank = sb("higher", [P, E * E]), sb("same", [P, E * E]), sb("rank", [P, 2 * E])
        gate = sb("gate", [P, 2 * E])
        hid = sb("hid", [P, EC * P])
        outs, moe = sb("outs", [P, E * M]), sb("moe", [P, 2 * P])
        moeT, spikeT = sb("moeT", [M + 1, 2 * P]), sb("spikeT", [P, 2 * H])
        decoded, res = sb("decoded", [P, 2 * D]), sb("res", [P, 2 * D])
        flip = Flip(k, sem, "h", ps[0])
        ready = sem("ready")
        enc_made, enc_set = sem("enc_made"), sem("enc_set")
        cont_made, cont_set = sem("cont_made"), sem("cont_set")
        route_made, route_set = sem("route_made"), sem("route_set")
        logit_made = sem("logit_made")
        gating = sem("gating")
        z_sig = sem("z_sig")
        hid_made, hid_set = sem("hid_made"), sem("hid_set")
        outs_made = sem("outs_made")
        combined = sem("combined")
        moe_turned, moe_copied = sem("moe_turned"), sem("moe_copied")
        spike_made, spike_set = sem("spike_made"), sem("spike_set")
        dec_made, dec_biased, dec_set = sem("dec_made"), sem("dec_biased"), sem("dec_set")
        finished = sem("finished")
        stored = sem("stored")
        GATING = 11

        with nc.Block() as block:

            @block.sync
            def _(sp):
                CHUNKS = 8
                n = TILES // CHUNKS
                for c in range(CHUNKS):
                    sp.wait_ge(finished, (c + 1) * n * 3)
                    sp.dma_start(k.d_out[c * n * P:(c + 1) * n * P, :].rearrange("(t p) d -> p t d", p=P),
                                 x[:, c * n * D:(c + 1) * n * D].rearrange("p (t d) -> p t d", d=D)).then_inc(stored, 16)
                sp.wait_ge(stored, 16 * CHUNKS)

            @block.tensor
            def _(pe):
                pe.wait_ge(ready, 4)

                def turn(t, q, _):
                    pe.wait_ge(pre.done, t + 1)
                    flip.turn(pe, lambda c: h[:, q * D + c * P:q * D + (c + 1) * P], t)

                def encode(t, q, _):
                    pe.wait_ge(flip.copied, t + 1)
                    at_least(pe, enc_set, t * HC)
                    for m in range(HC):
                        for c in range(DC):
                            last = nc.tensor.matmul(ps[1][:, m * P:(m + 1) * P], enc[:, c, m * P:(m + 1) * P],
                                                    hT[:, q * D + c * P:q * D + (c + 1) * P],
                                                    start=(c == 0), stop=(c == DC - 1))
                    last.then_inc(enc_made, 1)

                def condense(t, q, _):
                    pe.wait_ge(enc_set, t * HC + HC)
                    at_least(pe, gating, (t - 1) * GATING + 1)
                    for m in range(HC):
                        last = nc.tensor.matmul(ps[2][0:M, 0:P], s2c[:, m, :], encT[:, q * H + m * P:q * H + (m + 1) * P],
                                                start=(m == 0), stop=(m == HC - 1))
                    last.then_inc(cont_made, 1)

                def route(t, q, _):
                    pe.wait_ge(cont_set, t + 1)
                    nc.tensor.matmul(ps[2][0:M, P:2 * P], rw1, contT[:, q * P:(q + 1) * P], start=True,
                                     stop=True).then_inc(route_made, 1)

                def score(t, q, _):
                    pe.wait_ge(route_set, t + 1)
                    nc.tensor.matmul(ps[2][:, 2 * P:2 * P + E], routeT[:, q * P:(q + 1) * P], rw2, start=True,
                                     stop=True).then_inc(logit_made, 1)

                def hidden(t, q, j):
                    at_least(pe, hid_set, t * 4 + j - 1)
                    for i in range(4):
                        f = 4 * j + i
                        last = nc.tensor.matmul(ps[3 + j % 2][:, i * P:(i + 1) * P], we1[:, f * P:(f + 1) * P],
                                                contT[:, q * P:(q + 1) * P], start=True, stop=True)
                    last.then_inc(hid_made, 1)

                def out(t, q, j):
                    pe.wait_ge(hid_set, t * 4 + j + 1)
                    if j == 0:
                        at_least(pe, combined, (t - 1) * 3 + 1)
                    for e in (2 * j, 2 * j + 1):
                        for i in range(2):
                            f = 2 * e + i
                            last = nc.tensor.matmul(ps[5][:, e * M:(e + 1) * M], hid[:, f * P:(f + 1) * P], we2[:, f, :],
                                                    start=(i == 0), stop=(i == 1))
                    return last

                def experts(t, q, _):
                    hidden(t, q, 0)
                    hidden(t, q, 1)
                    for j in range(4):
                        last = out(t, q, j)
                        if j < 2:
                            hidden(t, q, j + 2)
                    last.then_inc(outs_made, 1)

                def turn_moe(t, q, _):
                    pe.wait_ge(combined, t * 3 + 3)
                    at_least(pe, dec_biased, t)
                    nc.tensor.transpose(ps[7][:, 0:P], moe[:, q * P:(q + 1) * P], ident).then_inc(moe_turned, 1)

                def spike(t, q, _):
                    pe.wait_ge(moe_copied, t + 1)
                    at_least(pe, spike_set, t)
                    for m in range(HC):
                        last = nc.tensor.matmul(ps[6][:, m * P:(m + 1) * P], c2s[:, m * P:(m + 1) * P],
                                                moeT[:, q * P:(q + 1) * P], start=True, stop=True)
                    last.then_inc(spike_made, 1)

                def decode(t, q, _):
                    pe.wait_ge(spike_set, t + 1)
                    for m in range(HC):
                        last = nc.tensor.matmul(ps[7][:, D:2 * D], spikeT[:, q * H + m * P:q * H + (m + 1) * P], dec[:, m, :],
                                                start=(m == 0), stop=(m == HC - 1))
                    last.then_inc(dec_made, 1)
                over_tiles(pe, lambda u: run_lagged(u, [(3, experts), (4, turn_moe), (1, turn), (2, condense), (4, spike),
                                                        (1, encode), (2, route), (4, decode), (2, score)]), 4)

            @block.scalar
            def _(act):
                def copy(t, q, _):
                    at_least(act, enc_made, t - 1)
                    flip.copy(act, hT[:, q * D:(q + 1) * D], t)

                def set_enc(t, q, _):
                    act.wait_ge(enc_made, t + 1)
                    at_least(act, cont_made, t - 1)
                    for m in range(HC):
                        nc.scalar.activation(encT[:, q * H + m * P:q * H + (m + 1) * P], ps[1][:, m * P:(m + 1) * P],
                                             ACT.Sigmoid, bias=enc_b[:, m:m + 1]).then_inc(enc_set, 1)

                def set_cont(t, q, _):
                    act.wait_ge(cont_made, t + 1)
                    at_least(act, outs_made, t - 1)
                    nc.scalar.activation(contT[0:M, q * P:(q + 1) * P], ps[2][0:M, 0:P], ACT.Identity,
                                         bias=s2c_b[0:M, :]).then_inc(cont_set, 1)

                def set_route(t, q, _):
                    act.wait_ge(route_made, t + 1)
                    at_least(act, logit_made, t - 1)
                    nc.scalar.activation(routeT[0:M, q * P:(q + 1) * P], ps[2][0:M, P:2 * P], ACT.Tanh).then_inc(route_set, 1)

                def gate_sig(t, q, _):
                    act.wait_ge(gating, t * GATING + 5)
                    nc.scalar.activation(z[:, q * E:(q + 1) * E], z[:, q * E:(q + 1) * E], ACT.Sigmoid).then_inc(z_sig, 1)

                def hidden(t, q, _):
                    at_least(act, outs_made, t)
                    for j in range(4):
                        act.wait_ge(hid_made, t * 4 + j + 1)
                        nc.scalar.activation(hid[:, 4 * j * P:4 * (j + 1) * P], ps[3 + j % 2][:, :], ACT.Relu).then_inc(hid_set, 1)

                def copy_moe(t, q, _):
                    act.wait_ge(moe_turned, t + 1)
                    at_least(act, spike_made, t - 1)
                    nc.scalar.activation(moeT[0:M, q * P:(q + 1) * P], ps[7][0:M, 0:P], ACT.Copy).then_inc(moe_copied, 1)

                def set_spike(t, q, _):
                    act.wait_ge(spike_made, t + 1)
                    at_least(act, dec_made, t - 1)
                    nc.scalar.activation(spikeT[:, q * H:(q + 1) * H], ps[6][:, :], ACT.Sigmoid).then_inc(spike_set, 1)

                def set_dec(t, q, _):
                    act.wait_ge(dec_biased, t + 1)
                    nc.scalar.activation(decoded[:, q * D:(q + 1) * D], decoded[:, q * D:(q + 1) * D],
                                         ACT.Sigmoid).then_inc(dec_set, 1)
                over_tiles(act, lambda u: run_lagged(u, [(5, set_dec), (3, hidden), (3, gate_sig), (4, copy_moe), (1, copy),
                                                         (2, set_cont), (4, set_spike), (2, set_route), (1, set_enc)]), 5)

            @block.vector
            def _(dve):
                nc.vector.memset(contT[M:M + 1, :], 1.0).then_inc(ready, 1)
                nc.vector.memset(routeT[M:M + 1, :], 1.0).then_inc(ready, 1)
                nc.vector.memset(moeT[M:M + 1, :], 1.0).then_inc(ready, 1)
                nc.vector.memset(moe[:, :], 0.0).then_inc(ready, 1)
                dve.wait_ge(ready, 4)

                def stats(t, q, _):
                    pre.stats(dve, x[:, cols(t)], t, q)

                def apply(t, q, _):
                    at_least(dve, flip.turned, t - 1)
                    pre.apply(dve, h[:, q * D:(q + 1) * D], x[:, cols(t)], t, q)

                def gates(t, q, _):
                    def step(ins, n):
                        ins.then_inc(gating, 1)
                        dve.wait_ge(gating, t * GATING + n)
                    zt = z[:, q * E:(q + 1) * E]
                    square = lambda a: a[:, :].rearrange("p (e f) -> p e f", f=E)
                    mine = logits[:, :].unsqueeze(2).to_broadcast([P, E, E])
                    other = logits[:, :].unsqueeze(1).to_broadcast([P, E, E])
                    at_least(dve, gating, t * GATING)
                    dve.wait_ge(logit_made, t + 1)
                    step(nc.vector.tensor_copy(logits[:, :], ps[2][:, 2 * P:2 * P + E]), 1)
                    step(nc.vector.memset(best[:, :], 0.0), 2)
                    wait_apart(nc, dve, gating, t * GATING + 2, k.spare)
                    step(nc.vector.max(best[:, :], logits[:, :]), 3)
                    step(nc.vector.tensor_scalar(lead[:, :], logits[:, :], best[:, 0:1], None, ALU.subtract), 4)
                    at_least(dve, gating, (t - 1) * GATING)
                    step(nc.vector.scalar_tensor_tensor(zt, logits[:, :], best[:, 1:2], lead[:, :], ALU.subtract,
                                                        ALU.add), 5)
                    step(nc.vector.tensor_tensor(square(higher), other, mine, ALU.is_gt), 6)
                    step(nc.vector.tensor_tensor(square(same), other, mine, ALU.is_equal), 7)
                    step(nc.vector.tensor_tensor(same[:, :], same[:, :], k.part("lower"), ALU.mult), 8)
                    step(nc.vector.tensor_tensor(higher[:, :], higher[:, :], same[:, :], ALU.add), 9)
                    step(nc.vector.tensor_reduce(rank[:, q * E:(q + 1) * E], square(higher), AX, ALU.add), 10)
                    dve.wait_ge(z_sig, t + 1)
                    step(nc.vector.scalar_tensor_tensor(gate[:, q * E:(q + 1) * E], rank[:, q * E:(q + 1) * E], 1.5, zt,
                                                        ALU.is_lt, ALU.mult), 11)

                def combine(t, q, _):
                    dve.wait_ge(outs_made, t + 1)
                    nc.vector.tensor_tensor(outs[:, :], ps[5][:, :], row("be2"), ALU.add).then_inc(combined, 1)
                    dve.wait_ge(combined, t * 3 + 1)
                    dve.wait_ge(gating, t * GATING + GATING)
                    o3 = outs[:, :].rearrange("p (e m) -> p e m", m=M)
                    nc.vector.tensor_tensor(o3, o3, gate[:, q * E:(q + 1) * E].unsqueeze(2).to_broadcast([P, E, M]),
                                            ALU.mult).then_inc(combined, 1)
                    dve.wait_ge(combined, t * 3 + 2)
                    at_least(dve, moe_turned, t - 1)
                    nc.vector.tensor_reduce(moe[:, q * P:q * P + M], outs[:, :].rearrange("p (e m) -> p m e", m=M),
                                            AX, ALU.add).then_inc(combined, 1)

                def bias_dec(t, q, _):
                    dve.wait_ge(dec_made, t + 1)
                    at_least(dve, post.done, t - 1)
                    nc.vector.tensor_tensor(decoded[:, q * D:(q + 1) * D], ps[7][:, D:2 * D], row("dec_b"),
                                            ALU.add).then_inc(dec_biased, 1)

                def post_stats(t, q, _):
                    dve.wait_ge(dec_set, t + 1)
                    post.stats(dve, decoded[:, q * D:(q + 1) * D], t, q)

                def post_apply(t, q, _):
                    at_least(dve, finished, t * 3 - 3)
                    post.apply(dve, res[:, q * D:(q + 1) * D], decoded[:, q * D:(q + 1) * D], t, q)
                over_tiles(dve, lambda u: run_lagged(u, [(1, apply), (6, post_apply), (0, stats), (3, gates),
                                                         (5, post_stats), (3, combine), (4, bias_dec)]), 6)

            @block.gpsimd
            def _(pool):
                def finish(t, q, _):
                    part = res[:, q * D:(q + 1) * D]
                    pool.wait_ge(post.done, t + 1)
                    nc.gpsimd.tensor_tensor(part, part, row("ln_g3"), ALU.mult).then_inc(finished, 1)
                    pool.wait_ge(finished, t * 3 + 1)
                    nc.gpsimd.tensor_tensor(part, part, row("ln_b3"), ALU.add).then_inc(finished, 1)
                    pool.wait_ge(finished, t * 3 + 2)
                    nc.gpsimd.tensor_tensor(x[:, cols(t)], part, x[:, cols(t)], ALU.add).then_inc(finished, 1)
                over_tiles(pool, lambda u: run_lagged(u, [(0, lambda t, q, _: pre.power(pool, t, q)),
                                                          (5, lambda t, q, _: post.power(pool, t, q)), (6, finish)]), 6)


def layer3(k):
    head_attention(k, "h3", 16, SEC3, k.secA, "bq3", "bk3", "bv3", "bo3", k.x, True)
    gated_experts(k)


def stages(k):
    layer0(k)
    head_attention(k, "h1", 16, SEC1, k.secA, "bq1", "bk1", "bv1", "bo1", k.x, True, causal=True)
    layer1_ffn(k)
    layer2(k)
    layer3(k)



def build(nc, args, out):
    k = Kit()
    k.nc = nc
    (k.d_x, k.d_mask, k.d_sec0, k.d_sec1, k.d_sec2, k.d_sec3, k.d_sec65, k.d_rows,
     k.d_w1a, k.d_w2a, k.d_b2a, k.d_w1b, k.d_w2b) = args
    k.d_out = out
    k.d_rows_in = nc.dram_tensor("rows_by_expert", [SORTED, D], FP32).ap()
    k.d_rows_out = nc.dram_tensor("expert_results", [SORTED, D], FP32).ap()
    with ExitStack() as ctx:
        sb = lambda n, s, d=FP32: ctx.enter_context(nc.sbuf_tensor(n, s, d))
        k.x = sb("x", [P, TILES * D])
        k.sec0 = sb("sec0", [P, offsets(SEC0)[1]])
        k.secA = sb("secA", [P, offsets(SEC3)[1]])
        k.sec2 = sb("sec2", [P, offsets(SEC2)[1]])
        k.sec65 = sb("sec65", [65, offsets(SEC65)[1]])
        k.rows = sb("rows", [P, offsets(ROWS)[1]])
        k.neghalf, k.eps, k.spare = [sb(n, [P, 1])[:, 0:1] for n in ("neghalf", "eps", "spare")]
        k.ones = sb("ones", [P, P])
        k.ident16 = sb("ident16", [P, P], BF16)
        k.causal = sb("causal16", [P, 2 * KEYS], BF16)[:, :].rearrange("p (a j) -> p a j", a=2)
        k.pos = sb("pos", [P, TILES], I32)
        k.tile_expert = sb("tile_expert", [P, 24], I32)
        k.onehot = sb("onehot", [P, EXPERTS * TILES])
        k.gate1 = sb("gate1", [P, TILES])
        k.tern, k.alpha = sb("tern", [P, DC * D], BF16), sb("alpha", [P, 1])
        k.packs = [(SEC0, k.sec0)]
        k.ident = k.part("ident")
        k.ps = [ctx.enter_context(nc.psum_tensor(f"bank{i}", [P, 512], FP32)) for i in range(8)]
        k.loaded0 = ctx.enter_context(nc.semaphore("sec0_loaded"))
        k.set_up = ctx.enter_context(nc.semaphore("constants_set"))
        stages(k)



def kernel(**inputs):
    import concourse.bacc as _bacc
    from concourse.bass_utils import run_bass_kernel_spmd as _run
    i = {n: np.asarray(a) for n, a in inputs.items()}

    def kmajor(w):
        return w.reshape(-1, P, w.shape[-1]).transpose(1, 0, 2).reshape(P, -1)

    def col(v):
        return v.reshape(-1, P).T

    def pack(table, parts, rows=P):
        parts = [np.asarray(parts[n]).reshape(rows, -1) for n, _ in table]
        assert [a.shape[1] for a in parts] == [w for _, w in table]
        return np.ascontiguousarray(np.concatenate(parts, axis=1))

    f32 = np.float32
    p = np.arange(P)
    ctx = i["ctx_1024"]
    ctxT = ctx.transpose(2, 0, 1).reshape(DC, P, B, KEYS).transpose(1, 0, 2, 3)
    qkv_w, qkv_b = i["L2_xattn_qkv_w"], i["L2_xattn_qkv_b"]
    inw, inb = i["L2_xattn_in_proj_w"], i["L2_xattn_in_proj_b"]
    sec0 = dict(
        ident=np.eye(P, dtype=f32), tri=(p[:, None] < p[None, :]).astype(f32),
        hmask16=(p[:, None] // 16 == np.arange(8)[None]).astype(f32),
        hmask8=(p[:, None] // 32 == np.arange(4)[None]).astype(f32),
        vmask=(p[:, None] // KEYS == np.arange(2)[None]).astype(f32),
        ctxT=np.concatenate([ctxT, ctxT], axis=3),
        ctx=np.concatenate([ctx, ctx], axis=1).transpose(1, 0, 2),
        centroids=kmajor(i["L0_ffn_centroids"].T), wr=kmajor(i["L1_ffn_Wr"]),
        bq1=col(i["L1_xattn_bq"]), bk1=col(i["L1_xattn_bk"]), bvs2=col(qkv_b[2 * D:]),
        bq2=col(inb[:D]), bk2=col(inb[D:2 * D]), lin1_b=col(i["L2_xattn_lin1_b"]),
        bq3=col(i["L3_xattn_bq"]), bk3=col(i["L3_xattn_bk"]), enc_b=col(i["L3_ffn_enc_b"]),
        s2c_b=np.concatenate([i["L3_ffn_s2c_b"]] * 2), eb1=col(i["L0_ffn_b1"].reshape(-1)),
        nibble=np.broadcast_to(np.arange(1, 16, dtype=f32), (P, 15)),
        base0=np.broadcast_to(np.arange(EXPERTS, dtype=f32) * (T // EXPERTS), (P, EXPERTS)),
        tstart=np.broadcast_to(np.arange(24, dtype=f32) * GROUP, (P, 24)),
        lower=np.broadcast_to((np.arange(8)[None, :] < np.arange(8)[:, None]).astype(f32).reshape(1, 64), (P, 64)),
        causal=np.where((p[:, None, None] < np.arange(KEYS)) & (np.arange(2)[:, None] == 0), f32(-1e30), f32(0)))
    sec1 = dict(wq=kmajor(i["L1_xattn_Wq"].T), wk=kmajor(i["L1_xattn_Wk"].T), wv=kmajor(i["L1_xattn_Wv"].T),
                wo=kmajor(i["L1_xattn_Wo"].T))
    sec2 = dict(vs=kmajor(qkv_w[2 * D:].T), os=kmajor(i["L2_xattn_sa_out_w"].T), wq=kmajor(inw[:D].T),
                wk=kmajor(inw[D:2 * D].T), wv=kmajor(inw[2 * D:].T), wo=kmajor(i["L2_xattn_mha_out_w"].T),
                lin1=kmajor(i["L2_xattn_lin1_w"].T), lin2=kmajor(i["L2_xattn_lin2_w"].T),
                tern=kmajor(i["L2_ffn_weight"].T))
    sec3 = dict(wq=kmajor(i["L3_xattn_Wq"]), wk=kmajor(i["L3_xattn_Wk"]), wv=kmajor(i["L3_xattn_Wv"]),
                wo=kmajor(i["L3_xattn_Wo"]), enc=kmajor(i["L3_ffn_enc_W"]), s2c=kmajor(i["L3_ffn_s2c_W"]),
                we2=kmajor(i["L3_ffn_We2"].reshape(-1, 64)), dec=kmajor(i["L3_ffn_dec_W"]))
    we1 = i["L3_ffn_We1"].transpose(1, 0, 2).reshape(64, -1)
    sec65 = dict(rw1=np.concatenate([i["L3_ffn_rW1"], i["L3_ffn_rb1"][None]]),
                 rw2=np.concatenate([i["L3_ffn_rW2"], i["L3_ffn_rb2"][None]]),
                 we1=np.concatenate([we1, i["L3_ffn_be1"].reshape(1, -1)]),
                 c2s=np.concatenate([i["L3_ffn_c2s_W"], i["L3_ffn_c2s_b"][None]]))
    rows = dict(ln_g0=i["L0_ffn_ln_g"], ln_b0=i["L0_ffn_ln_b"], bv1=i["L1_xattn_bv"], bo1=i["L1_xattn_bo"],
                bos2=i["L2_xattn_sa_out_b"], g1=i["L2_xattn_ln1_g"], b1=i["L2_xattn_ln1_b"], bv2=inb[2 * D:],
                bo2=i["L2_xattn_mha_out_b"], g2=i["L2_xattn_ln2_g"], b2=i["L2_xattn_ln2_b"],
                lin2_b=i["L2_xattn_lin2_b"], g3=i["L2_xattn_ln3_g"], b3=i["L2_xattn_ln3_b"],
                gamma=i["L2_ffn_gamma"], beta=i["L2_ffn_beta"], bv3=i["L3_xattn_bv"], bo3=i["L3_xattn_bo"],
                dec_b=i["L3_ffn_dec_b"], ln_g3=i["L3_ffn_ln_g"], ln_b3=i["L3_ffn_ln_b"], be2=i["L3_ffn_be2"])

    def experts(w):
        return np.ascontiguousarray(w.reshape(EXPERTS, -1, P, w.shape[-1]).transpose(0, 2, 1, 3).reshape(EXPERTS, P, -1))

    arrays = dict(
        x=i["x"].reshape(T, D), mask=i["mask_BxSxS2_fk0"].reshape(T, KEYS), sec0=pack(SEC0, sec0),
        sec1=pack(SEC1, sec1), sec2=pack(SEC2, sec2), sec3=pack(SEC3, sec3), sec65=pack(SEC65, sec65, 65),
        rows=pack(ROWS, rows, 1).reshape(-1), w1a=experts(i["L0_ffn_w1"]), w2a=experts(i["L0_ffn_w2"]),
        b2a=i["L0_ffn_b2"], w1b=experts(i["L1_ffn_W1"]), w2b=experts(i["L1_ffn_W2"]))
    nc = _bacc.Bacc("TRN2", target_bir_lowering=False, num_devices=1)
    args = [nc.dram_tensor("in_" + n, a.shape, FP32, kind="ExternalInput").ap() for n, a in arrays.items()]
    out = nc.dram_tensor("out", (T, D), FP32, kind="ExternalOutput").ap()
    build(nc, args, out)
    r = _run(nc, [{"in_" + n: np.ascontiguousarray(a) for n, a in arrays.items()}], core_ids=[0])
    return r.results[0]["out"].reshape(B, S, D)
```
